# Optimizing a Trainium2 kernel written in Bass

```python
import numpy as np
import jax
import jax.numpy as jnp

def _softmax(x, axis=-1):
    return jax.nn.softmax(x, axis=axis)

def _gelu(x):
    return jax.nn.gelu(x, approximate=True)

def _silu(x):
    return jax.nn.silu(x)

def _sigmoid(x):
    return jax.nn.sigmoid(x)

def _layernorm(x, axis=-1, eps=1e-05):
    m = jnp.mean(x, axis=axis, keepdims=True)
    v = jnp.var(x, axis=axis, keepdims=True)
    return (x - m) / jnp.sqrt(v + eps)

def _scatter_add(tgt, idx, src, axis=0):
    return tgt.at[idx].add(src)

def _segment_sum(src, seg, n):
    return jax.ops.segment_sum(src, seg, n)
kernel_name = 'mk_gnn_resnorm_d4_gnn_r16_b4ee9a'

def setup_inputs(seed: int=0):
    np.random.seed(seed)
    _w = jnp.asarray

    def _rec_inputs():
        import jax
        import jax.numpy as jnp
        _gk = jax.random.key(seed)
        x = -0.000202 + 1 * jax.random.normal(jax.random.fold_in(_gk, 1), (6250, 128), jnp.float32)
        src = jax.random.randint(jax.random.fold_in(_gk, 2), (200000,), 0, 6250, jnp.int32)
        dst = jnp.minimum((6250 * jax.random.uniform(jax.random.fold_in(_gk, 3), (200000,)) ** 2.0).astype(jnp.int32), 99999)
        _o = jnp.argsort(dst, stable=True)
        src = src[_o]
        dst = dst[_o]
        edge_attr_3 = 0.000844983 + 0.999762 * jax.random.normal(jax.random.fold_in(_gk, 11), (200000, 3), jnp.float32)
        edge_weight1 = jax.random.uniform(jax.random.fold_in(_gk, 13), (200000, 1), jnp.float32, 0.0, 5.99999)
        return (x, src, dst, edge_attr_3, edge_weight1)
    x, src, dst, edge_attr_3, edge_weight1 = _rec_inputs()

    def _L0_gnn_setup():
        import jax, jax.numpy as jnp
        import numpy as np
        N = 3125
        E = 50000
        C = 128

        def layer_norm(x, g, b, eps=1e-05):
            mu = x.mean(-1, keepdims=True)
            var = x.var(-1, keepdims=True)
            return (x - mu) * jax.lax.rsqrt(var + eps) * g + b

        def gcn_conv(x, W, b, src, dst, n):
            h = x @ W
            deg = jax.ops.segment_sum(jnp.ones(src.shape[0], h.dtype), dst, num_segments=n) + 1.0
            dinv = jax.lax.rsqrt(deg)
            norm = dinv[src] * dinv[dst]
            agg = jax.ops.segment_sum(h[src] * norm[:, None], dst, num_segments=n)
            return agg + h * (dinv * dinv)[:, None] + b
        key = jax.random.key(seed)
        ks = jax.random.split(key, 8)
        s = 1.0 / np.sqrt(C)
        return {'x': jax.random.normal(ks[0], (N, C), jnp.float32), 't_emb': jax.random.normal(ks[1], (C,), jnp.float32), 'edge_index': jax.random.randint(ks[2], (2, E), 0, N), 'g1': jnp.ones((C,), jnp.float32), 'bn1': jnp.zeros((C,), jnp.float32), 'W1': jax.random.normal(ks[3], (C, C), jnp.float32) * s, 'b1': jnp.zeros((C,), jnp.float32), 'Wt1': jax.random.normal(ks[4], (C, C), jnp.float32) * s, 'bt1': jnp.zeros((C,), jnp.float32), 'g2': jnp.ones((C,), jnp.float32), 'bn2': jnp.zeros((C,), jnp.float32), 'W2': jax.random.normal(ks[5], (C, C), jnp.float32) * s, 'b2': jnp.zeros((C,), jnp.float32), 'Wt2': jax.random.normal(ks[6], (C, C), jnp.float32) * s, 'bt2': jnp.zeros((C,), jnp.float32)}
    _L0_gnn_all = _L0_gnn_setup()
    _L0_gnn_in = {k: v for k, v in _L0_gnn_all.items() if k in ('t_emb', 'g1', 'bn1', 'W1', 'b1', 'Wt1', 'bt1', 'g2', 'bn2', 'W2', 'b2', 'Wt2', 'bt2')}
    del _L0_gnn_all

    def _L1_gnn_setup():
        import jax, jax.numpy as jnp
        import numpy as np
        N_NODES = 6250
        N_EDGES = 100000
        F_IN = 128
        HEADS = 4
        C_OUT = 32
        NEG_SLOPE = 0.2

        def _gat_forward(x, edge_index, W, att_src, att_dst, bias):
            N = x.shape[0]
            H, C = att_src.shape
            h = (x @ W).reshape(N, H, C)
            loops = jnp.arange(N, dtype=edge_index.dtype)
            src = jnp.concatenate([edge_index[0], loops])
            dst = jnp.concatenate([edge_index[1], loops])
            a_src = jnp.einsum('nhc,hc->nh', h, att_src)
            a_dst = jnp.einsum('nhc,hc->nh', h, att_dst)
            e = jax.nn.leaky_relu(a_src[src] + a_dst[dst], NEG_SLOPE)
            m = jax.ops.segment_max(e, dst, num_segments=N)
            e = jnp.exp(e - m[dst])
            s = jax.ops.segment_sum(e, dst, num_segments=N)
            alpha = e / (s[dst] + 1e-16)
            msg = h[src] * alpha[:, :, None]
            out = jax.ops.segment_sum(msg, dst, num_segments=N).reshape(N, H * C)
            return jnp.tanh(out + bias)
        key = jax.random.key(seed)
        k1, k2, k3, k4, k5, k6 = jax.random.split(key, 6)
        x = jax.random.normal(k1, (N_NODES, F_IN), dtype=jnp.float32)
        edge_index = jax.random.randint(k2, (2, N_EDGES), 0, N_NODES, dtype=jnp.int64)
        W = jax.random.normal(k3, (F_IN, HEADS * C_OUT), dtype=jnp.float32) * (1.0 / np.sqrt(F_IN))
        att_src = jax.random.normal(k4, (HEADS, C_OUT), dtype=jnp.float32) * (1.0 / np.sqrt(C_OUT))
        att_dst = jax.random.normal(k5, (HEADS, C_OUT), dtype=jnp.float32) * (1.0 / np.sqrt(C_OUT))
        bias = jnp.zeros((HEADS * C_OUT,), dtype=jnp.float32)
        return {'x': x, 'edge_index': edge_index, 'W': W, 'att_src': att_src, 'att_dst': att_dst, 'bias': bias}
    _L1_gnn_all = _L1_gnn_setup()
    _L1_gnn_in = {k: v for k, v in _L1_gnn_all.items() if k in ('W', 'att_src', 'att_dst', 'bias')}
    del _L1_gnn_all

    def _L2_gnn_setup():
        import jax, jax.numpy as jnp
        import numpy as np
        import math
        N = 2500
        E = 40000
        HID = 128
        H = 8
        HD = HID // H
        CUTOFF = 5.0
        LN_EPS = 1e-05

        def _linear_params(key, out_d, in_d):
            k1, k2 = jax.random.split(key)
            s = 1.0 / np.sqrt(in_d)
            W = jax.random.uniform(k1, (out_d, in_d), minval=-s, maxval=s, dtype=jnp.float32)
            b = jax.random.uniform(k2, (out_d,), minval=-s, maxval=s, dtype=jnp.float32)
            return (W, b)
        key = jax.random.key(seed)
        ks = jax.random.split(key, 12)
        x = jax.random.normal(ks[0], (N, HID), dtype=jnp.float32)
        edge_index = jax.random.randint(ks[1], (2, E), 0, N, dtype=jnp.int64)
        edge_vec = jax.random.normal(ks[2], (E, 3), dtype=jnp.float32)
        edge_length = jax.random.uniform(ks[3], (E, 1), dtype=jnp.float32) * 6.0
        Wq, bq = _linear_params(ks[4], HID, HID)
        Wk, bk = _linear_params(ks[5], HID, HID)
        Wv, bv = _linear_params(ks[6], HID, HID)
        We1, be1 = _linear_params(ks[7], HID, 1)
        We2, be2 = _linear_params(ks[8], H, HID)
        Wo, bo = _linear_params(ks[9], HID, HID)
        ln_g = jnp.ones((HID,), jnp.float32)
        ln_b = jnp.zeros((HID,), jnp.float32)
        return {'x': x, 'edge_vec': edge_vec, 'edge_length': edge_length, 'Wq': Wq, 'bq': bq, 'Wk': Wk, 'bk': bk, 'Wv': Wv, 'bv': bv, 'We1': We1, 'be1': be1, 'We2': We2, 'be2': be2, 'Wo': Wo, 'bo': bo, 'ln_g': ln_g, 'ln_b': ln_b, 'edge_index': edge_index}
    _L2_gnn_all = _L2_gnn_setup()
    _L2_gnn_in = {k: v for k, v in _L2_gnn_all.items() if k in ('Wq', 'bq', 'Wk', 'bk', 'Wv', 'bv', 'We1', 'be1', 'We2', 'be2', 'Wo', 'bo', 'ln_g', 'ln_b')}
    del _L2_gnn_all

    def _L3_gnn_setup():
        import jax, jax.numpy as jnp
        import numpy as np
        N_ATOMS = 625
        N_EDGES = 40000
        IN_F = 128
        OUT_F = 128
        key = jax.random.key(seed)
        k1, k2, k3, k4, k5, k6 = jax.random.split(key, 6)
        atom_features = jax.random.normal(k1, (N_ATOMS, IN_F), dtype=jnp.float32)
        edge_indices = jax.random.randint(k2, (2, N_EDGES), 0, N_ATOMS, dtype=jnp.int64)
        bm_lim = 1.0 / np.sqrt(IN_F * 2)
        bu_lim = 1.0 / np.sqrt(IN_F + OUT_F)
        W_msg = jax.random.uniform(k3, (IN_F * 2, OUT_F), jnp.float32, -bm_lim, bm_lim)
        b_msg = jax.random.uniform(k4, (OUT_F,), jnp.float32, -bm_lim, bm_lim)
        W_upd = jax.random.uniform(k5, (IN_F + OUT_F, OUT_F), jnp.float32, -bu_lim, bu_lim)
        b_upd = jax.random.uniform(k6, (OUT_F,), jnp.float32, -bu_lim, bu_lim)
        return {'atom_features': atom_features, 'edge_indices': edge_indices, 'W_msg': W_msg, 'b_msg': b_msg, 'W_upd': W_upd, 'b_upd': b_upd}
    _L3_gnn_all = _L3_gnn_setup()
    _L3_gnn_in = {k: v for k, v in _L3_gnn_all.items() if k in ('W_msg', 'b_msg', 'W_upd', 'b_upd')}
    del _L3_gnn_all
    return {'x': x, 'src': src, 'dst': dst, 'edge_attr_3': edge_attr_3, 'edge_weight1': edge_weight1, 'L0_gnn_t_emb': _L0_gnn_in['t_emb'], 'L0_gnn_g1': _L0_gnn_in['g1'], 'L0_gnn_bn1': _L0_gnn_in['bn1'], 'L0_gnn_W1': _L0_gnn_in['W1'], 'L0_gnn_b1': _L0_gnn_in['b1'], 'L0_gnn_Wt1': _L0_gnn_in['Wt1'], 'L0_gnn_bt1': _L0_gnn_in['bt1'], 'L0_gnn_g2': _L0_gnn_in['g2'], 'L0_gnn_bn2': _L0_gnn_in['bn2'], 'L0_gnn_W2': _L0_gnn_in['W2'], 'L0_gnn_b2': _L0_gnn_in['b2'], 'L0_gnn_Wt2': _L0_gnn_in['Wt2'], 'L0_gnn_bt2': _L0_gnn_in['bt2'], 'L1_gnn_W': _L1_gnn_in['W'], 'L1_gnn_att_src': _L1_gnn_in['att_src'], 'L1_gnn_att_dst': _L1_gnn_in['att_dst'], 'L1_gnn_bias': _L1_gnn_in['bias'], 'L2_gnn_Wq': _L2_gnn_in['Wq'], 'L2_gnn_bq': _L2_gnn_in['bq'], 'L2_gnn_Wk': _L2_gnn_in['Wk'], 'L2_gnn_bk': _L2_gnn_in['bk'], 'L2_gnn_Wv': _L2_gnn_in['Wv'], 'L2_gnn_bv': _L2_gnn_in['bv'], 'L2_gnn_We1': _L2_gnn_in['We1'], 'L2_gnn_be1': _L2_gnn_in['be1'], 'L2_gnn_We2': _L2_gnn_in['We2'], 'L2_gnn_be2': _L2_gnn_in['be2'], 'L2_gnn_Wo': _L2_gnn_in['Wo'], 'L2_gnn_bo': _L2_gnn_in['bo'], 'L2_gnn_ln_g': _L2_gnn_in['ln_g'], 'L2_gnn_ln_b': _L2_gnn_in['ln_b'], 'L3_gnn_W_msg': _L3_gnn_in['W_msg'], 'L3_gnn_b_msg': _L3_gnn_in['b_msg'], 'L3_gnn_W_upd': _L3_gnn_in['W_upd'], 'L3_gnn_b_upd': _L3_gnn_in['b_upd']}

def reference(x, src, dst, edge_attr_3, edge_weight1, L0_gnn_t_emb, L0_gnn_g1, L0_gnn_bn1, L0_gnn_W1, L0_gnn_b1, L0_gnn_Wt1, L0_gnn_bt1, L0_gnn_g2, L0_gnn_bn2, L0_gnn_W2, L0_gnn_b2, L0_gnn_Wt2, L0_gnn_bt2, L1_gnn_W, L1_gnn_att_src, L1_gnn_att_dst, L1_gnn_bias, L2_gnn_Wq, L2_gnn_bq, L2_gnn_Wk, L2_gnn_bk, L2_gnn_Wv, L2_gnn_bv, L2_gnn_We1, L2_gnn_be1, L2_gnn_We2, L2_gnn_be2, L2_gnn_Wo, L2_gnn_bo, L2_gnn_ln_g, L2_gnn_ln_b, L3_gnn_W_msg, L3_gnn_b_msg, L3_gnn_W_upd, L3_gnn_b_upd):
    import jax
    import jax.numpy as jnp

    def _L0_gnn_ref(x, t_emb, edge_index, g1, bn1, W1, b1, Wt1, bt1, g2, bn2, W2, b2, Wt2, bt2):
        import jax, jax.numpy as jnp
        import numpy as np
        N = 3125
        E = 50000
        C = 128

        def layer_norm(x, g, b, eps=1e-05):
            mu = x.mean(-1, keepdims=True)
            var = x.var(-1, keepdims=True)
            return (x - mu) * jax.lax.rsqrt(var + eps) * g + b

        def gcn_conv(x, W, b, src, dst, n):
            h = x @ W
            deg = jax.ops.segment_sum(jnp.ones(src.shape[0], h.dtype), dst, num_segments=n) + 1.0
            dinv = jax.lax.rsqrt(deg)
            norm = dinv[src] * dinv[dst]
            agg = jax.ops.segment_sum(h[src] * norm[:, None], dst, num_segments=n)
            return agg + h * (dinv * dinv)[:, None] + b
        src, dst = (edge_index[0], edge_index[1])
        n = x.shape[0]
        h = layer_norm(x, g1, bn1)
        h = gcn_conv(h, W1, b1, src, dst, n) + (t_emb @ Wt1 + bt1)
        h = jax.nn.silu(h)
        h = layer_norm(h, g2, bn2)
        h = gcn_conv(h, W2, b2, src, dst, n) + (t_emb @ Wt2 + bt2)
        h = jax.nn.silu(h)
        return h + x

    def _L1_gnn_ref(x, edge_index, W, att_src, att_dst, bias):
        import jax, jax.numpy as jnp
        import numpy as np
        N_NODES = 6250
        N_EDGES = 100000
        F_IN = 128
        HEADS = 4
        C_OUT = 32
        NEG_SLOPE = 0.2

        def _gat_forward(x, edge_index, W, att_src, att_dst, bias):
            N = x.shape[0]
            H, C = att_src.shape
            h = (x @ W).reshape(N, H, C)
            loops = jnp.arange(N, dtype=edge_index.dtype)
            src = jnp.concatenate([edge_index[0], loops])
            dst = jnp.concatenate([edge_index[1], loops])
            a_src = jnp.einsum('nhc,hc->nh', h, att_src)
            a_dst = jnp.einsum('nhc,hc->nh', h, att_dst)
            e = jax.nn.leaky_relu(a_src[src] + a_dst[dst], NEG_SLOPE)
            m = jax.ops.segment_max(e, dst, num_segments=N)
            e = jnp.exp(e - m[dst])
            s = jax.ops.segment_sum(e, dst, num_segments=N)
            alpha = e / (s[dst] + 1e-16)
            msg = h[src] * alpha[:, :, None]
            out = jax.ops.segment_sum(msg, dst, num_segments=N).reshape(N, H * C)
            return jnp.tanh(out + bias)
        return _gat_forward(x, edge_index, W, att_src, att_dst, bias)

    def _L2_gnn_ref(x, edge_vec, edge_length, Wq, bq, Wk, bk, Wv, bv, We1, be1, We2, be2, Wo, bo, ln_g, ln_b, edge_index):
        import jax, jax.numpy as jnp
        import numpy as np
        import math
        N = 2500
        E = 40000
        HID = 128
        H = 8
        HD = HID // H
        CUTOFF = 5.0
        LN_EPS = 1e-05

        def _linear_params(key, out_d, in_d):
            k1, k2 = jax.random.split(key)
            s = 1.0 / np.sqrt(in_d)
            W = jax.random.uniform(k1, (out_d, in_d), minval=-s, maxval=s, dtype=jnp.float32)
            b = jax.random.uniform(k2, (out_d,), minval=-s, maxval=s, dtype=jnp.float32)
            return (W, b)
        row, col = (edge_index[0], edge_index[1])
        n = x.shape[0]
        q = (x @ Wq.T + bq).reshape(n, H, HD)
        k = (x @ Wk.T + bk).reshape(n, H, HD)
        v = (x @ Wv.T + bv).reshape(n, H, HD)
        attn = jnp.einsum('ehd,ehd->eh', q[row], k[col]) / math.sqrt(HD)
        edge_bias = jax.nn.silu(edge_length @ We1.T + be1) @ We2.T + be2
        attn = attn + edge_bias
        cut = 0.5 * (jnp.cos(edge_length * math.pi / CUTOFF) + 1.0)
        cut = cut * (edge_length < CUTOFF).astype(jnp.float32)
        attn = attn * cut
        attn_exp = jnp.exp(attn - jnp.max(attn, axis=0, keepdims=True))
        attn_sum = jax.ops.segment_sum(attn_exp, row, num_segments=n)
        attn = attn_exp / (attn_sum[row] + 1e-08)
        out = jax.ops.segment_sum(attn[:, :, None] * v[col], row, num_segments=n)
        out = out.reshape(n, HID) @ Wo.T + bo
        h = x + out
        mu = jnp.mean(h, axis=-1, keepdims=True)
        var = jnp.mean(jnp.square(h - mu), axis=-1, keepdims=True)
        return (h - mu) / jnp.sqrt(var + LN_EPS) * ln_g + ln_b

    def _L3_gnn_ref(atom_features, edge_indices, W_msg, b_msg, W_upd, b_upd):
        import jax, jax.numpy as jnp
        import numpy as np
        N_ATOMS = 625
        N_EDGES = 40000
        IN_F = 128
        OUT_F = 128
        src, dst = (edge_indices[0], edge_indices[1])
        edge_in = jnp.concatenate([atom_features[src], atom_features[dst]], axis=-1)
        messages = edge_in @ W_msg + b_msg
        agg = jax.ops.segment_sum(messages, dst, num_segments=atom_features.shape[0])
        upd_in = jnp.concatenate([atom_features, agg], axis=-1)
        return upd_in @ W_upd + b_upd
    edge_index = jnp.stack([src, dst])
    x = _layernorm(x + _L0_gnn_ref(x, L0_gnn_t_emb, edge_index, L0_gnn_g1, L0_gnn_bn1, L0_gnn_W1, L0_gnn_b1, L0_gnn_Wt1, L0_gnn_bt1, L0_gnn_g2, L0_gnn_bn2, L0_gnn_W2, L0_gnn_b2, L0_gnn_Wt2, L0_gnn_bt2), axis=-1)
    x = _layernorm(x + _L1_gnn_ref(x, edge_index, L1_gnn_W, L1_gnn_att_src, L1_gnn_att_dst, L1_gnn_bias), axis=-1)
    x = _layernorm(x + _L2_gnn_ref(x, edge_attr_3, edge_weight1, L2_gnn_Wq, L2_gnn_bq, L2_gnn_Wk, L2_gnn_bk, L2_gnn_Wv, L2_gnn_bv, L2_gnn_We1, L2_gnn_be1, L2_gnn_We2, L2_gnn_be2, L2_gnn_Wo, L2_gnn_bo, L2_gnn_ln_g, L2_gnn_ln_b, edge_index), axis=-1)
    x = _layernorm(x + _L3_gnn_ref(x, edge_index, L3_gnn_W_msg, L3_gnn_b_msg, L3_gnn_W_upd, L3_gnn_b_upd), axis=-1)
    return x

_drawn_inputs = setup_inputs


def setup_inputs(seed=0):
    import zlib

    import numpy as np

    out = dict(_drawn_inputs(seed))
    spreads = {'L0_gnn_g1': (1.0, 0.6),
     'L0_gnn_bn1': (0.0, 0.1),
     'L0_gnn_b1': (0.0, 0.1),
     'L0_gnn_bt1': (0.0, 0.1),
     'L0_gnn_g2': (1.0, 0.2),
     'L0_gnn_bn2': (0.0, 0.1),
     'L0_gnn_b2': (0.0, 0.1),
     'L0_gnn_bt2': (0.0, 0.1),
     'L1_gnn_bias': (0.0, 0.1),
     'L2_gnn_ln_g': (1.0, 0.2),
     'L2_gnn_ln_b': (0.0, 0.1)}
    factors = {'edge_weight1': 64.0,
     'L2_gnn_Wq': 63.981,
     'L2_gnn_bq': 64.0,
     'L2_gnn_Wk': 60.748,
     'L2_gnn_bk': 64.0,
     'L2_gnn_bv': 27.912,
     'L2_gnn_We1': 64.0,
     'L2_gnn_be1': 64.0,
     'L2_gnn_We2': 64.0,
     'L2_gnn_be2': 64.0,
     'L3_gnn_b_upd': 6.015,
     'L2_gnn_Wv': 8.0,
     'L2_gnn_Wo': 8.0}
    for name, (base, spread) in spreads.items():
        noise = np.random.default_rng([zlib.crc32(name.encode()), seed]).standard_normal(out[name].shape)
        drawn = base * np.exp(spread * noise) if base else spread * noise
        out[name] = jnp.asarray(drawn.astype(out[name].dtype))
    for name, factor in factors.items():
        out[name] = (out[name] * factor).astype(out[name].dtype)
    return out
```

```python
import itertools
import math
from contextlib import ExitStack

import concourse.bass as bass
from concourse import mybir

F32 = mybir.dt.float32
BF16 = mybir.dt.bfloat16
I32 = mybir.dt.int32
ALU = mybir.AluOpType
ACT = mybir.ActivationFunctionType
AX = mybir.AxisListType

P = 128
N = 6250
C = 128
E = 200000
NB = -(-N // P)
NP = NB * P
REM = N - (NB - 1) * P
BC = 7
NCH = NB // BC
EP = 125
EC = E // EP
G = 2
GE = G * P
GSH = GE.bit_length() - 1
H1, D1 = 4, 32
H2, D2 = 8, 16
A1 = C + H1
A2 = C + H2
BODY = 16
HALF = BODY // 2
GB = BODY // G
NG = -(-((E + NB * (GE - 1)) // GE) // GB) * GB
T = NG * G
IT = T // BODY
PAD = 200.0
EPS = 1e-5
NEG = -1e30
CUTOFF = 5.0
ROUND = 12582912.0

assert NB % BC == 0 and EP * EC == E and EC % BODY == 0 and T % P == 0

MATS = ("L0_gnn_W1", "L0_gnn_Wt1", "L0_gnn_W2", "L0_gnn_Wt2", "L1_gnn_W", "L2_gnn_Wq", "L2_gnn_Wk",
        "L2_gnn_Wv", "L2_gnn_Wo")
HALVES = ("L3_gnn_W_msg", "L3_gnn_W_upd")
VECS = ("L0_gnn_g1", "L0_gnn_bn1", "L0_gnn_b1", "L0_gnn_bt1", "L0_gnn_g2", "L0_gnn_bn2",
        "L0_gnn_b2", "L0_gnn_bt2", "L1_gnn_bias", "L2_gnn_bq", "L2_gnn_bk", "L2_gnn_bv",
        "L2_gnn_bo", "L2_gnn_ln_g", "L2_gnn_ln_b", "L3_gnn_b_msg", "L3_gnn_b_upd")
ATTS = ("L1_gnn_att_src", "L1_gnn_att_dst")


def copy(dve, out, rows):
    return dve.tensor_scalar(out, rows, 1.0, None, ALU.mult)


class Link:

    def __init__(self, sem):
        self.sem, self.base, self.n, self.turn, self.per = sem, 0, 0, 0, 0

    def loop(self, turn, per):
        self.base += self.n
        self.turn, self.per, self.n = turn, per, 0

    def end(self, turns):
        assert self.n == self.per, (self.n, self.per)
        self.base += turns * self.per
        self.turn, self.per, self.n = 0, 0, 0

    def __call__(self, eng, ins):
        ins.then_inc(self.sem, 1)
        self.n += 1
        eng.wait_ge(self.sem, self.turn * self.per + self.base + self.n)


class Bufs:
    pass


def allocate(nc, ctx, a, out):
    k = Bufs()
    k.a, k.out = a, out

    def sb(name, shape, dt=F32):
        return ctx.enter_context(nc.sbuf_tensor(name, shape, dt))

    def dram(name, shape):
        return nc.dram_tensor(name, shape, F32, kind="Internal").ap()

    numbers = itertools.count()
    k.phase_sems = []

    def phase_sem(name):
        k.phase_sems.append(nc.alloc_semaphore(name=f"{name}_{next(numbers)}"))
        return k.phase_sems[-1]
    k.sem = phase_sem
    k.by_dst_dram = dram("by_dst", (P * T, 2))
    k.by_src_dram = dram("by_src", (P * T, 4))
    k.w_rows_dram = dram("w_rows", (T, P))
    k.tab_dram = dram("tab", (NP, C))
    k.tab_a_dram = dram("tab_a", (NP, H1))
    k.tab_h_dram = dram("tab_h", (NP, A1))
    k.tab_k_dram = dram("tab_k", (NP, C))
    k.tab_v_dram = dram("tab_v", (NP, C))
    k.ramp_i = sb("ramp_i", [P, P], I32)
    k.row_i = sb("row_i", [P, 1], I32)
    k.ramp = sb("ramp", [P, P])
    k.row = sb("row", [P, 1])
    k.ident = sb("ident", [P, P])
    k.below = sb("below", [P, P])
    k.upto = sb("upto", [P, P])
    k.ones = sb("ones", [P, P])
    k.x = sb("x", [P, NB, C])
    k.h = sb("h", [P, NB, C])
    k.acc = sb("acc", [P, NB * A2])
    k.deg = sb("deg", [P, NB])
    k.dinv = sb("dinv", [P, NB])
    k.nodev = sb("nodev", [P, NB, 2 * H1])
    k.asrc = sb("asrc", [P, NB, H1])
    k.maxa = sb("maxa", [P, NB * H1])
    k.idx = sb("idx", [P, T + HALF], I32)
    k.loc = sb("loc", [P, T + G])
    k.cut = sb("cut", [P, T])
    k.block_of = {"dst": sb("block_dst", [1, NG + 1], I32), "src": sb("block_src", [1, NG + 1], I32)}
    k.big = sb("big", [P, T * H2])
    sizes = (BODY * A2, HALF * P, 2 * G * P, 4 * G * C)
    room = sb("room", [P, sum(sizes)])
    ends = [sum(sizes[:m + 1]) for m in range(4)]
    k.gat = room[:, 0:ends[0]].rearrange("p (m c) -> p m c", c=A2)
    k.oneh = room[:, ends[0]:ends[1]].rearrange("p (m c) -> p m c", c=P)
    k.hot_t = room[:, ends[1]:ends[2]].rearrange("p (m c) -> p m c", c=G * P)
    k.wk = room[:, ends[2]:ends[3]]
    k.chunk_room = room
    k.stage = sb("stage", [P, BODY], I32)
    k.tmp = sb("tmp", [P, 256])
    k.offs = sb("offs", [P, NB])
    k.st = sb("st", [P, BC, 16])
    k.psum_pair = [ctx.enter_context(nc.psum_tensor(f"banks{i}", [P, 1024], F32))[:, :] for i in range(4)]
    k.psum = [k.psum_pair[i // 2][:, i % 2 * 512:(i % 2 + 1) * 512] for i in range(8)]
    k.w = {n: sb("m_" + n, [P, C]) for n in MATS}
    k.top = {n: sb("t_" + n, [P, C]) for n in HALVES}
    k.bot = {n: sb("b_" + n, [P, C]) for n in HALVES}
    k.v = {n: sb("v_" + n, [P, C]) for n in VECS + ATTS}
    k.be2 = sb("be2", [P, H2])
    k.temb = sb("temb", [P, 1])
    k.be1 = sb("be1", [P, 1])
    k.we1 = sb("we1", [1, P])
    k.we2 = sb("we2", [H2, P])
    k.we2t = sb("we2t", [P, H2])
    f = [k.big[0:EP, i * EC:(i + 1) * EC] for i in range(8)]
    k.src_f, k.dst_f, k.w_f, k.sloc, k.dloc, k.shi, k.dhi, k.mask = f
    hh = k.h[:, :, :].rearrange("p b c -> p (b c)")
    k.zeros = hh[0:EP, 0:EC]
    k.pos = {"src": hh[0:EP, EC:2 * EC].bitcast(I32), "dst": hh[0:EP, 2 * EC:3 * EC].bitcast(I32)}
    k.raw_s, k.raw_d = k.acc[0:EP, 0:EC].bitcast(I32), k.acc[0:EP, EC:2 * EC].bitcast(I32)
    k.shifted = k.acc[0:EP, 2 * EC:3 * EC].bitcast(I32)
    k.scan, k.posf = k.acc[0:EP, 3 * EC:4 * EC], k.acc[0:EP, 0:EC]
    lasting = lambda name: ctx.enter_context(nc.semaphore(name))
    k.gathered = [lasting(f"gathered{i}") for i in range(BODY)]
    k.gathered_base = 0
    k.const = lasting("const")
    k.passed = lasting("passed")
    return k


def load_phase(nc, k):
    a = k.a
    loaded, iotas, x_clear, filled, zero_done = (k.sem(n) for n in (
        "loaded", "iotas", "x_clear", "filled", "zero_done"))
    link = Link(k.sem("const_step"))
    pattern = k.h[:, :, :].rearrange("p b c -> p (b c)")
    with nc.Block() as block:
        @block.sync
        def _(sp):
            count = [0]

            def load(dst, src):
                sp.dma_start(dst, src).then_inc(loaded, 16)
                count[0] += 16
            load(k.raw_s, a["src"].rearrange("(p c) -> p c", p=EP))
            load(k.raw_d, a["dst"].rearrange("(p c) -> p c", p=EP))
            load(k.w_f, a["edge_weight1"].rearrange("(p c) o -> p (c o)", p=EP))
            load(k.x[:, 0:NB - 1, :], a["x"][0:(NB - 1) * P, :].rearrange("(b p) c -> p b c", p=P))
            for n in MATS:
                load(k.w[n][:, :], a[n])
            for n in HALVES:
                load(k.top[n][:, :], a[n][0:C, :])
                load(k.bot[n][:, :], a[n][C:2 * C, :])
            for n in VECS:
                load(k.v[n][:, :], a[n].partition_broadcast(P))
            for n in ATTS:
                load(k.v[n][:, :], a[n].rearrange("h c -> (h c)").partition_broadcast(P))
            load(k.be2[:, :], a["L2_gnn_be2"].partition_broadcast(P))
            load(k.temb[:, :], a["L0_gnn_t_emb"].rearrange("(c o) -> c o", o=1))
            load(k.be1[:, :], a["L2_gnn_be1"].rearrange("(c o) -> c o", o=1))
            load(k.we1[:, :], a["L2_gnn_We1"].rearrange("c o -> o c"))
            load(k.we2[:, :], a["L2_gnn_We2"])
            sp.wait_ge(x_clear, 1)
            load(k.x[0:REM, NB - 1, :], a["x"][(NB - 1) * P:N, :])
            sp.wait_ge(loaded, count[0])

        @block.scalar
        def _(act):
            act.wait_ge(filled, 2)
            half = P * T // 2 // P
            rows = k.by_src_dram.rearrange("(p s r) f -> p s (r f)", p=P, s=2)
            for s in range(2):
                act.dma_start(rows[:, s, :], pattern[:, 0:half * 4]).then_inc(zero_done, 16)
            rows = k.by_dst_dram.rearrange("(p s r) f -> p s (r f)", p=P, s=2)
            for s in range(2):
                act.dma_start(rows[:, s, :], pattern[:, half * 4:half * 6]).then_inc(zero_done, 16)
            act.wait_ge(zero_done, 64)

        @block.gpsimd
        def _(pool):
            pool.iota(k.ramp_i[:, :], pattern=[[1, P]], base=0, channel_multiplier=0).then_inc(iotas, 1)
            pool.iota(k.idx[:, 0:NG], pattern=[[1, NG]], base=0, channel_multiplier=0).then_inc(iotas, 1)
            pool.iota(k.row_i[:, :], pattern=[[1, 1]], base=0, channel_multiplier=1).then_inc(iotas, 1)

        @block.vector
        def _(dve):
            dve.memset(k.x[:, NB - 1, :], 0.0).then_inc(x_clear, 1)
            half = P * T // 2 // P
            link(dve, dve.memset(pattern[:, 0:half * 6], 0.0))
            p4 = pattern[:, 0:half * 4].rearrange("p (r f) -> p r f", f=4)
            p2 = pattern[:, half * 4:half * 6].rearrange("p (r f) -> p r f", f=2)
            dve.memset(p4[:, :, 1:2], PAD).then_inc(filled, 1)
            dve.memset(p2[:, :, 1:2], PAD).then_inc(filled, 1)
            dve.memset(k.ones[:, :], 1.0)
            dve.wait_ge(iotas, 3)
            dve.tensor_copy(k.loc[:, 0:NG], k.idx[:, 0:NG])
            link(dve, dve.tensor_copy(k.ramp[:, :], k.ramp_i[:, :]))
            link(dve, dve.tensor_copy(k.row[:, :], k.row_i[:, :]))
            dve.tensor_scalar(k.ident[:, :], k.ramp[:, :], k.row[:, 0:1], None, ALU.is_equal)
            dve.tensor_scalar(k.below[:, :], k.ramp[:, :], k.row[:, 0:1], None, ALU.is_gt)
            dve.tensor_scalar(k.upto[:, :], k.ramp[:, :], k.row[:, 0:1], None, ALU.is_ge).then_inc(k.const, 1)


def fields_phase(nc, k):
    link = Link(k.sem("field_step"))
    with nc.Block() as block:
        @block.vector
        def _(dve):
            for raw, full, loc, hi in ((k.raw_s, k.src_f, k.sloc, k.shi), (k.raw_d, k.dst_f, k.dloc, k.dhi)):
                dve.tensor_copy(full, raw)
                link(dve, dve.tensor_scalar(k.shifted, raw, 7, None, ALU.arith_shift_right))
                link(dve, dve.tensor_copy(hi, k.shifted))
                link(dve, dve.tensor_scalar(k.shifted, raw, P - 1, None, ALU.bitwise_and))
                link(dve, dve.tensor_copy(loc, k.shifted))


def rank_and_scatter_phase(nc, k, key, scatter):
    n = f"{key}_{scatter}_"
    counted, summed, rounded, ended, compared, tabled = (k.sem(n + s) for s in (
        "counted", "summed", "rounded", "ended", "compared", "tabled"))
    link = Link(k.sem(n + "step"))
    staged, scattered = k.sem(n + "staged"), [k.sem(n + f"scattered{h}") for h in range(2)]
    picked, merged, tabled_read = k.sem(n + "picked"), k.sem(n + "merged"), k.sem(n + "tabled_read")
    spans = [(lo, min(lo + 512, EC)) for lo in range(0, EC, 512)]
    ps = k.psum
    cnt = k.tmp[:, 0:NB]
    tot_i, tot = k.tmp[:, 64:64 + NB].bitcast(I32), k.tmp[:, 128:128 + NB]
    pre = k.tmp[:, 192:192 + NB]
    col_i, col = k.st[0:NB, 0, 0:1].bitcast(I32), k.st[0:NB, 0, 1:2]
    end = k.st[0:NB, 0, 2:3]
    fields = {"src": (k.dst_f, k.sloc, k.w_f), "dst": (k.src_f, k.dloc)}
    target = {"src": k.by_src_dram, "dst": k.by_dst_dram}
    hi = {"src": k.shi, "dst": k.dhi, None: None}[key]
    group = k.loc[0:NB, 0:NG]
    past = k.cut[0:NB, 0:NG]
    with nc.Block() as block:
        if key:
            @block.tensor
            def _(pe):
                pe.wait_ge(counted, 1)
                pe.matmul(ps[0][:, 0:NB], k.ones[0:EP, :], cnt[0:EP, :], start=True, stop=True)
                pe.matmul(ps[1][0:EP, 0:NB], k.below[0:EP, 0:EP], cnt[0:EP, :], start=True, stop=True)
                pe.matmul(ps[2][0:NB, 0:1], cnt[0:EP, :], k.ones[0:EP, 0:1], start=True, stop=True)\
                    .then_inc(summed, 1)
                pe.wait_ge(rounded, 1)
                pe.matmul(ps[3][0:NB, 0:1], k.upto[0:NB, 0:NB], col, start=True, stop=True).then_inc(ended, 1)
                pe.wait_ge(compared, 1)
                pe.matmul(ps[4][0:1, 0:512], k.ones[0:NB, 0:1], past[:, 0:512], start=True, stop=True)
                pe.matmul(ps[5][0:1, 0:NG - 512], k.ones[0:NB, 0:1], past[:, 512:NG], start=True, stop=True)\
                    .then_inc(tabled, 1)
                pe.wait_ge(tabled_read, 1)
                for m, (lo, up) in enumerate(spans):
                    last = pe.matmul(ps[m][0:EP, 0:up - lo], k.ident[0:EP, 0:EP], k.zeros[:, lo:up],
                                     start=True, stop=False, skip_group_check=True)
                last.then_inc(merged, 1)
                with pe.Fori(0, NB) as b:
                    pe.wait_ge(picked, b + 1)
                    for m, (lo, up) in enumerate(spans):
                        last = pe.matmul(ps[m][0:EP, 0:up - lo], k.ident[0:EP, 0:EP], k.posf[:, lo:up],
                                         start=False, stop=False, skip_group_check=True)
                    last.then_inc(merged, 1)
                for m, (lo, up) in enumerate(spans):
                    last = pe.matmul(ps[m][0:EP, 0:up - lo], k.ident[0:EP, 0:EP], k.zeros[:, lo:up],
                                     start=False, stop=True, skip_group_check=True)
                last.then_inc(merged, 1)

            @block.vector
            def _(dve):
                link(dve, dve.memset(k.zeros, 0.0))
                with dve.Fori(0, NB) as b:
                    link.loop(b, 1)
                    link(dve, dve.tensor_scalar(k.mask, hi, k.ramp[0:EP, bass.ds(b, 1)], 0.0, ALU.is_equal,
                                                ALU.add, accum_out=cnt[0:EP, bass.ds(b, 1)]))
                link.end(NB)
                dve.sem_inc(counted, 1)
                dve.wait_ge(summed, 1)
                link(dve, dve.tensor_scalar(tot_i, ps[0][:, 0:NB], float(GE - 1), None, ALU.add))
                link(dve, dve.tensor_scalar(tot_i, tot_i, GSH, None, ALU.arith_shift_right))
                link(dve, dve.tensor_copy(tot, tot_i))
                link(dve, dve.tensor_tensor_scan(pre[0:EP, :], tot[0:EP, :], k.zeros[:, 0:NB], 0.0, ALU.add,
                                                 ALU.add))
                link(dve, dve.tensor_tensor(pre[0:EP, :], pre[0:EP, :], tot[0:EP, :], ALU.subtract))
                link(dve, dve.scalar_tensor_tensor(k.offs[0:EP, :], pre[0:EP, :], float(GE), ps[1][0:EP, 0:NB],
                                                   ALU.mult, ALU.add))
                link(dve, dve.tensor_scalar(col_i, ps[2][0:NB, 0:1], float(GE - 1), None, ALU.add))
                link(dve, dve.tensor_scalar(col_i, col_i, GSH, None, ALU.arith_shift_right))
                dve.tensor_copy(col, col_i).then_inc(rounded, 1)
                dve.wait_ge(ended, 1)
                link(dve, dve.tensor_copy(end, ps[3][0:NB, 0:1]))
                dve.tensor_scalar(past, group, end, None, ALU.is_ge).then_inc(compared, 1)
                dve.wait_ge(tabled, 1)
                table = k.block_of[key]
                dve.memset(table[0:1, NG:NG + 1], 0)
                dve.tensor_scalar(table[0:1, 0:512], ps[4][0:1, 0:512], float(NB - 1), None, ALU.min)
                dve.tensor_scalar(table[0:1, 512:NG], ps[5][0:1, 0:NG - 512], float(NB - 1), None, ALU.min)\
                    .then_inc(tabled_read, 1)
                with dve.Fori(0, NB) as b:
                    link.loop(b, 2)
                    link(dve, dve.tensor_scalar(k.mask, hi, k.ramp[0:EP, bass.ds(b, 1)], None, ALU.is_equal))
                    link(dve, dve.tensor_tensor_scan(k.scan, k.mask, k.zeros, k.offs[0:EP, bass.ds(b, 1)],
                                                     ALU.add, ALU.add))
                    dve.wait_ge(merged, b + 1)
                    dve.tensor_tensor(k.posf, k.scan, k.mask, ALU.mult).then_inc(picked, 1)
                    dve.wait_ge(picked, b + 1)
                link.end(NB)
                dve.wait_ge(merged, NB + 2)
                for m, (lo, up) in enumerate(spans):
                    link(dve, dve.tensor_copy(k.posf[:, lo:up], ps[m][0:EP, 0:up - lo]))
                slot = k.pos[key]
                link(dve, dve.tensor_scalar(slot, k.posf, -1.0, None, ALU.add))
                link(dve, dve.tensor_scalar(k.shifted, slot, 7, None, ALU.arith_shift_right))
                link(dve, dve.tensor_copy(k.scan, k.shifted))
                link(dve, dve.tensor_scalar(k.shifted, slot, P - 1, None, ALU.bitwise_and))
                link(dve, dve.tensor_copy(k.posf, k.shifted))
                dve.scalar_tensor_tensor(slot, k.posf, float(T), k.scan, ALU.mult, ALU.add)

        if scatter:
            width = len(fields[scatter])
            full = {"src": 4, "dst": 2}[scatter]
            turns = EC // BODY
            rec = k.gat[:, :, 0:full]
            cols = k.pos[scatter]

            def stage_half(act, i, h):
                at = bass.ds(i * BODY + h * HALF, HALF)
                act.activation(k.stage[0:EP, h * HALF:(h + 1) * HALF], cols[:, at], ACT.Copy).then_inc(staged, 1)
                for m, field in enumerate(fields[scatter]):
                    act.activation(rec[0:EP, h * HALF:(h + 1) * HALF, m], field[:, at], ACT.Copy)\
                        .then_inc(staged, 1)

            @block.scalar
            def _(act):
                if full > width:
                    act.activation(rec[0:EP, :, width], k.src_f[:, 0:BODY], ACT.Copy)
                for h in range(2):
                    stage_half(act, 0, h)
                with act.Fori(1, turns) as i:
                    for h in range(2):
                        act.wait_ge(scattered[h], i * (16 * HALF))
                        stage_half(act, i, h)

            def scatter_half(pool, h):
                for m in range(h * HALF, (h + 1) * HALF):
                    pool.indirect_dma_start(
                        target[scatter], bass.IndirectOffsetOnAxis(k.stage[0:EP, m:m + 1], axis=0),
                        rec[0:EP, m, :], None).then_inc(scattered[h], 16)

            def scatters(pool):
                for h in range(2):
                    pool.wait_ge(staged, (width + 1) * (h + 1))
                    scatter_half(pool, h)
                with pool.Fori(1, turns) as i:
                    for h in range(2):
                        pool.wait_ge(staged, i * (2 * (width + 1)) + (width + 1) * (h + 1))
                        pool.sem_inc(k.passed, 1)
                        scatter_half(pool, h)
                for h in range(2):
                    pool.wait_ge(scattered[h], turns * 16 * HALF)

            @block.gpsimd
            def _(pool):
                scatters(pool)


def degree_and_lists_phase(nc, k):
    hot, taken, zeroed, summed = (k.sem("deg_" + n) for n in ("hot", "taken", "zeroed", "summed"))
    link = Link(k.sem("deg_step"))
    lo = k.wk[:, 0:G * C].bitcast(BF16).rearrange("p (r c) -> p r c", r=4)
    hi = k.wk[:, G * C:2 * G * C].bitcast(BF16).rearrange("p (r c) -> p r c", r=4)
    dest = k.psum[7][:, 0:NB]
    flat = k.wk[:, 2 * G * C:3 * G * C].bitcast(BF16)[0:EP, 0:P]
    with nc.Block() as block:
        @block.vector
        def _(dve):
            dve.memset(flat, 0.0).then_inc(zeroed, 1)
            with dve.Fori(0, EC // 4) as i:
                for r in range(4):
                    dve.wait_ge(taken, i * 4 + r + 1)
                    dve.tensor_scalar(lo[0:EP, r, :], k.ramp[0:EP, :], k.dloc[:, bass.ds(i * 4 + r, 1)], None,
                                      ALU.is_equal).then_inc(hot, 1)
                    dve.tensor_scalar(hi[0:EP, r, 0:NB], k.ramp[0:EP, 0:NB], k.dhi[:, bass.ds(i * 4 + r, 1)],
                                      None, ALU.is_equal).then_inc(hot, 1)
            dve.wait_ge(summed, 1)
            link(dve, dve.tensor_copy(k.deg[:, :], dest))

        @block.tensor
        def _(pe):
            pe.wait_ge(zeroed, 1)
            pe.matmul(dest, flat, flat[:, 0:NB], start=True, stop=False, skip_group_check=True)\
                .then_inc(taken, 4)
            with pe.Fori(0, EC // 4) as i:
                for r in range(4):
                    pe.wait_ge(hot, i * 8 + 2 * (r + 1))
                    pe.matmul(dest, lo[0:EP, r, :], hi[0:EP, r, 0:NB], start=False, stop=False,
                              skip_group_check=True).then_inc(taken, 1)
            pe.matmul(dest, flat, flat[:, 0:NB], start=False, stop=True, skip_group_check=True)\
                .then_inc(summed, 1)


def prepare_phase(nc, k):
    turned, copied, summed, spread, plus_one, rooted = (k.sem("prep_" + n) for n in (
        "turned", "copied", "summed", "spread", "plus_one", "rooted"))
    link = Link(k.sem("prep_step"))
    turn = ("L2_gnn_Wq", "L2_gnn_Wk", "L2_gnn_Wv", "L2_gnn_Wo")
    temb_rep = k.wk[:, 0:C]
    with nc.Block() as block:
        @block.tensor
        def _(pe):
            for m, n in enumerate(turn):
                pe.transpose(k.psum[0][:, m * C:(m + 1) * C], k.w[n][:, :], k.ident[:, :])
            pe.transpose(k.psum[1][:, 0:H2], k.we2[:, :], k.ident[0:H2, 0:H2]).then_inc(turned, 1)
            pe.wait_ge(spread, 1)
            pe.matmul(k.psum[2][:, 0:C], temb_rep, k.w["L0_gnn_Wt1"][:, :], start=True, stop=True)
            pe.matmul(k.psum[2][:, C:2 * C], temb_rep, k.w["L0_gnn_Wt2"][:, :], start=True, stop=True)\
                .then_inc(summed, 1)

        @block.scalar
        def _(act):
            act.wait_ge(plus_one, 1)
            act.activation(k.dinv[:, :], k.dinv[:, :], ACT.Sqrt).then_inc(rooted, 1)

        @block.vector
        def _(dve):
            dve.tensor_scalar(k.dinv[:, :], k.deg[:, :], 1.0, None, ALU.add).then_inc(plus_one, 1)
            dve.tensor_scalar(temb_rep, k.ones[:, :], k.temb[:, 0:1], None, ALU.mult).then_inc(spread, 1)
            dve.wait_ge(turned, 1)
            for m, n in enumerate(turn):
                dve.tensor_copy(k.w[n][:, :], k.psum[0][:, m * C:(m + 1) * C])
            dve.tensor_copy(k.we2t[:, :], k.psum[1][:, 0:H2])
            dve.wait_ge(rooted, 1)
            link(dve, dve.reciprocal(k.dinv[:, :], k.dinv[:, :]))
            dve.wait_ge(summed, 1)
            for m, (b, bt) in enumerate((("L0_gnn_b1", "L0_gnn_bt1"), ("L0_gnn_b2", "L0_gnn_bt2"))):
                link(dve, dve.tensor_tensor(k.v[b][:, :], k.v[b][:, :], k.v[bt][:, :], ALU.add))
                link(dve, dve.tensor_tensor(k.v[b][:, :], k.v[b][:, :], k.psum[2][:, m * C:(m + 1) * C],
                                            ALU.add))


def lists_phase(nc, k, which):
    n = "lists_" + which + "_"
    loaded, turned, copied, rowed, halved, sined = (k.sem(n + s) for s in (
        "loaded", "turned", "copied", "rowed", "halved", "sined"))
    link = Link(k.sem(n + "step"))
    full = {"dst": 2, "src": 4}[which]
    source = {"dst": k.by_dst_dram, "src": k.by_src_dram}[which]
    rec = k.acc[:, 0:T * full].rearrange("p (t f) -> p t f", f=full)
    w, hh = k.big[:, 0:T], k.big[:, T:2 * T]
    with nc.Block() as block:
        @block.sync
        def _(sp):
            sp.dma_start(rec, source.rearrange("(p t) f -> p t f", p=P)).then_inc(loaded, 16)
            sp.wait_ge(loaded, 16)
            if which == "src":
                for m in range(T // P):
                    sp.wait_ge(copied, m + 1)
                    sp.dma_start(k.w_rows_dram[m * P:(m + 1) * P, :], k.wk[:, m % 4 * P:(m % 4 + 1) * P])\
                        .then_inc(rowed, 16)
                    sp.wait_ge(rowed, 16 * (m + 1))

        @block.vector
        def _(dve):
            dve.wait_ge(loaded, 16)
            dve.tensor_copy(k.idx[:, 0:T], rec[:, :, 0])
            dve.memset(k.idx[:, T:T + HALF], 0)
            dve.tensor_copy(k.loc[:, 0:T], rec[:, :, 1])
            link(dve, dve.memset(k.loc[:, T:T + G], PAD))
            if which == "src":
                link(dve, dve.tensor_scalar(w, rec[:, :, 2], 0.5 / CUTOFF, None, ALU.mult))
                link(dve, dve.tensor_scalar(hh, w, ROUND, -ROUND, ALU.add, ALU.add))
                link(dve, dve.tensor_tensor(w, w, hh, ALU.subtract))
                link(dve, dve.tensor_scalar(hh, w, -1.0, None, ALU.mult))
                link(dve, dve.tensor_tensor(w, w, hh, ALU.max))
                link(dve, dve.tensor_scalar(w, w, -2.0 * math.pi, 0.5 * math.pi, ALU.mult, ALU.add))
                dve.tensor_scalar(w, w, 1.5707963, -1.5707963, ALU.min, ALU.max).then_inc(halved, 1)
                dve.wait_ge(sined, 1)
                link(dve, dve.tensor_scalar(w, w, 0.5, 0.5, ALU.mult, ALU.add))
                link(dve, dve.scalar_tensor_tensor(k.cut[:, :], rec[:, :, 2], CUTOFF, w, ALU.is_lt, ALU.mult))
                for m in range(T // P):
                    dve.wait_ge(turned, m + 1)
                    if m >= 4:
                        dve.wait_ge(rowed, 16 * (m - 3))
                    dve.tensor_copy(k.wk[:, m % 4 * P:(m % 4 + 1) * P], k.psum[m % 2][:, 0:P])\
                        .then_inc(copied, 1)

        if which == "src":
            @block.scalar
            def _(act):
                act.wait_ge(halved, 1)
                act.activation(w, w, ACT.Sin).then_inc(sined, 1)

            @block.tensor
            def _(pe):
                pe.wait_ge(loaded, 16)
                for m in range(T // P):
                    if m >= 2:
                        pe.wait_ge(copied, m - 1)
                    pe.transpose(k.psum[m % 2][:, 0:P], rec[:, m * P:(m + 1) * P, 2], k.ident[:, :])\
                        .then_inc(turned, 1)


def edge_bias_phase(nc, k):
    rows, outer, hidden, mixed, added = (k.sem("bias_" + n) for n in (
        "rows", "outer", "hidden", "mixed", "added"))
    link = Link(k.sem("bias_step"))
    W = 4
    wrow = k.acc[0:1, 0:2 * W * P].rearrange("o (r c) -> o r c", r=2)
    hid = k.acc[:, 2 * W * P:4 * W * P].rearrange("p (r c) -> p r c", r=2)
    turns = T // W // 2
    row_sem = [rows, k.sem("bias_rows1")]
    with nc.Block() as block:
        @block.sync
        def _(sp):
            def body(i, first):
                for r in range(2):
                    if not first:
                        sp.wait_ge(outer, i * 2 + r - 1)
                    sp.dma_start(wrow[:, r, :], k.w_rows_dram[bass.ds((i * 2 + r) * W, W), :]
                                 .rearrange("(o t) q -> o (t q)", o=1)).then_inc(row_sem[r], 16)
            body(0, True)
            with sp.Fori(1, turns) as i:
                body(i, False)

        @block.tensor
        def _(pe):
            def body(i, first):
                for r in range(2):
                    pe.wait_ge(row_sem[r], i * 16 + 16)
                    if not first:
                        pe.wait_ge(hidden, i * 2 + r - 1)
                    pe.matmul(k.psum[r][:, :], k.we1[:, :], wrow[:, r, :], start=True, stop=True)\
                        .then_inc(outer, 1)
                    pe.wait_ge(hidden, i * 2 + r + 1)
                    if not first:
                        pe.wait_ge(added, i * 2 + r - 1)
                    for t in range(W):
                        last = pe.matmul(k.psum[2 + r][:, t * H2:(t + 1) * H2], hid[:, r, t * P:(t + 1) * P],
                                         k.we2t[:, :], start=True, stop=True)
                    last.then_inc(mixed, 1)
            body(0, True)
            with pe.Fori(1, turns) as i:
                body(i, False)

        @block.scalar
        def _(act):
            def body(i, first):
                for r in range(2):
                    act.wait_ge(outer, i * 2 + r + 1)
                    if not first:
                        act.wait_ge(mixed, i * 2 + r - 1)
                    act.activation(hid[:, r, :], k.psum[r][:, :], ACT.Silu, bias=k.be1[:, 0:1])\
                        .then_inc(hidden, 1)
            body(0, True)
            with act.Fori(1, turns) as i:
                body(i, False)

        @block.vector
        def _(dve):
            b2 = k.be2[:, :].unsqueeze(1).to_broadcast([P, W, H2])
            with dve.Fori(0, turns) as i:
                for r in range(2):
                    dve.wait_ge(mixed, i * 2 + r + 1)
                    dve.tensor_tensor(
                        k.big[:, bass.ds((i * 2 + r) * (W * H2), W * H2)].rearrange("p (t h) -> p t h", h=H2),
                        k.psum[2 + r][:, 0:W * H2].rearrange("p (t h) -> p t h", h=H2), b2, ALU.add)\
                        .then_inc(added, 1)
            dve.wait_ge(added, turns * 2)
            neg = k.acc[:, 4 * W * P:4 * W * P + T]
            lg = k.big[:, :].rearrange("p (t h) -> p t h", h=H2)
            link(dve, dve.tensor_scalar(neg, k.loc[:, 0:T], float(P), NEG, ALU.is_ge, ALU.mult))
            link(dve, dve.tensor_tensor(lg, lg, neg.unsqueeze(2).to_broadcast([P, T, H2]), ALU.add))


def pass_phase(nc, k, name, which, table, row, kind):
    n = name + "_"
    staged, hot, turned, copied, looked, scored, weighed, ready, matched, added = (k.sem(n + s) for s in (
        "staged", "hot", "turned", "copied", "looked", "scored", "weighed", "ready", "matched", "added"))
    link, plink = Link(k.sem(n + "step")), None
    base = k.gathered_base
    k.gathered_base += 16 * IT
    width = {"sum": C, "gat": A1, "value": A2, "max": 0, "logit": 0}[kind]
    looks = {"gat": 2 * H1, "logit": C}.get(kind, 0)
    near = {"gat": k.nodev[:, :, :].rearrange("p b c -> p (b c)"),
            "logit": k.h[:, :, :].rearrange("p b c -> p (b c)")}.get(kind)
    blocks = k.block_of[which]
    agg, tb, vb = k.psum[0:2], k.psum[2:4], k.psum[4:6]
    diag = k.acc[:, 0:4 * H1 * P].rearrange("p (s h c) -> p s h c", s=4, h=H1)
    peaks = k.wk[:, 0:H1]
    z = k.wk[:, 0:2 * G * H1].rearrange("p (s t h) -> p s t h", s=2, h=H1)
    prod = k.wk[:, G * C:2 * G * C].rearrange("p (t c) -> p t c", t=G)
    qk = k.wk[:, 0:G * H2]

    def turns(eng, body):
        body(0, True)
        with eng.Fori(1, IT) as i:
            body(i, False)

    def arrived(eng, i, j):
        for t in range(G):
            eng.wait_ge(k.gathered[G * j + t], i * 16 + base + 16)

    used = {"logit": scored}.get(kind, matched)

    with nc.Block() as block:
        @block.gpsimd
        def _(pool):
            with pool.Fori(0, IT) as i:
                for h in range(2):
                    pool.wait_ge(staged, i * 2 + h + 1)
                    pool.sem_inc(k.passed, 1)
                    for m in range(h * HALF, (h + 1) * HALF):
                        pool.indirect_dma_start(
                            k.gat[:, m, 0:row], None, table,
                            bass.IndirectOffsetOnAxis(k.stage[:, m:m + 1], axis=0)).then_inc(k.gathered[m], 16)

        @block.scalar
        def _(act):
            def stage_half(i, h, first):
                if not first:
                    act.wait_ge(used, i * GB + (h - 1) * (GB // 2))
                act.activation(k.stage[:, h * HALF:(h + 1) * HALF], k.idx[:, bass.ds(i * BODY + h * HALF, HALF)],
                               ACT.Copy).then_inc(staged, 1)

            def turn_hot(g, j):
                act.wait_ge(turned, g + 1)
                act.activation(k.hot_t[:, j % 2, :], tb[j % 2][:, 0:G * P], ACT.Copy).then_inc(copied, 1)

            def body(i, first):
                if first:
                    stage_half(0, 0, True)
                    stage_half(0, 1, True)
                    if looks:
                        turn_hot(0, 0)
                for j in range(GB):
                    g = i * GB + j
                    if not first and j == 1:
                        stage_half(i, 1, False)
                    if j == GB // 2 + 1:
                        stage_half(i + 1, 0, False)
                    if kind == "max":
                        arrived(act, i, j)
                        if not first or j >= 2:
                            act.wait_ge(matched, g - 1)
                        for t in range(G):
                            for hd in range(H1):
                                last = act.activation(diag[:, G * (j % 2) + t, hd, :], k.ident[:, :], ACT.Copy,
                                                      scale=k.gat[:, G * j + t, hd:hd + 1])
                        last.then_inc(ready, 1)
                    if looks:
                        turn_hot(g + 1, j + 1)
                    if kind == "gat":
                        act.wait_ge(scored, g + 1)
                        act.activation(k.gat[:, G * j:G * j + G, C:A1], z[:, 0, :, :], ACT.Exp)\
                            .then_inc(weighed, 1)
            turns(act, body)

        @block.tensor
        def _(pe):
            def look(g, j):
                b = pe.value_load(blocks[0:1, bass.ds(g, 1)], min_val=0, max_val=NB - 1)
                pe.wait_ge(hot, g + 1)
                for t in range(G):
                    last = pe.transpose(tb[j % 2][:, t * P:(t + 1) * P], k.oneh[:, (G * j + t) % HALF, :],
                                        k.ident[:, :])
                last.then_inc(turned, 1)
                pe.wait_ge(copied, g + 1)
                for t in range(G):
                    last = pe.matmul(vb[j % 2][:, t * looks:(t + 1) * looks],
                                     k.hot_t[:, j % 2, t * P:(t + 1) * P], near[:, bass.ds(b * looks, looks)],
                                     start=True, stop=True)
                last.then_inc(looked, 1)

            def body(i, first):
                if looks and first:
                    look(0, 0)
                for j in range(GB):
                    g = i * GB + j
                    if looks:
                        if kind == "logit" and (not first or j >= 1):
                            pe.wait_ge(scored, g)
                        look(g + 1, j + 1)
                    if kind == "logit":
                        continue
                    pe.wait_ge(hot, g + 1)
                    if not first or j >= 2:
                        pe.wait_ge(added, g - 1)
                    if kind == "sum":
                        arrived(pe, i, j)
                    else:
                        pe.wait_ge(ready, g + 1)
                    for t in range(G):
                        oh = k.oneh[:, (G * j + t) % HALF, :]
                        if kind == "max":
                            rhs = diag[:, G * (j % 2) + t, :, :].rearrange("p h c -> p (h c)")
                            last = pe.matmul(k.psum[G * (j % 2) + t][:, :], oh, rhs, start=True, stop=True)
                        else:
                            last = pe.matmul(agg[j % 2][:, 0:width], oh, k.gat[:, G * j + t, 0:width],
                                             start=(t == 0), stop=(t == G - 1))
                    last.then_inc(matched, 1)
            turns(pe, body)

        @block.vector
        def _(dve):
            def make_hot(g, i, j):
                for t in range(G):
                    last = dve.tensor_scalar(k.oneh[:, (G * j + t) % HALF, :], k.ramp[:, :],
                                             k.loc[:, bass.ds(i * BODY + G * j + t, 1)], None, ALU.is_equal)
                last.then_inc(hot, 1)

            def add(g, j):
                b = dve.value_load(blocks[0:1, bass.ds(g, 1)], min_val=0, max_val=NB - 1)
                dve.wait_ge(matched, g + 1)
                if kind == "max":
                    view = k.psum_pair[j % 2].rearrange("p (t h c) -> p h t c", t=G, h=H1)
                    link(dve, dve.tensor_reduce(peaks, view, AX.XY, ALU.max))
                    mine = k.maxa[:, bass.ds(b * H1, H1)]
                    dve.tensor_tensor(mine, mine, peaks, ALU.max).then_inc(added, 1)
                else:
                    mine = k.acc[:, bass.ds(b * width, width)]
                    dve.tensor_tensor(mine, mine, agg[j % 2][:, 0:width], ALU.add).then_inc(added, 1)
                dve.wait_ge(added, g + 1)

            def score_gat(i, g, j):
                v = vb[j % 2][:, 0:G * looks].rearrange("p (t c) -> p t c", t=G)
                arrived(dve, i, j)
                dve.wait_ge(looked, g + 1)
                link(dve, dve.tensor_tensor(z[:, 0, :, :], k.gat[:, G * j:G * j + G, C:A1], v[:, :, 0:H1], ALU.add))
                link(dve, dve.scalar_tensor_tensor(z[:, 1, :, :], z[:, 0, :, :], 0.2, z[:, 0, :, :], ALU.mult,
                                                   ALU.max))
                link(dve, dve.tensor_tensor(z[:, 1, :, :], z[:, 1, :, :], v[:, :, H1:2 * H1], ALU.subtract))
                dve.tensor_scalar(z[:, 0, :, :], z[:, 1, :, :], 0.0, None, ALU.min).then_inc(scored, 1)

            def message(i, g, j, heads, dim):
                rows = k.gat[:, G * j:G * j + G, 0:C].rearrange("p t (h c) -> p t h c", h=heads)
                wts = k.gat[:, G * j:G * j + G, C:C + heads].unsqueeze(3).to_broadcast([P, G, heads, dim])
                dve.tensor_tensor(rows, rows, wts, ALU.mult).then_inc(ready, 1)

            def logit(i, g, j):
                v = vb[j % 2][:, 0:G * looks].rearrange("p (t c) -> p t c", t=G)
                arrived(dve, i, j)
                dve.wait_ge(looked, g + 1)
                link(dve, dve.tensor_tensor(prod, k.gat[:, G * j:G * j + G, 0:C], v, ALU.mult))
                dve.tensor_reduce(qk, prod.rearrange("p t (h d) -> p (t h) d", d=D2), AX.X, ALU.add)\
                    .then_inc(scored, 1)
                dve.wait_ge(scored, g + 1)
                at = (i * BODY + G * j) * H2
                link(dve, dve.scalar_tensor_tensor(qk, qk, 1.0 / math.sqrt(D2), k.big[:, bass.ds(at, G * H2)],
                                                   ALU.mult, ALU.add))
                for t in range(G):
                    last = dve.tensor_scalar(k.big[:, bass.ds(at + t * H2, H2)], qk[:, t * H2:(t + 1) * H2],
                                             k.cut[:, bass.ds(i * BODY + G * j + t, 1)], None, ALU.mult)
                link(dve, last)

            per = {"sum": 0, "max": 1, "gat": 3, "logit": 3, "value": 1}[kind]

            def body(i, first):
                if first:
                    if kind == "max":
                        link(dve, dve.tensor_copy(k.maxa[:, :], k.asrc[:, :, :].rearrange("p b h -> p (b h)")))
                    elif width:
                        link(dve, dve.memset(k.acc[:, 0:NB * width], 0.0))
                    make_hot(0, 0, 0)
                else:
                    link.loop(i - 1, per * GB)
                for j in range(GB):
                    g = i * GB + j
                    if kind == "gat":
                        score_gat(i, g, j)
                    make_hot(g + 1, i, j + 1)
                    if kind in ("sum", "max", "gat", "value") and not (first and j == 0):
                        add(g - 1, j - 1)
                    if kind == "gat":
                        dve.wait_ge(weighed, g + 1)
                        message(i, g, j, H1, D1)
                    if kind == "value":
                        arrived(dve, i, j)
                        at = (i * BODY + G * j) * H2
                        link(dve, copy(
                            dve, k.gat[:, G * j:G * j + G, C:A2],
                            k.big[:, bass.ds(at, G * H2)].rearrange("p (t h) -> p t h", h=H2)))
                        message(i, g, j, H2, D2)
                    if kind == "logit":
                        logit(i, g, j)
            turns(dve, body)
            link.end(IT - 1)
            if kind != "logit":
                add(NG - 1, GB - 1)


class Chunk:

    def __init__(self, nc, k, name):
        self.nc, self.k, self.name = nc, k, name
        self.link = Link(k.sem(name + "_step"))
        self.rows_ready, self.turned, self.copied, self.product, self.asked, self.given, self.to_store, \
            self.stored = (k.sem(f"{name}_{s}") for s in (
                "rows_ready", "turned", "copied", "product", "asked", "given", "to_store", "stored"))
        self.room = k.sem(name + "_room")
        f = k.chunk_room
        w = BC * C
        self.y, self.yt, self.s, self.o = (f[:, m * w:(m + 1) * w].rearrange("p (b c) -> p b c", c=C)
                                           for m in range(4))

    def ask(self, dve, i, n, per):
        dve.wait_ge(self.given, i * per + n)

    def norm(self, dve, i, n, per, src, dst):
        k, link, st = self.k, self.link, self.k.st
        for b in range(BC):
            last = dve.bn_stats(st[:, b, 0:6], src[:, b, :])
        link(dve, last)
        dve.sem_inc(k.passed, 1)
        for b in range(BC):
            last = dve.bn_aggr(st[:, b, 6:8], st[:, b, 0:6])
        link(dve, last)
        dve.tensor_scalar(st[:, :, 8], st[:, :, 7], EPS, None, ALU.add).then_inc(self.asked, 1)
        self.ask(dve, i, n, per)
        link(dve, dve.reciprocal(st[:, :, 10], st[:, :, 9]))
        for b in range(BC):
            last = dve.tensor_scalar(dst[:, b, :], src[:, b, :], st[:, b, 6:7], st[:, b, 10:11],
                                     ALU.subtract, ALU.mult)
        link(dve, last)

    def bc(self, vector):
        return vector.unsqueeze(1).to_broadcast([P, BC, C])


def by_blocks(tensor, i):
    return tensor[:, bass.ds(i * BC, BC), :]


def by_heads(rows, heads):
    return rows.rearrange("p b (h d) -> p b h d", h=heads)


def halves():
    return ((0, 0, 4), (1, 4, BC))


def dense_phase(nc, k, name, before, after, mats, jobs, stores=(), turn=1, second=None):
    c = Chunk(nc, k, name)
    link = c.link
    with nc.Block() as block:
        @block.vector
        def _(dve):
            with dve.Fori(0, NCH) as i:
                link.loop(i, before.links + after.links)
                before(c, dve, i)
                if mats:
                    dve.wait_ge(c.product, i + 1)
                after(c, dve, i)
            link.end(NCH)

        @block.scalar
        def _(act):
            with act.Fori(0, NCH) as i:
                for n, job in enumerate(jobs):
                    if job == "turn":
                        act.wait_ge(c.turned, i + 1)
                        for bank, lo, up in halves():
                            last = act.activation(c.yt[:, lo:up, :], k.psum[bank][:, 0:(up - lo) * C]
                                                  .rearrange("p (b c) -> p b c", c=C), ACT.Copy)
                        last.then_inc(c.copied, 1)
                    else:
                        m = len([q for q in jobs[:n + 1] if q != "turn"])
                        act.wait_ge(c.asked, i * len([q for q in jobs if q != "turn"]) + m)
                        job(c, act).then_inc(c.given, 1)

        if mats:
            @block.tensor
            def _(pe):
                with pe.Fori(0, NCH) as i:
                    pe.wait_ge(c.rows_ready, i + 1)
                    for bank, lo, up in halves():
                        for b in range(lo, up):
                            last = pe.transpose(k.psum[bank][:, (b - lo) * C:(b - lo + 1) * C], c.y[:, b, :],
                                                k.ident[:, :])
                    last.then_inc(c.turned, 1)
                    pe.wait_ge(c.copied, i + 1)
                    for m, mat in enumerate(mats):
                        for bank, lo, up in halves():
                            for b in range(lo, up):
                                last = pe.matmul(k.psum[2 + 2 * m + bank][:, (b - lo) * C:(b - lo + 1) * C],
                                                 c.yt[:, b, :], mat[:, :], start=True, stop=True)
                    last.then_inc(c.product, 1)

        if stores:
            @block.sync
            def _(sp):
                sp.sem_inc(c.room, 1)
                with sp.Fori(0, NCH) as i:
                    sp.wait_ge(c.to_store, i + 1)
                    for table, rows in stores:
                        sp.dma_start(table.rearrange("(b p) c -> p b c", p=P)[:, bass.ds(i * BC, BC), :], rows(c))\
                            .then_inc(c.stored, 16)
                    sp.wait_ge(c.stored, i * (16 * len(stores)) + 16 * len(stores))
                    sp.sem_inc(c.room, 1)


def product(k, m):
    return k.psum_pair[1 + m][:, 0:BC * C].rearrange("p (b c) -> p b c", c=C)


def sqrt_job(c, act):
    return act.activation(c.k.st[:, :, 9], c.k.st[:, :, 8], ACT.Sqrt)


def silu_job(c, act):
    return act.activation(c.s, c.s, ACT.Silu)


def stage_gcn_in(k):
    def before(c, dve, i):
        link = c.link
        c.norm(dve, i, 1, 1, by_blocks(k.x, i), c.y)
        link(dve, dve.tensor_tensor(c.y, c.y, c.bc(k.v["L0_gnn_g1"][:, :]), ALU.mult))
        dve.tensor_tensor(c.y, c.y, c.bc(k.v["L0_gnn_bn1"][:, :]), ALU.add).then_inc(c.rows_ready, 1)
    before.links = 5
    return before, gcn_out(k)


def gcn_out(k):
    def after(c, dve, i):
        link = c.link
        h = by_blocks(k.h, i)
        link(dve, copy(dve, h, product(k, 0)))
        dve.wait_ge(c.room, i + 1)
        inv = k.dinv[:, bass.ds(i * BC, BC)].unsqueeze(2).to_broadcast([P, BC, C])
        dve.tensor_tensor(c.o, h, inv, ALU.mult).then_inc(c.to_store, 1)
    after.links = 1
    return after


def gcn_sum(k, c, dve, i, bias):
    link = c.link
    inv = k.dinv[:, bass.ds(i * BC, BC)].unsqueeze(2).to_broadcast([P, BC, C])
    link(dve, dve.tensor_tensor(c.s, by_blocks(k.h, i), inv, ALU.mult))
    acc = k.acc[:, bass.ds(i * (BC * C), BC * C)].rearrange("p (b c) -> p b c", c=C)
    link(dve, dve.tensor_tensor(c.s, c.s, acc, ALU.add))
    link(dve, dve.tensor_tensor(c.s, c.s, inv, ALU.mult))
    dve.tensor_tensor(c.s, c.s, c.bc(bias[:, :]), ALU.add).then_inc(c.asked, 1)
    c.ask(dve, i, 1, 2)


def stage_gcn_mid(k):
    def before(c, dve, i):
        link = c.link
        gcn_sum(k, c, dve, i, k.v["L0_gnn_b1"])
        c.norm(dve, i, 2, 2, c.s, c.y)
        link(dve, dve.tensor_tensor(c.y, c.y, c.bc(k.v["L0_gnn_g2"][:, :]), ALU.mult))
        dve.tensor_tensor(c.y, c.y, c.bc(k.v["L0_gnn_bn2"][:, :]), ALU.add).then_inc(c.rows_ready, 1)
    before.links = 8
    return before, gcn_out(k)


def stage_gcn_out(k):
    def before(c, dve, i):
        link = c.link
        gcn_sum(k, c, dve, i, k.v["L0_gnn_b2"])
        x = by_blocks(k.x, i)
        link(dve, dve.tensor_tensor(c.s, c.s, x, ALU.add))
        link(dve, dve.tensor_tensor(c.s, c.s, x, ALU.add))
        c.norm(dve, i, 2, 2, c.s, x)
        copy(dve, c.y, x).then_inc(c.rows_ready, 1)
    before.links = 9

    def after(c, dve, i):
        link = c.link
        h = by_blocks(k.h, i)
        link(dve, copy(dve, h, product(k, 0)))
        link(dve, dve.tensor_tensor(c.s, h, c.bc(k.v["L1_gnn_att_src"][:, :]), ALU.mult))
        link(dve, dve.tensor_reduce(by_blocks(k.asrc, i), by_heads(c.s, H1), AX.X, ALU.add))
        link(dve, dve.tensor_tensor(c.s, h, c.bc(k.v["L1_gnn_att_dst"][:, :]), ALU.mult))
        link(dve, dve.tensor_reduce(by_blocks(k.nodev, i)[:, :, 0:H1], by_heads(c.s, H1), AX.X, ALU.add))
    after.links = 5
    return before, after


def extreme_phase(nc, k, name, src, width, use):
    turned, diagonal, spread, ready = (k.sem(f"{name}_{s}") for s in ("turned", "diagonal", "spread", "ready"))
    link = Link(k.sem(name + "_step"))
    part = k.tmp[:, 32:32 + width]
    top = k.tmp[0:width, 64:65]
    diag = k.tmp[0:width, 96:96 + width]
    with nc.Block() as block:
        @block.vector
        def _(dve):
            src(dve, link, part)
            dve.sem_inc(ready, 1)
            dve.wait_ge(turned, 1)
            link(dve, dve.tensor_reduce(top, k.psum[0][0:width, 0:P], AX.X, ALU.max))
            dve.tensor_scalar(diag, k.ident[0:width, 0:width], top, None, ALU.mult).then_inc(diagonal, 1)
            dve.wait_ge(spread, 1)
            link(dve, dve.tensor_copy(k.tmp[:, 0:width], k.psum[1][:, 0:width]))
            use(dve, link)

        @block.tensor
        def _(pe):
            pe.wait_ge(ready, 1)
            pe.transpose(k.psum[0][0:width, 0:P], part, k.ident[:, :]).then_inc(turned, 1)
            pe.wait_ge(diagonal, 1)
            pe.matmul(k.psum[1][:, 0:width], k.ones[0:width, :], diag, start=True, stop=True)\
                .then_inc(spread, 1)


def shift_phase(nc, k):
    stored, to_store, room = k.sem("shift_stored"), k.sem("shift_to_store"), k.sem("shift_room")

    def src(dve, link, part):
        link(dve, dve.tensor_reduce(part, k.asrc[:, :, :].rearrange("p b h -> p h b"), AX.X, ALU.min))
        link(dve, dve.tensor_scalar(part, part, -1.0, None, ALU.mult))

    def use(dve, link):
        low = k.tmp[:, 0:H1].unsqueeze(1).to_broadcast([P, NB, H1])
        link(dve, dve.tensor_tensor(k.asrc[:, :, :], k.asrc[:, :, :], low, ALU.add))
        link(dve, dve.tensor_tensor(k.nodev[:, :, 0:H1], k.nodev[:, :, 0:H1], low, ALU.subtract))
        link(dve, dve.tensor_scalar(k.asrc[:, :, :], k.asrc[:, :, :], 0.0, None, ALU.max))
    extreme_phase(nc, k, "low", src, H1, use)
    with nc.Block() as block:
        @block.sync
        def _(sp):
            rows = k.tab_h_dram.rearrange("(b p) c -> p b c", p=P)
            with nc.allow_non_contiguous_dma(reason="four floats beside each row"):
                sp.dma_start(k.tab_a_dram.rearrange("(b p) c -> p b c", p=P), k.asrc[:, :, :])\
                    .then_inc(stored, 16)
                sp.dma_start(rows[:, :, 0:C], k.h[:, :, :]).then_inc(stored, 16)
                sp.dma_start(rows[:, :, C:A1], k.asrc[:, :, :]).then_inc(stored, 16)
            sp.wait_ge(stored, 48)


def leaky(dve, link, out, rows, tmp):
    link(dve, dve.tensor_scalar(tmp, rows, 0.2, None, ALU.mult))
    link(dve, dve.tensor_tensor(out, rows, tmp, ALU.max))


def gat_maximum_phase(nc, k):
    asked, given = k.sem("self_asked"), k.sem("self_given")
    link = Link(k.sem("self_step"))
    with nc.Block() as block:
        d = k.nodev[:, :, 0:H1]
        m = k.nodev[:, :, H1:2 * H1]
        maxa = k.maxa[:, :].rearrange("p (b h) -> p b h", h=H1)
        tmp = k.wk[:, 0:NB * H1].rearrange("p (b h) -> p b h", h=H1)
        tmp2 = k.wk[:, NB * H1:2 * NB * H1].rearrange("p (b h) -> p b h", h=H1)

        @block.vector
        def _(dve):
            link(dve, dve.tensor_tensor(maxa, maxa, d, ALU.add))
            leaky(dve, link, m, maxa, tmp)
            link(dve, dve.tensor_tensor(tmp2, k.asrc[:, :, :], d, ALU.add))
            leaky(dve, link, maxa, tmp2, tmp)
            dve.tensor_tensor(maxa, maxa, m, ALU.subtract).then_inc(asked, 1)

        @block.scalar
        def _(act):
            act.wait_ge(asked, 1)
            act.activation(maxa, maxa, ACT.Exp).then_inc(given, 1)
            act.wait_ge(given, 1)


def stage_gat_out(k):
    def tanh_job(c, act):
        return act.activation(c.s, c.s, ACT.Tanh)

    def before(c, dve, i):
        link = c.link
        acc = k.acc[:, bass.ds(i * (BC * A1), BC * A1)].rearrange("p (b c) -> p b c", c=A1)
        own = k.maxa[:, bass.ds(i * (BC * H1), BC * H1)].rearrange("p (b h) -> p b h", h=H1)
        rep = own.unsqueeze(3).to_broadcast([P, BC, H1, D1])
        link(dve, dve.tensor_tensor(by_heads(c.s, H1), by_heads(by_blocks(k.h, i), H1), rep, ALU.mult))
        link(dve, dve.tensor_tensor(c.s, c.s, acc[:, :, 0:C], ALU.add))
        den = c.o[:, 0, 0:BC * H1].rearrange("p (b h) -> p b h", h=H1)
        link(dve, dve.tensor_tensor(den, own, acc[:, :, C:A1], ALU.add))
        link(dve, dve.tensor_scalar(den, den, 1e-16, None, ALU.add))
        link(dve, dve.reciprocal(den, den))
        link(dve, dve.tensor_tensor(by_heads(c.s, H1), by_heads(c.s, H1),
                                    den.unsqueeze(3).to_broadcast([P, BC, H1, D1]), ALU.mult))
        dve.tensor_tensor(c.s, c.s, c.bc(k.v["L1_gnn_bias"][:, :]), ALU.add).then_inc(c.asked, 1)
        c.ask(dve, i, 1, 2)
        x = by_blocks(k.x, i)
        link(dve, dve.tensor_tensor(c.s, c.s, x, ALU.add))
        c.norm(dve, i, 2, 2, c.s, x)
        copy(dve, c.y, x).then_inc(c.rows_ready, 1)
    before.links = 11

    def after(c, dve, i):
        link = c.link
        link(dve, dve.tensor_tensor(by_blocks(k.h, i), product(k, 0), c.bc(k.v["L2_gnn_bq"][:, :]), ALU.add))
        dve.wait_ge(c.room, i + 1)
        link(dve, dve.tensor_tensor(c.o, product(k, 1), c.bc(k.v["L2_gnn_bk"][:, :]), ALU.add))
        dve.tensor_tensor(c.s, product(k, 2), c.bc(k.v["L2_gnn_bv"][:, :]), ALU.add).then_inc(c.to_store, 1)
        dve.wait_ge(c.room, i + 2)
    after.links = 2
    return before, after, tanh_job


def softmax_phase(nc, k):
    lg = k.big[:, :].rearrange("p (t h) -> p t h", h=H2)

    def src(dve, link, part):
        link(dve, dve.tensor_reduce(part, k.big[:, :].rearrange("p (t h) -> p h t", h=H2), AX.X, ALU.max))

    def use(dve, link):
        top = k.tmp[:, 0:H2].unsqueeze(1).to_broadcast([P, T, H2])
        link(dve, dve.tensor_tensor(lg, lg, top, ALU.subtract))
    extreme_phase(nc, k, "top", src, H2, use)
    done = k.sem("exp_done")
    with nc.Block() as block:
        @block.scalar
        def _(act):
            act.activation(k.big[:, :], k.big[:, :], ACT.Exp).then_inc(done, 1)
            act.wait_ge(done, 1)


def stage_attention_out(k):
    def before(c, dve, i):
        link = c.link
        acc = k.acc[:, bass.ds(i * (BC * A2), BC * A2)].rearrange("p (b c) -> p b c", c=A2)
        den = c.s[:, 0, 0:BC * H2].rearrange("p (b h) -> p b h", h=H2)
        link(dve, dve.tensor_scalar(den, acc[:, :, C:A2], 1e-8, None, ALU.add))
        link(dve, dve.reciprocal(den, den))
        dve.tensor_tensor(by_heads(c.y, H2), by_heads(acc[:, :, 0:C], H2),
                          den.unsqueeze(3).to_broadcast([P, BC, H2, D2]), ALU.mult).then_inc(c.rows_ready, 1)
    before.links = 2

    def after(c, dve, i):
        link = c.link
        x = by_blocks(k.x, i)
        link(dve, dve.tensor_tensor(c.s, product(k, 0), c.bc(k.v["L2_gnn_bo"][:, :]), ALU.add))
        link(dve, dve.tensor_tensor(c.s, c.s, x, ALU.add))
        c.norm(dve, i, 1, 2, c.s, c.s)
        link(dve, dve.tensor_tensor(c.s, c.s, c.bc(k.v["L2_gnn_ln_g"][:, :]), ALU.mult))
        link(dve, dve.tensor_tensor(c.s, c.s, c.bc(k.v["L2_gnn_ln_b"][:, :]), ALU.add))
        link(dve, dve.tensor_tensor(c.s, c.s, x, ALU.add))
        c.norm(dve, i, 2, 2, c.s, x)
        dve.wait_ge(c.room, i + 1)
        copy(dve, c.o, x).then_inc(c.to_store, 1)
    after.links = 13
    return before, after


def stage_message_mid(k):
    def before(c, dve, i):
        copy(dve, c.y, by_blocks(k.x, i)).then_inc(c.rows_ready, 1)
    before.links = 0

    def after(c, dve, i):
        link = c.link
        link(dve, dve.tensor_tensor(c.s, product(k, 0), c.bc(k.v["L3_gnn_b_msg"][:, :]), ALU.add))
        times = k.deg[:, bass.ds(i * BC, BC)].unsqueeze(2).to_broadcast([P, BC, C])
        link(dve, dve.tensor_tensor(by_blocks(k.h, i), c.s, times, ALU.mult))
        part = k.big[:, bass.ds(i * (BC * C), BC * C)].rearrange("p (b c) -> p b c", c=C)
        link(dve, dve.tensor_tensor(part, product(k, 1), c.bc(k.v["L3_gnn_b_upd"][:, :]), ALU.add))
        link(dve, dve.tensor_tensor(part, part, by_blocks(k.x, i), ALU.add))
    after.links = 4
    return before, after


def stage_message_sum(k):
    def before(c, dve, i):
        acc = k.acc[:, bass.ds(i * (BC * C), BC * C)].rearrange("p (b c) -> p b c", c=C)
        copy(dve, c.y, acc).then_inc(c.rows_ready, 1)
    before.links = 0

    def after(c, dve, i):
        c.link(dve, dve.tensor_tensor(by_blocks(k.h, i), by_blocks(k.h, i), product(k, 0), ALU.add))
    after.links = 1
    return before, after


def stage_message_out(k):
    def before(c, dve, i):
        copy(dve, c.y, by_blocks(k.h, i)).then_inc(c.rows_ready, 1)
    before.links = 0

    def after(c, dve, i):
        link = c.link
        part = k.big[:, bass.ds(i * (BC * C), BC * C)].rearrange("p (b c) -> p b c", c=C)
        link(dve, dve.tensor_tensor(c.s, part, product(k, 0), ALU.add))
        c.norm(dve, i, 1, 1, c.s, by_blocks(k.x, i))
    after.links = 5
    return before, after


def store_phase(nc, k):
    stored = k.sem("out_stored")
    with nc.Block() as block:
        @block.sync
        def _(sp):
            sp.dma_start(k.out[0:(NB - 1) * P, :].rearrange("(b p) c -> p b c", p=P), k.x[:, 0:NB - 1, :])\
                .then_inc(stored, 16)
            sp.dma_start(k.out[(NB - 1) * P:N, :], k.x[0:REM, NB - 1, :]).then_inc(stored, 16)
            sp.wait_ge(stored, 32)


def build(nc, a, out):
    with ExitStack() as ctx:
        k = allocate(nc, ctx, a, out)

        def run(phase, *args):
            phase(nc, k, *args)
            nc.clear_and_free_semaphores(k.phase_sems)
            k.phase_sems = []
            nc.all_engine_barrier()

        run(load_phase)
        run(fields_phase)
        run(rank_and_scatter_phase, "src", None)
        run(rank_and_scatter_phase, "dst", "src")
        run(rank_and_scatter_phase, None, "dst")
        run(degree_and_lists_phase)
        run(prepare_phase)
        run(lists_phase, "dst")
        run(dense_phase, "gcn_in", *stage_gcn_in(k), [k.w["L0_gnn_W1"]], [sqrt_job, "turn"],
                    [(k.tab_dram, lambda c: c.o)])
        run(pass_phase, "gcn1", "dst", k.tab_dram, C, "sum")
        run(dense_phase, "gcn_mid", *stage_gcn_mid(k), [k.w["L0_gnn_W2"]], [silu_job, sqrt_job, "turn"],
                    [(k.tab_dram, lambda c: c.o)])
        run(pass_phase, "gcn2", "dst", k.tab_dram, C, "sum")
        run(dense_phase, "gcn_out", *stage_gcn_out(k), [k.w["L1_gnn_W"]], [silu_job, sqrt_job, "turn"])
        run(shift_phase)
        run(pass_phase, "gat_max", "dst", k.tab_a_dram, H1, "max")
        run(gat_maximum_phase)
        run(pass_phase, "gat", "dst", k.tab_h_dram, A1, "gat")
        before, after, tanh_job = stage_gat_out(k)
        run(dense_phase, "gat_out", before, after, [k.w[n] for n in ("L2_gnn_Wq", "L2_gnn_Wk", "L2_gnn_Wv")],
                    [tanh_job, sqrt_job, "turn"], [(k.tab_k_dram, lambda c: c.o), (k.tab_v_dram, lambda c: c.s)])
        run(lists_phase, "src")
        run(edge_bias_phase)
        run(pass_phase, "logit", "src", k.tab_k_dram, C, "logit")
        run(softmax_phase)
        run(pass_phase, "value", "src", k.tab_v_dram, C, "value")
        run(dense_phase, "att_out", *stage_attention_out(k), [k.w["L2_gnn_Wo"]], ["turn", sqrt_job, sqrt_job],
                    [(k.tab_dram, lambda c: c.o)])
        run(lists_phase, "dst")
        run(dense_phase, "msg_mid", *stage_message_mid(k), [k.bot["L3_gnn_W_msg"], k.top["L3_gnn_W_upd"]],
                    ["turn"])
        run(pass_phase, "msg", "dst", k.tab_dram, C, "sum")
        run(dense_phase, "msg_sum", *stage_message_sum(k), [k.top["L3_gnn_W_msg"]], ["turn"])
        run(dense_phase, "msg_out", *stage_message_out(k), [k.bot["L3_gnn_W_upd"]], ["turn", sqrt_job])
        run(store_phase)


INPUTS = ("x", "src", "dst", "edge_weight1") + MATS + HALVES + VECS + ATTS + (
    "L0_gnn_t_emb", "L2_gnn_We1", "L2_gnn_be1", "L2_gnn_We2", "L2_gnn_be2")


def kernel(**inputs):
    import numpy as _np
    import concourse.bacc as _bacc
    from concourse.bass_utils import run_bass_kernel_spmd as _run

    nc = _bacc.Bacc("TRN2", target_bir_lowering=False, num_devices=1)
    arrays, args = {}, {}
    for name in INPUTS:
        arr = _np.ascontiguousarray(inputs[name])
        arrays[f"in_{name}"] = arr
        args[name] = nc.dram_tensor(f"in_{name}", arr.shape, mybir.dt.from_np(arr.dtype), kind="ExternalInput").ap()
    out = nc.dram_tensor("out", (N, C), F32, kind="ExternalOutput").ap()
    build(nc, args, out)
    return _run(nc, [arrays], core_ids=[0]).results[0]["out"]
```

```python
import itertools
import math
from contextlib import ExitStack

import concourse.bass as bass
from concourse import mybir

F32 = mybir.dt.float32
BF16 = mybir.dt.bfloat16
I32 = mybir.dt.int32
ALU = mybir.AluOpType
ACT = mybir.ActivationFunctionType
AX = mybir.AxisListType

P = 128
N = 6250
C = 128
E = 200000
NB = -(-N // P)
NP = NB * P
REM = N - (NB - 1) * P
BC = 7
NCH = NB // BC
EP = 125
EC = E // EP
G = 2
GE = G * P
GSH = GE.bit_length() - 1
H1, D1 = 4, 32
H2, D2 = 8, 16
A1 = C + H1
A2 = C + H2
BODY = 16
HALF = BODY // 2
GB = BODY // G
NG = -(-((E + NB * (GE - 1)) // GE) // GB) * GB
T = NG * G
IT = T // BODY
PAD = 200.0
EPS = 1e-5
NEG = -1e30
CUTOFF = 5.0
ROUND = 12582912.0

assert NB % BC == 0 and EP * EC == E and EC % BODY == 0 and T % P == 0

MATS = ("L0_gnn_W1", "L0_gnn_Wt1", "L0_gnn_W2", "L0_gnn_Wt2", "L1_gnn_W", "L2_gnn_Wq", "L2_gnn_Wk",
        "L2_gnn_Wv", "L2_gnn_Wo")
HALVES = ("L3_gnn_W_msg", "L3_gnn_W_upd")
VECS = ("L0_gnn_g1", "L0_gnn_bn1", "L0_gnn_b1", "L0_gnn_bt1", "L0_gnn_g2", "L0_gnn_bn2",
        "L0_gnn_b2", "L0_gnn_bt2", "L1_gnn_bias", "L2_gnn_bq", "L2_gnn_bk", "L2_gnn_bv",
        "L2_gnn_bo", "L2_gnn_ln_g", "L2_gnn_ln_b", "L3_gnn_b_msg", "L3_gnn_b_upd")
ATTS = ("L1_gnn_att_src", "L1_gnn_att_dst")


def copy(dve, out, rows):
    return dve.tensor_scalar(out, rows, 1.0, None, ALU.mult)


class Link:

    def __init__(self, sem):
        self.sem, self.base, self.n, self.turn, self.per = sem, 0, 0, 0, 0

    def loop(self, turn, per):
        self.base += self.n
        self.turn, self.per, self.n = turn, per, 0

    def end(self, turns):
        assert self.n == self.per, (self.n, self.per)
        self.base += turns * self.per
        self.turn, self.per, self.n = 0, 0, 0

    def __call__(self, eng, ins):
        ins.then_inc(self.sem, 1)
        self.n += 1
        eng.wait_ge(self.sem, self.turn * self.per + self.base + self.n)


class Bufs:
    pass


def allocate(nc, ctx, a, out):
    k = Bufs()
    k.a, k.out = a, out

    def sb(name, shape, dt=F32):
        return ctx.enter_context(nc.sbuf_tensor(name, shape, dt))

    def dram(name, shape):
        return nc.dram_tensor(name, shape, F32, kind="Internal").ap()

    numbers = itertools.count()
    k.phase_sems = []

    def phase_sem(name):
        k.phase_sems.append(nc.alloc_semaphore(name=f"{name}_{next(numbers)}"))
        return k.phase_sems[-1]
    k.sem = phase_sem
    k.by_dst_dram = dram("by_dst", (P * T, 2))
    k.by_src_dram = dram("by_src", (P * T, 4))
    k.w_rows_dram = dram("w_rows", (T, P))
    k.tab_dram = dram("tab", (NP, C))
    k.tab_a_dram = dram("tab_a", (NP, H1))
    k.tab_h_dram = dram("tab_h", (NP, A1))
    k.tab_k_dram = dram("tab_k", (NP, C))
    k.tab_v_dram = dram("tab_v", (NP, C))
    k.ramp_i = sb("ramp_i", [P, P], I32)
    k.row_i = sb("row_i", [P, 1], I32)
    k.ramp = sb("ramp", [P, P])
    k.row = sb("row", [P, 1])
    k.ident = sb("ident", [P, P])
    k.below = sb("below", [P, P])
    k.upto = sb("upto", [P, P])
    k.ones = sb("ones", [P, P])
    k.x = sb("x", [P, NB, C])
    k.h = sb("h", [P, NB, C])
    k.acc = sb("acc", [P, NB * A2])
    k.deg = sb("deg", [P, NB])
    k.dinv = sb("dinv", [P, NB])
    k.nodev = sb("nodev", [P, NB, 2 * H1])
    k.asrc = sb("asrc", [P, NB, H1])
    k.maxa = sb("maxa", [P, NB * H1])
    k.idx = sb("idx", [P, T + HALF], I32)
    k.loc = sb("loc", [P, T + G])
    k.cut = sb("cut", [P, T])
    k.block_of = {"dst": sb("block_dst", [1, NG + 1], I32), "src": sb("block_src", [1, NG + 1], I32)}
    k.big = sb("big", [P, T * H2])
    sizes = (BODY * A2, HALF * P, 2 * G * P, 4 * G * C)
    room = sb("room", [P, sum(sizes)])
    ends = [sum(sizes[:m + 1]) for m in range(4)]
    k.gat = room[:, 0:ends[0]].rearrange("p (m c) -> p m c", c=A2)
    k.oneh = room[:, ends[0]:ends[1]].rearrange("p (m c) -> p m c", c=P)
    k.hot_t = room[:, ends[1]:ends[2]].rearrange("p (m c) -> p m c", c=G * P)
    k.wk = room[:, ends[2]:ends[3]]
    k.chunk_room = room
    k.stage = sb("stage", [P, BODY], I32)
    k.tmp = sb("tmp", [P, 256])
    k.offs = sb("offs", [P, NB])
    k.st = sb("st", [P, BC, 16])
    k.psum_pair = [ctx.enter_context(nc.psum_tensor(f"banks{i}", [P, 1024], F32))[:, :] for i in range(4)]
    k.psum = [k.psum_pair[i // 2][:, i % 2 * 512:(i % 2 + 1) * 512] for i in range(8)]
    k.w = {n: sb("m_" + n, [P, C]) for n in MATS}
    k.top = {n: sb("t_" + n, [P, C]) for n in HALVES}
    k.bot = {n: sb("b_" + n, [P, C]) for n in HALVES}
    k.v = {n: sb("v_" + n, [P, C]) for n in VECS + ATTS}
    k.be2 = sb("be2", [P, H2])
    k.temb = sb("temb", [P, 1])
    k.be1 = sb("be1", [P, 1])
    k.we1 = sb("we1", [1, P])
    k.we2 = sb("we2", [H2, P])
    k.we2t = sb("we2t", [P, H2])
    f = [k.big[0:EP, i * EC:(i + 1) * EC] for i in range(6)]
    k.dst_f, k.w_f, k.sloc, k.shi, k.dhi, k.mask = f
    xx = k.x[:, :, :].rearrange("p b c -> p (b c)")
    k.src_f, k.dloc = xx[0:EP, 0:EC], xx[0:EP, EC:2 * EC]
    hh = k.h[:, :, :].rearrange("p b c -> p (b c)")
    k.zeros = hh[0:EP, 0:EC]
    k.pos = {"src": hh[0:EP, EC:2 * EC].bitcast(I32), "dst": hh[0:EP, 2 * EC:3 * EC].bitcast(I32)}
    k.raw_s, k.raw_d = k.acc[0:EP, 0:EC].bitcast(I32), k.acc[0:EP, EC:2 * EC].bitcast(I32)
    k.shifted = k.acc[0:EP, 2 * EC:3 * EC].bitcast(I32)
    k.scan, k.posf = k.acc[0:EP, 3 * EC:4 * EC], k.acc[0:EP, 0:EC]
    lasting = lambda name: ctx.enter_context(nc.semaphore(name))
    k.gathered = [lasting(f"gathered{i}") for i in range(BODY)]
    k.gathered_base = 0
    k.const = lasting("const")
    k.passed = lasting("passed")
    return k


def load_phase(nc, k):
    a = k.a
    loaded, iotas, filled, zero_done = (k.sem(n) for n in ("loaded", "iotas", "filled", "zero_done"))
    link = Link(k.sem("const_step"))
    pattern = k.h[:, :, :].rearrange("p b c -> p (b c)")
    with nc.Block() as block:
        @block.sync
        def _(sp):
            count = [0]

            def load(dst, src):
                sp.dma_start(dst, src).then_inc(loaded, 16)
                count[0] += 16
            load(k.raw_s, a["src"].rearrange("(p c) -> p c", p=EP))
            load(k.raw_d, a["dst"].rearrange("(p c) -> p c", p=EP))
            load(k.w_f, a["edge_weight1"].rearrange("(p c) o -> p (c o)", p=EP))
            for n in MATS:
                load(k.w[n][:, :], a[n])
            for n in HALVES:
                load(k.top[n][:, :], a[n][0:C, :])
                load(k.bot[n][:, :], a[n][C:2 * C, :])
            for n in VECS:
                load(k.v[n][:, :], a[n].partition_broadcast(P))
            for n in ATTS:
                load(k.v[n][:, :], a[n].rearrange("h c -> (h c)").partition_broadcast(P))
            load(k.be2[:, :], a["L2_gnn_be2"].partition_broadcast(P))
            load(k.temb[:, :], a["L0_gnn_t_emb"].rearrange("(c o) -> c o", o=1))
            load(k.be1[:, :], a["L2_gnn_be1"].rearrange("(c o) -> c o", o=1))
            load(k.we1[:, :], a["L2_gnn_We1"].rearrange("c o -> o c"))
            load(k.we2[:, :], a["L2_gnn_We2"])
            sp.wait_ge(loaded, count[0])

        @block.scalar
        def _(act):
            act.wait_ge(filled, 2)
            half = P * T // 2 // P
            rows = k.by_src_dram.rearrange("(p s r) f -> p s (r f)", p=P, s=2)
            for s in range(2):
                act.dma_start(rows[:, s, :], pattern[:, 0:half * 4]).then_inc(zero_done, 16)
            rows = k.by_dst_dram.rearrange("(p s r) f -> p s (r f)", p=P, s=2)
            for s in range(2):
                act.dma_start(rows[:, s, :], pattern[:, half * 4:half * 6]).then_inc(zero_done, 16)
            act.wait_ge(zero_done, 64)

        @block.gpsimd
        def _(pool):
            pool.iota(k.ramp_i[:, :], pattern=[[1, P]], base=0, channel_multiplier=0).then_inc(iotas, 1)
            pool.iota(k.idx[:, 0:NG], pattern=[[1, NG]], base=0, channel_multiplier=0).then_inc(iotas, 1)
            pool.iota(k.row_i[:, :], pattern=[[1, 1]], base=0, channel_multiplier=1).then_inc(iotas, 1)

        @block.vector
        def _(dve):
            half = P * T // 2 // P
            link(dve, dve.memset(pattern[:, 0:half * 6], 0.0))
            p4 = pattern[:, 0:half * 4].rearrange("p (r f) -> p r f", f=4)
            p2 = pattern[:, half * 4:half * 6].rearrange("p (r f) -> p r f", f=2)
            dve.memset(p4[:, :, 1:2], PAD).then_inc(filled, 1)
            dve.memset(p2[:, :, 1:2], PAD).then_inc(filled, 1)
            dve.memset(k.ones[:, :], 1.0)
            dve.wait_ge(iotas, 3)
            dve.tensor_copy(k.loc[:, 0:NG], k.idx[:, 0:NG])
            link(dve, dve.tensor_copy(k.ramp[:, :], k.ramp_i[:, :]))
            link(dve, dve.tensor_copy(k.row[:, :], k.row_i[:, :]))
            dve.tensor_scalar(k.ident[:, :], k.ramp[:, :], k.row[:, 0:1], None, ALU.is_equal)
            dve.tensor_scalar(k.below[:, :], k.ramp[:, :], k.row[:, 0:1], None, ALU.is_gt)
            dve.tensor_scalar(k.upto[:, :], k.ramp[:, :], k.row[:, 0:1], None, ALU.is_ge).then_inc(k.const, 1)


def fields_phase(nc, k):
    link = Link(k.sem("field_step"))
    with nc.Block() as block:
        @block.vector
        def _(dve):
            for raw, full, loc, hi in ((k.raw_s, k.src_f, k.sloc, k.shi), (k.raw_d, k.dst_f, k.dloc, k.dhi)):
                dve.tensor_copy(full, raw)
                link(dve, dve.tensor_scalar(k.shifted, raw, 7, None, ALU.arith_shift_right))
                link(dve, dve.tensor_copy(hi, k.shifted))
                link(dve, dve.tensor_scalar(k.shifted, raw, P - 1, None, ALU.bitwise_and))
                link(dve, dve.tensor_copy(loc, k.shifted))


class Rank:

    def __init__(self, k, key):
        self.k, self.key = k, key
        self.counted, self.summed, self.rounded, self.ended, self.compared, self.tabled, self.tabled_read, \
            self.picked, self.merged = (k.sem(f"{key}_{s}") for s in (
                "counted", "summed", "rounded", "ended", "compared", "tabled", "tabled_read", "picked", "merged"))
        self.link = Link(k.sem(key + "_step"))
        self.spans = [(lo, min(lo + 512, EC)) for lo in range(0, EC, 512)]
        self.cnt = k.tmp[:, 0:NB]
        self.col_i, self.col = k.st[0:NB, 0, 0:1].bitcast(I32), k.st[0:NB, 0, 1:2]
        self.group = k.loc[0:NB, 0:NG]
        self.past = k.cut[0:NB, 0:NG]

    def tensor(self, pe):
        k, ps, cnt = self.k, self.k.psum, self.cnt
        pe.wait_ge(self.counted, 1)
        pe.matmul(ps[0][:, 0:NB], k.ones[0:EP, :], cnt[0:EP, :], start=True, stop=True)
        pe.matmul(ps[1][0:EP, 0:NB], k.below[0:EP, 0:EP], cnt[0:EP, :], start=True, stop=True)
        pe.matmul(ps[2][0:NB, 0:1], cnt[0:EP, :], k.ones[0:EP, 0:1], start=True, stop=True)\
            .then_inc(self.summed, 1)
        pe.wait_ge(self.rounded, 1)
        pe.matmul(ps[3][0:NB, 0:1], k.upto[0:NB, 0:NB], self.col, start=True, stop=True).then_inc(self.ended, 1)
        pe.wait_ge(self.compared, 1)
        pe.matmul(ps[4][0:1, 0:512], k.ones[0:NB, 0:1], self.past[:, 0:512], start=True, stop=True)
        pe.matmul(ps[5][0:1, 0:NG - 512], k.ones[0:NB, 0:1], self.past[:, 512:NG], start=True, stop=True)\
            .then_inc(self.tabled, 1)
        pe.wait_ge(self.tabled_read, 1)

        def add(rows, start, stop):
            for m, (lo, up) in enumerate(self.spans):
                last = pe.matmul(ps[m][0:EP, 0:up - lo], k.ident[0:EP, 0:EP], rows[:, lo:up], start=start,
                                 stop=stop, skip_group_check=True)
            last.then_inc(self.merged, 1)
        add(k.zeros, True, False)
        with pe.Fori(0, NB) as b:
            pe.wait_ge(self.picked, b + 1)
            add(k.posf, False, False)
        add(k.zeros, False, True)

    def vector(self, dve):
        k, ps, link, cnt = self.k, self.k.psum, self.link, self.cnt
        hi = {"src": k.shi, "dst": k.dhi}[self.key]
        tot_i, tot = k.tmp[:, 64:64 + NB].bitcast(I32), k.tmp[:, 128:128 + NB]
        pre = k.tmp[:, 192:192 + NB]
        end = k.st[0:NB, 0, 2:3]
        link(dve, dve.memset(k.zeros, 0.0))
        with dve.Fori(0, NB) as b:
            link.loop(b, 1)
            link(dve, dve.tensor_scalar(k.mask, hi, k.ramp[0:EP, bass.ds(b, 1)], 0.0, ALU.is_equal,
                                        ALU.add, accum_out=cnt[0:EP, bass.ds(b, 1)]))
        link.end(NB)
        dve.sem_inc(self.counted, 1)
        dve.wait_ge(self.summed, 1)
        link(dve, dve.tensor_scalar(tot_i, ps[0][:, 0:NB], float(GE - 1), None, ALU.add))
        link(dve, dve.tensor_scalar(tot_i, tot_i, GSH, None, ALU.arith_shift_right))
        link(dve, dve.tensor_copy(tot, tot_i))
        link(dve, dve.tensor_tensor_scan(pre[0:EP, :], tot[0:EP, :], k.zeros[:, 0:NB], 0.0, ALU.add, ALU.add))
        link(dve, dve.tensor_tensor(pre[0:EP, :], pre[0:EP, :], tot[0:EP, :], ALU.subtract))
        link(dve, dve.scalar_tensor_tensor(k.offs[0:EP, :], pre[0:EP, :], float(GE), ps[1][0:EP, 0:NB],
                                           ALU.mult, ALU.add))
        link(dve, dve.tensor_scalar(self.col_i, ps[2][0:NB, 0:1], float(GE - 1), None, ALU.add))
        link(dve, dve.tensor_scalar(self.col_i, self.col_i, GSH, None, ALU.arith_shift_right))
        dve.tensor_copy(self.col, self.col_i).then_inc(self.rounded, 1)
        dve.wait_ge(self.ended, 1)
        link(dve, dve.tensor_copy(end, ps[3][0:NB, 0:1]))
        dve.tensor_scalar(self.past, self.group, end, None, ALU.is_ge).then_inc(self.compared, 1)
        dve.wait_ge(self.tabled, 1)
        table = k.block_of[self.key]
        dve.memset(table[0:1, NG:NG + 1], 0)
        dve.tensor_scalar(table[0:1, 0:512], ps[4][0:1, 0:512], float(NB - 1), None, ALU.min)
        dve.tensor_scalar(table[0:1, 512:NG], ps[5][0:1, 0:NG - 512], float(NB - 1), None, ALU.min)\
            .then_inc(self.tabled_read, 1)
        with dve.Fori(0, NB) as b:
            link.loop(b, 2)
            link(dve, dve.tensor_scalar(k.mask, hi, k.ramp[0:EP, bass.ds(b, 1)], None, ALU.is_equal))
            link(dve, dve.tensor_tensor_scan(k.scan, k.mask, k.zeros, k.offs[0:EP, bass.ds(b, 1)],
                                             ALU.add, ALU.add))
            dve.wait_ge(self.merged, b + 1)
            dve.tensor_tensor(k.posf, k.scan, k.mask, ALU.mult).then_inc(self.picked, 1)
            dve.wait_ge(self.picked, b + 1)
        link.end(NB)
        dve.wait_ge(self.merged, NB + 2)
        for m, (lo, up) in enumerate(self.spans):
            link(dve, dve.tensor_copy(k.posf[:, lo:up], ps[m][0:EP, 0:up - lo]))
        slot = k.pos[self.key]
        link(dve, dve.tensor_scalar(slot, k.posf, -1.0, None, ALU.add))
        link(dve, dve.tensor_scalar(k.shifted, slot, 7, None, ALU.arith_shift_right))
        link(dve, dve.tensor_copy(k.scan, k.shifted))
        link(dve, dve.tensor_scalar(k.shifted, slot, P - 1, None, ALU.bitwise_and))
        link(dve, dve.tensor_copy(k.posf, k.shifted))
        link(dve, dve.scalar_tensor_tensor(slot, k.posf, float(T), k.scan, ALU.mult, ALU.add))


class Scatter:

    def __init__(self, k, key):
        self.k = k
        self.staged, self.scattered = k.sem("staged"), [k.sem(f"scattered{h}") for h in range(2)]
        self.fields = {"src": (k.dst_f, k.sloc, k.w_f), "dst": (k.src_f, k.dloc)}[key]
        self.target = {"src": k.by_src_dram, "dst": k.by_dst_dram}[key]
        self.rec = k.gat[:, :, 0:len(self.fields) + len(self.fields) % 2]
        self.slots = k.pos[key]
        self.per = len(self.fields) + 1

    def clear(self, act):
        if len(self.fields) % 2:
            act.activation(self.rec[0:EP, :, len(self.fields)], self.fields[0][:, 0:BODY], ACT.Copy)

    def stage(self, act, i, h, first=False):
        if not first:
            act.wait_ge(self.scattered[h], i * (16 * HALF))
        at, to = bass.ds(i * BODY + h * HALF, HALF), slice(h * HALF, (h + 1) * HALF)
        act.activation(self.k.stage[0:EP, to], self.slots[:, at], ACT.Copy).then_inc(self.staged, 1)
        for m, field in enumerate(self.fields):
            act.activation(self.rec[0:EP, to, m], field[:, at], ACT.Copy).then_inc(self.staged, 1)

    def gpsimd(self, pool):
        k, turns = self.k, EC // BODY
        with pool.Fori(0, turns) as i:
            for h in range(2):
                pool.wait_ge(self.staged, i * (2 * self.per) + self.per * (h + 1))
                pool.sem_inc(k.passed, 1)
                for m in range(h * HALF, (h + 1) * HALF):
                    pool.indirect_dma_start(
                        self.target, bass.IndirectOffsetOnAxis(k.stage[0:EP, m:m + 1], axis=0),
                        self.rec[0:EP, m, :], None).then_inc(self.scattered[h], 16)
        for h in range(2):
            pool.wait_ge(self.scattered[h], turns * 16 * HALF)


class Degree:

    def __init__(self, k):
        self.k = k
        self.hot, self.taken, self.zeroed, self.summed = (k.sem("deg_" + n) for n in (
            "hot", "taken", "zeroed", "summed"))
        self.link = Link(k.sem("deg_step"))
        self.lo = k.wk[:, 0:G * C].bitcast(BF16).rearrange("p (r c) -> p r c", r=4)
        self.hi = k.wk[:, G * C:2 * G * C].bitcast(BF16).rearrange("p (r c) -> p r c", r=4)
        self.none = k.wk[:, 2 * G * C:3 * G * C].bitcast(BF16)[0:EP, 0:P]
        self.dest = k.psum[7][:, 0:NB]

    def vector(self, dve):
        k = self.k
        dve.memset(self.none, 0.0).then_inc(self.zeroed, 1)
        with dve.Fori(0, EC // 4) as i:
            for r in range(4):
                dve.wait_ge(self.taken, i * 4 + r + 1)
                dve.tensor_scalar(self.lo[0:EP, r, :], k.ramp[0:EP, :], k.dloc[:, bass.ds(i * 4 + r, 1)], None,
                                  ALU.is_equal).then_inc(self.hot, 1)
                dve.tensor_scalar(self.hi[0:EP, r, 0:NB], k.ramp[0:EP, 0:NB], k.dhi[:, bass.ds(i * 4 + r, 1)],
                                  None, ALU.is_equal).then_inc(self.hot, 1)
        dve.wait_ge(self.summed, 1)
        self.link(dve, dve.tensor_copy(k.deg[:, :], self.dest))

    def tensor(self, pe):
        pe.wait_ge(self.zeroed, 1)
        pe.matmul(self.dest, self.none, self.none[:, 0:NB], start=True, stop=False, skip_group_check=True)\
            .then_inc(self.taken, 4)
        with pe.Fori(0, EC // 4) as i:
            for r in range(4):
                pe.wait_ge(self.hot, i * 8 + 2 * (r + 1))
                pe.matmul(self.dest, self.lo[0:EP, r, :], self.hi[0:EP, r, 0:NB], start=False, stop=False,
                          skip_group_check=True).then_inc(self.taken, 1)
        pe.matmul(self.dest, self.none, self.none[:, 0:NB], start=False, stop=True, skip_group_check=True)\
            .then_inc(self.summed, 1)


def rank_phase(nc, k):
    rank = Rank(k, "src")
    turned = k.sem("we2_turned")
    with nc.Block() as block:
        @block.tensor
        def _(pe):
            pe.transpose(k.psum[7][:, 0:H2], k.we2[:, :], k.ident[0:H2, 0:H2]).then_inc(turned, 1)
            rank.tensor(pe)

        @block.vector
        def _(dve):
            dve.wait_ge(turned, 1)
            dve.tensor_copy(k.we2t[:, :], k.psum[7][:, 0:H2])
            rank.vector(dve)


def first_scatter_phase(nc, k):
    scatter, rank, degree = Scatter(k, "src"), Rank(k, "dst"), Degree(k)
    with nc.Block() as block:
        @block.gpsimd
        def _(pool):
            scatter.gpsimd(pool)

        @block.scalar
        def _(act):
            scatter.clear(act)
            for h in range(2):
                scatter.stage(act, 0, h, first=True)
            with act.Fori(1, EC // BODY) as i:
                for h in range(2):
                    scatter.stage(act, i, h)

        @block.tensor
        def _(pe):
            rank.tensor(pe)
            degree.tensor(pe)

        @block.vector
        def _(dve):
            rank.vector(dve)
            degree.vector(dve)


def second_scatter_phase(nc, k):
    scatter = Scatter(k, "dst")
    loaded, turned, copied, rowed, halved, sined = (k.sem("cut_" + s) for s in (
        "loaded", "turned", "copied", "rowed", "halved", "sined"))
    fetched = [k.sem("bias_fetched0"), k.sem("bias_fetched1")]
    outer, hidden, mixed, added = (k.sem("bias_" + n) for n in ("outer", "hidden", "mixed", "added"))
    link = Link(k.sem("cut_step"))
    rec = k.acc[:, 0:T * 4].rearrange("p (t f) -> p t f", f=4)
    w, hh = k.big[:, 0:T], k.big[:, T:2 * T]
    W = 4
    S = BODY // W
    wrow = k.acc[0:1, 0:2 * BODY * P].rearrange("o (r c) -> o r c", r=2)
    hid = k.acc[:, 2 * BODY * P:2 * BODY * P + 2 * W * P].rearrange("p (r c) -> p r c", r=2)
    bank, mix = (k.psum[2], k.psum[3]), (k.psum[4], k.psum[5])
    with nc.Block() as block:
        @block.gpsimd
        def _(pool):
            scatter.gpsimd(pool)

        @block.sync
        def _(sp):
            sp.dma_start(rec, k.by_src_dram.rearrange("(p t) f -> p t f", p=P)).then_inc(loaded, 16)
            for m in range(T // P):
                sp.wait_ge(copied, m + 1)
                sp.dma_start(k.w_rows_dram[m * P:(m + 1) * P, :], k.wk[:, m % 4 * P:(m % 4 + 1) * P])\
                    .then_inc(rowed, 16)
                sp.wait_ge(rowed, 16 * (m + 1))
            link_done = 10
            sp.wait_ge(link.sem, link_done)

            def fetch(i, r):
                sp.dma_start(wrow[:, r, :], k.w_rows_dram[bass.ds(i * BODY, BODY), :]
                             .rearrange("(o t) q -> o (t q)", o=1)).then_inc(fetched[r], 16)
            fetch(0, 0)
            fetch(1, 1)
            with sp.Fori(1, IT // 2) as i:
                for r in range(2):
                    sp.wait_ge(outer, i * (2 * S) + (r - 1) * S)
                    fetch(i * 2 + r, r)

        @block.tensor
        def _(pe):
            pe.wait_ge(loaded, 16)
            for m in range(T // P):
                if m >= 2:
                    pe.wait_ge(copied, m - 1)
                pe.transpose(k.psum[m % 2][:, 0:P], rec[:, m * P:(m + 1) * P, 2], k.ident[:, :])\
                    .then_inc(turned, 1)

            def body(i, first):
                for n in range(2 * S):
                    r, q = n // S, n % 2
                    if n % S == 0:
                        pe.wait_ge(fetched[r], i * 16 + 16)
                    if not first or n >= 2:
                        pe.wait_ge(hidden, i * (2 * S) + n - 1)
                    pe.matmul(bank[q][:, :], k.we1[:, :], wrow[:, r, n % S * W * P:(n % S + 1) * W * P],
                              start=True, stop=True).then_inc(outer, 1)
                    if not first or n >= 1:
                        mix_step(i, n - 1, first)

            def mix_step(i, n, first):
                pe.wait_ge(hidden, i * (2 * S) + n + 1)
                if not first or n >= 2:
                    pe.wait_ge(added, i * (2 * S) + n - 1)
                for t in range(W):
                    last = pe.matmul(mix[n % 2][:, t * H2:(t + 1) * H2], hid[:, n % 2, t * P:(t + 1) * P],
                                     k.we2t[:, :], start=True, stop=True)
                last.then_inc(mixed, 1)
            body(0, True)
            with pe.Fori(1, IT // 2) as i:
                body(i, False)
            mix_step(IT // 2 - 1, 2 * S - 1, False)

        @block.scalar
        def _(act):
            for h in range(2):
                scatter.stage(act, 0, h, first=True)
            act.wait_ge(halved, 1)
            act.activation(w, w, ACT.Sin).then_inc(sined, 1)

            def silu(i, n, first):
                act.wait_ge(outer, i * (2 * S) + n + 1)
                if not first or n >= 2:
                    act.wait_ge(mixed, i * (2 * S) + n - 1)
                act.activation(hid[:, n % 2, :], bank[n % 2][:, :], ACT.Silu, bias=k.be1[:, 0:1])\
                    .then_inc(hidden, 1)

            def body(i, first, stage=True):
                for n in range(2 * S):
                    silu(i, n, first)
                    if n % 2 and stage and not (first and n < 4):
                        scatter.stage(act, i * 2 + n // 4, n // 2 % 2)
            body(0, True)
            turns = EC // BODY // 2
            with act.Fori(1, turns) as i:
                body(i, False)
            with act.Fori(turns, IT // 2) as i:
                body(i, False, stage=False)

        @block.vector
        def _(dve):
            dve.wait_ge(loaded, 16)
            link(dve, dve.tensor_scalar(w, rec[:, :, 2], 0.5 / CUTOFF, None, ALU.mult))
            link(dve, dve.tensor_scalar(hh, w, ROUND, -ROUND, ALU.add, ALU.add))
            link(dve, dve.tensor_tensor(w, w, hh, ALU.subtract))
            link(dve, dve.tensor_scalar(hh, w, -1.0, None, ALU.mult))
            link(dve, dve.tensor_tensor(w, w, hh, ALU.max))
            link(dve, dve.tensor_scalar(w, w, -2.0 * math.pi, 0.5 * math.pi, ALU.mult, ALU.add))
            dve.tensor_scalar(w, w, 1.5707963, -1.5707963, ALU.min, ALU.max).then_inc(halved, 1)
            neg = k.loc[:, 0:T]
            link(dve, dve.tensor_scalar(neg, rec[:, :, 1], float(P), NEG, ALU.is_ge, ALU.mult))
            dve.wait_ge(sined, 1)
            link(dve, dve.tensor_scalar(w, w, 0.5, 0.5, ALU.mult, ALU.add))
            link(dve, dve.scalar_tensor_tensor(k.cut[:, :], rec[:, :, 2], CUTOFF, w, ALU.is_lt, ALU.mult))
            for m in range(T // P):
                dve.wait_ge(turned, m + 1)
                if m >= 4:
                    dve.wait_ge(rowed, 16 * (m - 3))
                dve.tensor_copy(k.wk[:, m % 4 * P:(m % 4 + 1) * P], k.psum[m % 2][:, 0:P])\
                    .then_inc(copied, 1)
            dve.wait_ge(copied, T // P)
            dve.sem_inc(link.sem, 1)
            b2 = k.be2[:, :].unsqueeze(1).to_broadcast([P, W, H2])
            with dve.Fori(0, IT // 2) as i:
                for n in range(2 * S):
                    dve.wait_ge(mixed, i * (2 * S) + n + 1)
                    dve.tensor_tensor(
                        k.big[:, bass.ds((i * (2 * S) + n) * (W * H2), W * H2)]
                        .rearrange("p (t h) -> p t h", h=H2),
                        mix[n % 2][:, 0:W * H2].rearrange("p (t h) -> p t h", h=H2), b2, ALU.add)\
                        .then_inc(added, 1)
            dve.wait_ge(added, T // W)
            lg = k.big[:, :].rearrange("p (t h) -> p t h", h=H2)
            dve.tensor_tensor(lg, lg, neg.unsqueeze(2).to_broadcast([P, T, H2]), ALU.add)


def prepare_phase(nc, k):
    turned, copied, summed, spread, plus_one, rooted = (k.sem("prep_" + n) for n in (
        "turned", "copied", "summed", "spread", "plus_one", "rooted"))
    link = Link(k.sem("prep_step"))
    turn = ("L2_gnn_Wq", "L2_gnn_Wk", "L2_gnn_Wv", "L2_gnn_Wo")
    temb_rep = k.wk[:, 0:C]
    x_clear, x_loaded = k.sem("x_clear"), k.sem("x_loaded")
    with nc.Block() as block:
        @block.sync
        def _(sp):
            sp.dma_start(k.x[:, 0:NB - 1, :], k.a["x"][0:(NB - 1) * P, :].rearrange("(b p) c -> p b c", p=P))\
                .then_inc(x_loaded, 16)
            sp.wait_ge(x_clear, 1)
            sp.dma_start(k.x[0:REM, NB - 1, :], k.a["x"][(NB - 1) * P:N, :]).then_inc(x_loaded, 16)
            sp.wait_ge(x_loaded, 32)

        @block.tensor
        def _(pe):
            for m, n in enumerate(turn):
                last = pe.transpose(k.psum[0][:, m * C:(m + 1) * C], k.w[n][:, :], k.ident[:, :])
            last.then_inc(turned, 1)
            pe.wait_ge(spread, 1)
            pe.matmul(k.psum[2][:, 0:C], temb_rep, k.w["L0_gnn_Wt1"][:, :], start=True, stop=True)
            pe.matmul(k.psum[2][:, C:2 * C], temb_rep, k.w["L0_gnn_Wt2"][:, :], start=True, stop=True)\
                .then_inc(summed, 1)

        @block.scalar
        def _(act):
            act.wait_ge(plus_one, 1)
            act.activation(k.dinv[:, :], k.dinv[:, :], ACT.Sqrt).then_inc(rooted, 1)

        @block.vector
        def _(dve):
            dve.memset(k.x[:, NB - 1, :], 0.0).then_inc(x_clear, 1)
            dve.tensor_scalar(k.dinv[:, :], k.deg[:, :], 1.0, None, ALU.add).then_inc(plus_one, 1)
            dve.tensor_scalar(temb_rep, k.ones[:, :], k.temb[:, 0:1], None, ALU.mult).then_inc(spread, 1)
            dve.wait_ge(turned, 1)
            for m, n in enumerate(turn):
                dve.tensor_copy(k.w[n][:, :], k.psum[0][:, m * C:(m + 1) * C])
            dve.wait_ge(rooted, 1)
            link(dve, dve.reciprocal(k.dinv[:, :], k.dinv[:, :]))
            dve.wait_ge(summed, 1)
            for m, (b, bt) in enumerate((("L0_gnn_b1", "L0_gnn_bt1"), ("L0_gnn_b2", "L0_gnn_bt2"))):
                link(dve, dve.tensor_tensor(k.v[b][:, :], k.v[b][:, :], k.v[bt][:, :], ALU.add))
                link(dve, dve.tensor_tensor(k.v[b][:, :], k.v[b][:, :], k.psum[2][:, m * C:(m + 1) * C],
                                            ALU.add))


def lists_phase(nc, k, which):
    loaded = k.sem("lists_loaded")
    full = {"dst": 2, "src": 4}[which]
    source = {"dst": k.by_dst_dram, "src": k.by_src_dram}[which]
    rec = k.acc[:, 0:T * full].rearrange("p (t f) -> p t f", f=full)
    with nc.Block() as block:
        @block.sync
        def _(sp):
            sp.dma_start(rec, source.rearrange("(p t) f -> p t f", p=P)).then_inc(loaded, 16)

        @block.vector
        def _(dve):
            dve.wait_ge(loaded, 16)
            dve.tensor_copy(k.idx[:, 0:T], rec[:, :, 0])
            dve.memset(k.idx[:, T:T + HALF], 0)
            dve.tensor_copy(k.loc[:, 0:T], rec[:, :, 1])
            dve.memset(k.loc[:, T:T + G], PAD)


def pass_phase(nc, k, name, which, table, row, kind):
    n = name + "_"
    staged, hot, turned, copied, looked, scored, weighed, ready, matched, added = (k.sem(n + s) for s in (
        "staged", "hot", "turned", "copied", "looked", "scored", "weighed", "ready", "matched", "added"))
    link, plink = Link(k.sem(n + "step")), None
    base = k.gathered_base
    k.gathered_base += 16 * IT
    width = {"sum": C, "gat": A1, "value": A2, "max": 0, "logit": 0}[kind]
    looks = {"gat": 2 * H1, "logit": C}.get(kind, 0)
    near = {"gat": k.nodev[:, :, :].rearrange("p b c -> p (b c)"),
            "logit": k.h[:, :, :].rearrange("p b c -> p (b c)")}.get(kind)
    blocks = k.block_of[which]
    agg, tb, vb = k.psum[0:2], k.psum[2:4], k.psum[4:6]
    diag = k.acc[:, 0:4 * H1 * P].rearrange("p (s h c) -> p s h c", s=4, h=H1)
    peaks = k.wk[:, 0:H1]
    z = k.wk[:, 0:2 * G * H1].rearrange("p (s t h) -> p s t h", s=2, h=H1)
    prod = k.wk[:, G * C:2 * G * C].rearrange("p (t c) -> p t c", t=G)
    qk = k.wk[:, 0:G * H2]

    def turns(eng, body):
        body(0, True)
        with eng.Fori(1, IT) as i:
            body(i, False)

    def arrived(eng, i, j):
        for t in range(G):
            eng.wait_ge(k.gathered[G * j + t], i * 16 + base + 16)

    used = {"logit": scored}.get(kind, matched)

    with nc.Block() as block:
        @block.gpsimd
        def _(pool):
            with pool.Fori(0, IT) as i:
                for h in range(2):
                    pool.wait_ge(staged, i * 2 + h + 1)
                    pool.sem_inc(k.passed, 1)
                    for m in range(h * HALF, (h + 1) * HALF):
                        pool.indirect_dma_start(
                            k.gat[:, m, 0:row], None, table,
                            bass.IndirectOffsetOnAxis(k.stage[:, m:m + 1], axis=0)).then_inc(k.gathered[m], 16)

        @block.scalar
        def _(act):
            def stage_half(i, h, first):
                if not first:
                    act.wait_ge(used, i * GB + (h - 1) * (GB // 2))
                act.activation(k.stage[:, h * HALF:(h + 1) * HALF], k.idx[:, bass.ds(i * BODY + h * HALF, HALF)],
                               ACT.Copy).then_inc(staged, 1)

            def turn_hot(g, j):
                act.wait_ge(turned, g + 1)
                act.activation(k.hot_t[:, j % 2, :], tb[j % 2][:, 0:G * P], ACT.Copy).then_inc(copied, 1)

            def body(i, first):
                if first:
                    stage_half(0, 0, True)
                    stage_half(0, 1, True)
                    if looks:
                        turn_hot(0, 0)
                for j in range(GB):
                    g = i * GB + j
                    if not first and j == 1:
                        stage_half(i, 1, False)
                    if j == GB // 2 + 1:
                        stage_half(i + 1, 0, False)
                    if kind == "max":
                        arrived(act, i, j)
                        if not first or j >= 2:
                            act.wait_ge(matched, g - 1)
                        for t in range(G):
                            for hd in range(H1):
                                last = act.activation(diag[:, G * (j % 2) + t, hd, :], k.ident[:, :], ACT.Copy,
                                                      scale=k.gat[:, G * j + t, hd:hd + 1])
                        last.then_inc(ready, 1)
                    if looks:
                        turn_hot(g + 1, j + 1)
                    if kind == "gat":
                        act.wait_ge(scored, g + 1)
                        act.activation(k.gat[:, G * j:G * j + G, C:A1], z[:, 0, :, :], ACT.Exp)\
                            .then_inc(weighed, 1)
            turns(act, body)

        @block.tensor
        def _(pe):
            def look(g, j):
                b = pe.value_load(blocks[0:1, bass.ds(g, 1)], min_val=0, max_val=NB - 1)
                pe.wait_ge(hot, g + 1)
                for t in range(G):
                    last = pe.transpose(tb[j % 2][:, t * P:(t + 1) * P], k.oneh[:, (G * j + t) % HALF, :],
                                        k.ident[:, :])
                last.then_inc(turned, 1)
                pe.wait_ge(copied, g + 1)
                for t in range(G):
                    last = pe.matmul(vb[j % 2][:, t * looks:(t + 1) * looks],
                                     k.hot_t[:, j % 2, t * P:(t + 1) * P], near[:, bass.ds(b * looks, looks)],
                                     start=True, stop=True)
                last.then_inc(looked, 1)

            def body(i, first):
                if looks and first:
                    look(0, 0)
                for j in range(GB):
                    g = i * GB + j
                    if looks:
                        if kind == "logit" and (not first or j >= 1):
                            pe.wait_ge(scored, g)
                        look(g + 1, j + 1)
                    if kind == "logit":
                        continue
                    pe.wait_ge(hot, g + 1)
                    if not first or j >= 2:
                        pe.wait_ge(added, g - 1)
                    if kind == "sum":
                        arrived(pe, i, j)
                    else:
                        pe.wait_ge(ready, g + 1)
                    for t in range(G):
                        oh = k.oneh[:, (G * j + t) % HALF, :]
                        if kind == "max":
                            rhs = diag[:, G * (j % 2) + t, :, :].rearrange("p h c -> p (h c)")
                            last = pe.matmul(k.psum[G * (j % 2) + t][:, :], oh, rhs, start=True, stop=True)
                        else:
                            last = pe.matmul(agg[j % 2][:, 0:width], oh, k.gat[:, G * j + t, 0:width],
                                             start=(t == 0), stop=(t == G - 1))
                    last.then_inc(matched, 1)
            turns(pe, body)

        @block.vector
        def _(dve):
            def make_hot(g, i, j):
                for t in range(G):
                    last = dve.tensor_scalar(k.oneh[:, (G * j + t) % HALF, :], k.ramp[:, :],
                                             k.loc[:, bass.ds(i * BODY + G * j + t, 1)], None, ALU.is_equal)
                last.then_inc(hot, 1)

            def add(g, j):
                b = dve.value_load(blocks[0:1, bass.ds(g, 1)], min_val=0, max_val=NB - 1)
                dve.wait_ge(matched, g + 1)
                if kind == "max":
                    view = k.psum_pair[j % 2].rearrange("p (t h c) -> p h t c", t=G, h=H1)
                    link(dve, dve.tensor_reduce(peaks, view, AX.XY, ALU.max))
                    mine = k.maxa[:, bass.ds(b * H1, H1)]
                    dve.tensor_tensor(mine, mine, peaks, ALU.max).then_inc(added, 1)
                else:
                    mine = k.acc[:, bass.ds(b * width, width)]
                    dve.tensor_tensor(mine, mine, agg[j % 2][:, 0:width], ALU.add).then_inc(added, 1)
                dve.wait_ge(added, g + 1)

            def score_gat(i, g, j):
                v = vb[j % 2][:, 0:G * looks].rearrange("p (t c) -> p t c", t=G)
                arrived(dve, i, j)
                dve.wait_ge(looked, g + 1)
                link(dve, dve.tensor_tensor(z[:, 0, :, :], k.gat[:, G * j:G * j + G, C:A1], v[:, :, 0:H1], ALU.add))
                link(dve, dve.scalar_tensor_tensor(z[:, 1, :, :], z[:, 0, :, :], 0.2, z[:, 0, :, :], ALU.mult,
                                                   ALU.max))
                link(dve, dve.tensor_tensor(z[:, 1, :, :], z[:, 1, :, :], v[:, :, H1:2 * H1], ALU.subtract))
                dve.tensor_scalar(z[:, 0, :, :], z[:, 1, :, :], 0.0, None, ALU.min).then_inc(scored, 1)

            def message(i, g, j, heads, dim):
                rows = k.gat[:, G * j:G * j + G, 0:C].rearrange("p t (h c) -> p t h c", h=heads)
                wts = k.gat[:, G * j:G * j + G, C:C + heads].unsqueeze(3).to_broadcast([P, G, heads, dim])
                dve.tensor_tensor(rows, rows, wts, ALU.mult).then_inc(ready, 1)

            def logit(i, g, j):
                v = vb[j % 2][:, 0:G * looks].rearrange("p (t c) -> p t c", t=G)
                arrived(dve, i, j)
                dve.wait_ge(looked, g + 1)
                link(dve, dve.tensor_tensor(prod, k.gat[:, G * j:G * j + G, 0:C], v, ALU.mult))
                dve.tensor_reduce(qk, prod.rearrange("p t (h d) -> p (t h) d", d=D2), AX.X, ALU.add)\
                    .then_inc(scored, 1)
                dve.wait_ge(scored, g + 1)
                at = (i * BODY + G * j) * H2
                link(dve, dve.scalar_tensor_tensor(qk, qk, 1.0 / math.sqrt(D2), k.big[:, bass.ds(at, G * H2)],
                                                   ALU.mult, ALU.add))
                for t in range(G):
                    last = dve.tensor_scalar(k.big[:, bass.ds(at + t * H2, H2)], qk[:, t * H2:(t + 1) * H2],
                                             k.cut[:, bass.ds(i * BODY + G * j + t, 1)], None, ALU.mult)
                link(dve, last)

            per = {"sum": 0, "max": 1, "gat": 3, "logit": 3, "value": 1}[kind]

            def body(i, first):
                if first:
                    if kind == "max":
                        link(dve, dve.tensor_copy(k.maxa[:, :], k.asrc[:, :, :].rearrange("p b h -> p (b h)")))
                    elif width:
                        link(dve, dve.memset(k.acc[:, 0:NB * width], 0.0))
                    make_hot(0, 0, 0)
                else:
                    link.loop(i - 1, per * GB)
                for j in range(GB):
                    g = i * GB + j
                    if kind == "gat":
                        score_gat(i, g, j)
                    make_hot(g + 1, i, j + 1)
                    if kind in ("sum", "max", "gat", "value") and not (first and j == 0):
                        add(g - 1, j - 1)
                    if kind == "gat":
                        dve.wait_ge(weighed, g + 1)
                        message(i, g, j, H1, D1)
                    if kind == "value":
                        arrived(dve, i, j)
                        at = (i * BODY + G * j) * H2
                        link(dve, copy(
                            dve, k.gat[:, G * j:G * j + G, C:A2],
                            k.big[:, bass.ds(at, G * H2)].rearrange("p (t h) -> p t h", h=H2)))
                        message(i, g, j, H2, D2)
                    if kind == "logit":
                        logit(i, g, j)
            turns(dve, body)
            link.end(IT - 1)
            if kind != "logit":
                add(NG - 1, GB - 1)


class Chunk:

    def __init__(self, nc, k, name):
        self.nc, self.k, self.name = nc, k, name
        self.link = Link(k.sem(name + "_step"))
        self.rows_ready, self.turned, self.copied, self.product, self.asked, self.given, self.to_store, \
            self.stored = (k.sem(f"{name}_{s}") for s in (
                "rows_ready", "turned", "copied", "product", "asked", "given", "to_store", "stored"))
        self.room = k.sem(name + "_room")
        f = k.chunk_room
        w = BC * C
        self.y, self.yt, self.s, self.o = (f[:, m * w:(m + 1) * w].rearrange("p (b c) -> p b c", c=C)
                                           for m in range(4))

    def ask(self, dve, i, n, per):
        dve.wait_ge(self.given, i * per + n)

    def norm(self, dve, i, n, per, src, dst):
        k, link, st = self.k, self.link, self.k.st
        for b in range(BC):
            last = dve.bn_stats(st[:, b, 0:6], src[:, b, :])
        link(dve, last)
        dve.sem_inc(k.passed, 1)
        for b in range(BC):
            last = dve.bn_aggr(st[:, b, 6:8], st[:, b, 0:6])
        link(dve, last)
        dve.tensor_scalar(st[:, :, 8], st[:, :, 7], EPS, None, ALU.add).then_inc(self.asked, 1)
        self.ask(dve, i, n, per)
        link(dve, dve.reciprocal(st[:, :, 10], st[:, :, 9]))
        for b in range(BC):
            last = dve.tensor_scalar(dst[:, b, :], src[:, b, :], st[:, b, 6:7], st[:, b, 10:11],
                                     ALU.subtract, ALU.mult)
        link(dve, last)

    def bc(self, vector):
        return vector.unsqueeze(1).to_broadcast([P, BC, C])


def by_blocks(tensor, i):
    return tensor[:, bass.ds(i * BC, BC), :]


def by_heads(rows, heads):
    return rows.rearrange("p b (h d) -> p b h d", h=heads)


def halves():
    return ((0, 0, 4), (1, 4, BC))


def dense_phase(nc, k, name, before, after, mats, jobs, stores=(), turn=1, second=None):
    c = Chunk(nc, k, name)
    link = c.link
    with nc.Block() as block:
        @block.vector
        def _(dve):
            with dve.Fori(0, NCH) as i:
                link.loop(i, before.links + after.links)
                before(c, dve, i)
                if mats:
                    dve.wait_ge(c.product, i + 1)
                after(c, dve, i)
            link.end(NCH)

        @block.scalar
        def _(act):
            with act.Fori(0, NCH) as i:
                for n, job in enumerate(jobs):
                    if job == "turn":
                        act.wait_ge(c.turned, i + 1)
                        for bank, lo, up in halves():
                            last = act.activation(c.yt[:, lo:up, :], k.psum[bank][:, 0:(up - lo) * C]
                                                  .rearrange("p (b c) -> p b c", c=C), ACT.Copy)
                        last.then_inc(c.copied, 1)
                    else:
                        m = len([q for q in jobs[:n + 1] if q != "turn"])
                        act.wait_ge(c.asked, i * len([q for q in jobs if q != "turn"]) + m)
                        job(c, act).then_inc(c.given, 1)

        if mats:
            @block.tensor
            def _(pe):
                with pe.Fori(0, NCH) as i:
                    pe.wait_ge(c.rows_ready, i + 1)
                    for bank, lo, up in halves():
                        for b in range(lo, up):
                            last = pe.transpose(k.psum[bank][:, (b - lo) * C:(b - lo + 1) * C], c.y[:, b, :],
                                                k.ident[:, :])
                    last.then_inc(c.turned, 1)
                    pe.wait_ge(c.copied, i + 1)
                    for m, mat in enumerate(mats):
                        for bank, lo, up in halves():
                            for b in range(lo, up):
                                last = pe.matmul(k.psum[2 + 2 * m + bank][:, (b - lo) * C:(b - lo + 1) * C],
                                                 c.yt[:, b, :], mat[:, :], start=True, stop=True)
                    last.then_inc(c.product, 1)

        if stores:
            @block.sync
            def _(sp):
                sp.sem_inc(c.room, 1)
                with sp.Fori(0, NCH) as i:
                    sp.wait_ge(c.to_store, i + 1)
                    for table, rows in stores:
                        sp.dma_start(table.rearrange("(b p) c -> p b c", p=P)[:, bass.ds(i * BC, BC), :], rows(c))\
                            .then_inc(c.stored, 16)
                    sp.wait_ge(c.stored, i * (16 * len(stores)) + 16 * len(stores))
                    sp.sem_inc(c.room, 1)


def product(k, m):
    return k.psum_pair[1 + m][:, 0:BC * C].rearrange("p (b c) -> p b c", c=C)


def sqrt_job(c, act):
    return act.activation(c.k.st[:, :, 9], c.k.st[:, :, 8], ACT.Sqrt)


def silu_job(c, act):
    return act.activation(c.s, c.s, ACT.Silu)


def stage_gcn_in(k):
    def before(c, dve, i):
        link = c.link
        c.norm(dve, i, 1, 1, by_blocks(k.x, i), c.y)
        link(dve, dve.tensor_tensor(c.y, c.y, c.bc(k.v["L0_gnn_g1"][:, :]), ALU.mult))
        dve.tensor_tensor(c.y, c.y, c.bc(k.v["L0_gnn_bn1"][:, :]), ALU.add).then_inc(c.rows_ready, 1)
    before.links = 5
    return before, gcn_out(k)


def gcn_out(k):
    def after(c, dve, i):
        link = c.link
        h = by_blocks(k.h, i)
        link(dve, copy(dve, h, product(k, 0)))
        dve.wait_ge(c.room, i + 1)
        inv = k.dinv[:, bass.ds(i * BC, BC)].unsqueeze(2).to_broadcast([P, BC, C])
        dve.tensor_tensor(c.o, h, inv, ALU.mult).then_inc(c.to_store, 1)
    after.links = 1
    return after


def gcn_sum(k, c, dve, i, bias):
    link = c.link
    inv = k.dinv[:, bass.ds(i * BC, BC)].unsqueeze(2).to_broadcast([P, BC, C])
    link(dve, dve.tensor_tensor(c.s, by_blocks(k.h, i), inv, ALU.mult))
    acc = k.acc[:, bass.ds(i * (BC * C), BC * C)].rearrange("p (b c) -> p b c", c=C)
    link(dve, dve.tensor_tensor(c.s, c.s, acc, ALU.add))
    link(dve, dve.tensor_tensor(c.s, c.s, inv, ALU.mult))
    dve.tensor_tensor(c.s, c.s, c.bc(bias[:, :]), ALU.add).then_inc(c.asked, 1)
    c.ask(dve, i, 1, 2)


def stage_gcn_mid(k):
    def before(c, dve, i):
        link = c.link
        gcn_sum(k, c, dve, i, k.v["L0_gnn_b1"])
        c.norm(dve, i, 2, 2, c.s, c.y)
        link(dve, dve.tensor_tensor(c.y, c.y, c.bc(k.v["L0_gnn_g2"][:, :]), ALU.mult))
        dve.tensor_tensor(c.y, c.y, c.bc(k.v["L0_gnn_bn2"][:, :]), ALU.add).then_inc(c.rows_ready, 1)
    before.links = 8
    return before, gcn_out(k)


def stage_gcn_out(k):
    def before(c, dve, i):
        link = c.link
        gcn_sum(k, c, dve, i, k.v["L0_gnn_b2"])
        x = by_blocks(k.x, i)
        link(dve, dve.tensor_tensor(c.s, c.s, x, ALU.add))
        link(dve, dve.tensor_tensor(c.s, c.s, x, ALU.add))
        c.norm(dve, i, 2, 2, c.s, x)
        copy(dve, c.y, x).then_inc(c.rows_ready, 1)
    before.links = 9

    def after(c, dve, i):
        link = c.link
        h = by_blocks(k.h, i)
        link(dve, copy(dve, h, product(k, 0)))
        link(dve, dve.tensor_tensor(c.s, h, c.bc(k.v["L1_gnn_att_src"][:, :]), ALU.mult))
        link(dve, dve.tensor_reduce(by_blocks(k.asrc, i), by_heads(c.s, H1), AX.X, ALU.add))
        link(dve, dve.tensor_tensor(c.s, h, c.bc(k.v["L1_gnn_att_dst"][:, :]), ALU.mult))
        link(dve, dve.tensor_reduce(by_blocks(k.nodev, i)[:, :, 0:H1], by_heads(c.s, H1), AX.X, ALU.add))
    after.links = 5
    return before, after


def extreme_phase(nc, k, name, src, width, use):
    turned, diagonal, spread, ready = (k.sem(f"{name}_{s}") for s in ("turned", "diagonal", "spread", "ready"))
    link = Link(k.sem(name + "_step"))
    part = k.tmp[:, 32:32 + width]
    top = k.tmp[0:width, 64:65]
    diag = k.tmp[0:width, 96:96 + width]
    with nc.Block() as block:
        @block.vector
        def _(dve):
            src(dve, link, part)
            dve.sem_inc(ready, 1)
            dve.wait_ge(turned, 1)
            link(dve, dve.tensor_reduce(top, k.psum[0][0:width, 0:P], AX.X, ALU.max))
            dve.tensor_scalar(diag, k.ident[0:width, 0:width], top, None, ALU.mult).then_inc(diagonal, 1)
            dve.wait_ge(spread, 1)
            link(dve, dve.tensor_copy(k.tmp[:, 0:width], k.psum[1][:, 0:width]))
            use(dve, link)

        @block.tensor
        def _(pe):
            pe.wait_ge(ready, 1)
            pe.transpose(k.psum[0][0:width, 0:P], part, k.ident[:, :]).then_inc(turned, 1)
            pe.wait_ge(diagonal, 1)
            pe.matmul(k.psum[1][:, 0:width], k.ones[0:width, :], diag, start=True, stop=True)\
                .then_inc(spread, 1)


def shift_phase(nc, k):
    stored, to_store, room = k.sem("shift_stored"), k.sem("shift_to_store"), k.sem("shift_room")

    def src(dve, link, part):
        link(dve, dve.tensor_reduce(part, k.asrc[:, :, :].rearrange("p b h -> p h b"), AX.X, ALU.min))
        link(dve, dve.tensor_scalar(part, part, -1.0, None, ALU.mult))

    def use(dve, link):
        low = k.tmp[:, 0:H1].unsqueeze(1).to_broadcast([P, NB, H1])
        link(dve, dve.tensor_tensor(k.asrc[:, :, :], k.asrc[:, :, :], low, ALU.add))
        link(dve, dve.tensor_tensor(k.nodev[:, :, 0:H1], k.nodev[:, :, 0:H1], low, ALU.subtract))
        link(dve, dve.tensor_scalar(k.asrc[:, :, :], k.asrc[:, :, :], 0.0, None, ALU.max))
    extreme_phase(nc, k, "low", src, H1, use)
    with nc.Block() as block:
        @block.sync
        def _(sp):
            rows = k.tab_h_dram.rearrange("(b p) c -> p b c", p=P)
            with nc.allow_non_contiguous_dma(reason="four floats beside each row"):
                sp.dma_start(k.tab_a_dram.rearrange("(b p) c -> p b c", p=P), k.asrc[:, :, :])\
                    .then_inc(stored, 16)
                sp.dma_start(rows[:, :, 0:C], k.h[:, :, :]).then_inc(stored, 16)
                sp.dma_start(rows[:, :, C:A1], k.asrc[:, :, :]).then_inc(stored, 16)
            sp.wait_ge(stored, 48)


def leaky(dve, link, out, rows, tmp):
    link(dve, dve.tensor_scalar(tmp, rows, 0.2, None, ALU.mult))
    link(dve, dve.tensor_tensor(out, rows, tmp, ALU.max))


def gat_maximum_phase(nc, k):
    asked, given = k.sem("self_asked"), k.sem("self_given")
    link = Link(k.sem("self_step"))
    with nc.Block() as block:
        d = k.nodev[:, :, 0:H1]
        m = k.nodev[:, :, H1:2 * H1]
        maxa = k.maxa[:, :].rearrange("p (b h) -> p b h", h=H1)
        tmp = k.wk[:, 0:NB * H1].rearrange("p (b h) -> p b h", h=H1)
        tmp2 = k.wk[:, NB * H1:2 * NB * H1].rearrange("p (b h) -> p b h", h=H1)

        @block.vector
        def _(dve):
            link(dve, dve.tensor_tensor(maxa, maxa, d, ALU.add))
            leaky(dve, link, m, maxa, tmp)
            link(dve, dve.tensor_tensor(tmp2, k.asrc[:, :, :], d, ALU.add))
            leaky(dve, link, maxa, tmp2, tmp)
            dve.tensor_tensor(maxa, maxa, m, ALU.subtract).then_inc(asked, 1)

        @block.scalar
        def _(act):
            act.wait_ge(asked, 1)
            act.activation(maxa, maxa, ACT.Exp).then_inc(given, 1)
            act.wait_ge(given, 1)


def stage_gat_out(k):
    def tanh_job(c, act):
        return act.activation(c.s, c.s, ACT.Tanh)

    def before(c, dve, i):
        link = c.link
        acc = k.acc[:, bass.ds(i * (BC * A1), BC * A1)].rearrange("p (b c) -> p b c", c=A1)
        own = k.maxa[:, bass.ds(i * (BC * H1), BC * H1)].rearrange("p (b h) -> p b h", h=H1)
        rep = own.unsqueeze(3).to_broadcast([P, BC, H1, D1])
        link(dve, dve.tensor_tensor(by_heads(c.s, H1), by_heads(by_blocks(k.h, i), H1), rep, ALU.mult))
        link(dve, dve.tensor_tensor(c.s, c.s, acc[:, :, 0:C], ALU.add))
        den = c.o[:, 0, 0:BC * H1].rearrange("p (b h) -> p b h", h=H1)
        link(dve, dve.tensor_tensor(den, own, acc[:, :, C:A1], ALU.add))
        link(dve, dve.tensor_scalar(den, den, 1e-16, None, ALU.add))
        link(dve, dve.reciprocal(den, den))
        link(dve, dve.tensor_tensor(by_heads(c.s, H1), by_heads(c.s, H1),
                                    den.unsqueeze(3).to_broadcast([P, BC, H1, D1]), ALU.mult))
        dve.tensor_tensor(c.s, c.s, c.bc(k.v["L1_gnn_bias"][:, :]), ALU.add).then_inc(c.asked, 1)
        c.ask(dve, i, 1, 2)
        x = by_blocks(k.x, i)
        link(dve, dve.tensor_tensor(c.s, c.s, x, ALU.add))
        c.norm(dve, i, 2, 2, c.s, x)
        copy(dve, c.y, x).then_inc(c.rows_ready, 1)
    before.links = 11

    def after(c, dve, i):
        link = c.link
        link(dve, dve.tensor_tensor(by_blocks(k.h, i), product(k, 0), c.bc(k.v["L2_gnn_bq"][:, :]), ALU.add))
        dve.wait_ge(c.room, i + 1)
        link(dve, dve.tensor_tensor(c.o, product(k, 1), c.bc(k.v["L2_gnn_bk"][:, :]), ALU.add))
        dve.tensor_tensor(c.s, product(k, 2), c.bc(k.v["L2_gnn_bv"][:, :]), ALU.add).then_inc(c.to_store, 1)
        dve.wait_ge(c.room, i + 2)
    after.links = 2
    return before, after, tanh_job


def softmax_phase(nc, k):
    lg = k.big[:, :].rearrange("p (t h) -> p t h", h=H2)

    def src(dve, link, part):
        link(dve, dve.tensor_reduce(part, k.big[:, :].rearrange("p (t h) -> p h t", h=H2), AX.X, ALU.max))

    def use(dve, link):
        top = k.tmp[:, 0:H2].unsqueeze(1).to_broadcast([P, T, H2])
        link(dve, dve.tensor_tensor(lg, lg, top, ALU.subtract))
    extreme_phase(nc, k, "top", src, H2, use)
    done = k.sem("exp_done")
    with nc.Block() as block:
        @block.scalar
        def _(act):
            act.activation(k.big[:, :], k.big[:, :], ACT.Exp).then_inc(done, 1)
            act.wait_ge(done, 1)


def stage_attention_out(k):
    def before(c, dve, i):
        link = c.link
        acc = k.acc[:, bass.ds(i * (BC * A2), BC * A2)].rearrange("p (b c) -> p b c", c=A2)
        den = c.s[:, 0, 0:BC * H2].rearrange("p (b h) -> p b h", h=H2)
        link(dve, dve.tensor_scalar(den, acc[:, :, C:A2], 1e-8, None, ALU.add))
        link(dve, dve.reciprocal(den, den))
        dve.tensor_tensor(by_heads(c.y, H2), by_heads(acc[:, :, 0:C], H2),
                          den.unsqueeze(3).to_broadcast([P, BC, H2, D2]), ALU.mult).then_inc(c.rows_ready, 1)
    before.links = 2

    def after(c, dve, i):
        link = c.link
        x = by_blocks(k.x, i)
        link(dve, dve.tensor_tensor(c.s, product(k, 0), c.bc(k.v["L2_gnn_bo"][:, :]), ALU.add))
        link(dve, dve.tensor_tensor(c.s, c.s, x, ALU.add))
        c.norm(dve, i, 1, 2, c.s, c.s)
        link(dve, dve.tensor_tensor(c.s, c.s, c.bc(k.v["L2_gnn_ln_g"][:, :]), ALU.mult))
        link(dve, dve.tensor_tensor(c.s, c.s, c.bc(k.v["L2_gnn_ln_b"][:, :]), ALU.add))
        link(dve, dve.tensor_tensor(c.s, c.s, x, ALU.add))
        c.norm(dve, i, 2, 2, c.s, x)
        dve.wait_ge(c.room, i + 1)
        copy(dve, c.o, x).then_inc(c.to_store, 1)
    after.links = 13
    return before, after


def stage_message_mid(k):
    def before(c, dve, i):
        copy(dve, c.y, by_blocks(k.x, i)).then_inc(c.rows_ready, 1)
    before.links = 0

    def after(c, dve, i):
        link = c.link
        link(dve, dve.tensor_tensor(c.s, product(k, 0), c.bc(k.v["L3_gnn_b_msg"][:, :]), ALU.add))
        times = k.deg[:, bass.ds(i * BC, BC)].unsqueeze(2).to_broadcast([P, BC, C])
        link(dve, dve.tensor_tensor(by_blocks(k.h, i), c.s, times, ALU.mult))
        part = k.big[:, bass.ds(i * (BC * C), BC * C)].rearrange("p (b c) -> p b c", c=C)
        link(dve, dve.tensor_tensor(part, product(k, 1), c.bc(k.v["L3_gnn_b_upd"][:, :]), ALU.add))
        link(dve, dve.tensor_tensor(part, part, by_blocks(k.x, i), ALU.add))
    after.links = 4
    return before, after


def stage_message_sum(k):
    def before(c, dve, i):
        acc = k.acc[:, bass.ds(i * (BC * C), BC * C)].rearrange("p (b c) -> p b c", c=C)
        copy(dve, c.y, acc).then_inc(c.rows_ready, 1)
    before.links = 0

    def after(c, dve, i):
        c.link(dve, dve.tensor_tensor(by_blocks(k.h, i), by_blocks(k.h, i), product(k, 0), ALU.add))
    after.links = 1
    return before, after


def stage_message_out(k):
    def before(c, dve, i):
        copy(dve, c.y, by_blocks(k.h, i)).then_inc(c.rows_ready, 1)
    before.links = 0

    def after(c, dve, i):
        link = c.link
        part = k.big[:, bass.ds(i * (BC * C), BC * C)].rearrange("p (b c) -> p b c", c=C)
        link(dve, dve.tensor_tensor(c.s, part, product(k, 0), ALU.add))
        c.norm(dve, i, 1, 1, c.s, by_blocks(k.x, i))
    after.links = 5
    return before, after


def store_phase(nc, k):
    stored = k.sem("out_stored")
    with nc.Block() as block:
        @block.sync
        def _(sp):
            sp.dma_start(k.out[0:(NB - 1) * P, :].rearrange("(b p) c -> p b c", p=P), k.x[:, 0:NB - 1, :])\
                .then_inc(stored, 16)
            sp.dma_start(k.out[(NB - 1) * P:N, :], k.x[0:REM, NB - 1, :]).then_inc(stored, 16)
            sp.wait_ge(stored, 32)


def build(nc, a, out):
    with ExitStack() as ctx:
        k = allocate(nc, ctx, a, out)

        def run(phase, *args):
            phase(nc, k, *args)
            nc.clear_and_free_semaphores(k.phase_sems)
            k.phase_sems = []
            nc.all_engine_barrier()

        run(load_phase)
        run(fields_phase)
        run(rank_phase)
        run(first_scatter_phase)
        run(second_scatter_phase)
        run(prepare_phase)
        run(lists_phase, "dst")
        run(dense_phase, "gcn_in", *stage_gcn_in(k), [k.w["L0_gnn_W1"]], [sqrt_job, "turn"],
                    [(k.tab_dram, lambda c: c.o)])
        run(pass_phase, "gcn1", "dst", k.tab_dram, C, "sum")
        run(dense_phase, "gcn_mid", *stage_gcn_mid(k), [k.w["L0_gnn_W2"]], [silu_job, sqrt_job, "turn"],
                    [(k.tab_dram, lambda c: c.o)])
        run(pass_phase, "gcn2", "dst", k.tab_dram, C, "sum")
        run(dense_phase, "gcn_out", *stage_gcn_out(k), [k.w["L1_gnn_W"]], [silu_job, sqrt_job, "turn"])
        run(shift_phase)
        run(pass_phase, "gat_max", "dst", k.tab_a_dram, H1, "max")
        run(gat_maximum_phase)
        run(pass_phase, "gat", "dst", k.tab_h_dram, A1, "gat")
        before, after, tanh_job = stage_gat_out(k)
        run(dense_phase, "gat_out", before, after, [k.w[n] for n in ("L2_gnn_Wq", "L2_gnn_Wk", "L2_gnn_Wv")],
                    [tanh_job, sqrt_job, "turn"], [(k.tab_k_dram, lambda c: c.o), (k.tab_v_dram, lambda c: c.s)])
        run(lists_phase, "src")
        run(pass_phase, "logit", "src", k.tab_k_dram, C, "logit")
        run(softmax_phase)
        run(pass_phase, "value", "src", k.tab_v_dram, C, "value")
        run(dense_phase, "att_out", *stage_attention_out(k), [k.w["L2_gnn_Wo"]], ["turn", sqrt_job, sqrt_job],
                    [(k.tab_dram, lambda c: c.o)])
        run(lists_phase, "dst")
        run(dense_phase, "msg_mid", *stage_message_mid(k), [k.bot["L3_gnn_W_msg"], k.top["L3_gnn_W_upd"]],
                    ["turn"])
        run(pass_phase, "msg", "dst", k.tab_dram, C, "sum")
        run(dense_phase, "msg_sum", *stage_message_sum(k), [k.top["L3_gnn_W_msg"]], ["turn"])
        run(dense_phase, "msg_out", *stage_message_out(k), [k.bot["L3_gnn_W_upd"]], ["turn", sqrt_job])
        run(store_phase)


INPUTS = ("x", "src", "dst", "edge_weight1") + MATS + HALVES + VECS + ATTS + (
    "L0_gnn_t_emb", "L2_gnn_We1", "L2_gnn_be1", "L2_gnn_We2", "L2_gnn_be2")


def kernel(**inputs):
    import numpy as _np
    import concourse.bacc as _bacc
    from concourse.bass_utils import run_bass_kernel_spmd as _run

    nc = _bacc.Bacc("TRN2", target_bir_lowering=False, num_devices=1)
    arrays, args = {}, {}
    for name in INPUTS:
        arr = _np.ascontiguousarray(inputs[name])
        arrays[f"in_{name}"] = arr
        args[name] = nc.dram_tensor(f"in_{name}", arr.shape, mybir.dt.from_np(arr.dtype), kind="ExternalInput").ap()
    out = nc.dram_tensor("out", (N, C), F32, kind="ExternalOutput").ap()
    build(nc, args, out)
    return _run(nc, [arrays], core_ids=[0]).results[0]["out"]
```

```python
import itertools
import math
from contextlib import ExitStack

import concourse.bass as bass
from concourse import mybir

F32 = mybir.dt.float32
BF16 = mybir.dt.bfloat16
I32 = mybir.dt.int32
ALU = mybir.AluOpType
ACT = mybir.ActivationFunctionType
AX = mybir.AxisListType

P = 128
N = 6250
C = 128
E = 200000
NB = -(-N // P)
NP = NB * P
REM = N - (NB - 1) * P
BC = 7
NCH = NB // BC
EP = 125
EC = E // EP
G = 2
GE = G * P
GSH = GE.bit_length() - 1
H1, D1 = 4, 32
H2, D2 = 8, 16
A1 = C + H1
A2 = C + H2
BODY = 16
HALF = BODY // 2
QUARTER = BODY // 4
QUARTERS = BODY // QUARTER
GB = BODY // G
MAX_RING = 4
SUM_RING = 4
NG = -(-((E + NB * (GE - 1)) // GE) // GB) * GB
T = NG * G
IT = T // BODY
PAD = 200.0
EPS = 1e-5
NEG = -1e30
CUTOFF = 5.0
ROUND = 12582912.0

assert NB % BC == 0 and EP * EC == E and EC % BODY == 0 and T % P == 0

MATS = ("L0_gnn_W1", "L0_gnn_Wt1", "L0_gnn_W2", "L0_gnn_Wt2", "L1_gnn_W", "L2_gnn_Wq", "L2_gnn_Wk",
        "L2_gnn_Wv", "L2_gnn_Wo")
HALVES = ("L3_gnn_W_msg", "L3_gnn_W_upd")
VECS = ("L0_gnn_g1", "L0_gnn_bn1", "L0_gnn_b1", "L0_gnn_bt1", "L0_gnn_g2", "L0_gnn_bn2",
        "L0_gnn_b2", "L0_gnn_bt2", "L1_gnn_bias", "L2_gnn_bq", "L2_gnn_bk", "L2_gnn_bv",
        "L2_gnn_bo", "L2_gnn_ln_g", "L2_gnn_ln_b", "L3_gnn_b_msg", "L3_gnn_b_upd")
ATTS = ("L1_gnn_att_src", "L1_gnn_att_dst")


def copy(dve, out, rows):
    return dve.tensor_scalar(out, rows, 1.0, None, ALU.mult)


class Link:

    def __init__(self, sem):
        self.sem, self.base, self.n, self.turn, self.per = sem, 0, 0, 0, 0

    def loop(self, turn, per):
        self.base += self.n
        self.turn, self.per, self.n = turn, per, 0

    def end(self, turns):
        assert self.n == self.per, (self.n, self.per)
        self.base += turns * self.per
        self.turn, self.per, self.n = 0, 0, 0

    def __call__(self, eng, ins):
        ins.then_inc(self.sem, 1)
        self.n += 1
        eng.wait_ge(self.sem, self.turn * self.per + self.base + self.n)


class Bufs:
    pass


def allocate(nc, ctx, a, out):
    k = Bufs()
    k.a, k.out = a, out

    def sb(name, shape, dt=F32):
        return ctx.enter_context(nc.sbuf_tensor(name, shape, dt))

    def dram(name, shape):
        return nc.dram_tensor(name, shape, F32, kind="Internal").ap()

    numbers = itertools.count()
    k.phase_sems = []

    def phase_sem(name):
        k.phase_sems.append(nc.alloc_semaphore(name=f"{name}_{next(numbers)}"))
        return k.phase_sems[-1]
    k.sem = phase_sem
    k.by_dst_dram = dram("by_dst", (P * T, 2))
    k.by_src_dram = dram("by_src", (P * T, 4))
    k.w_rows_dram = dram("w_rows", (T, P))
    k.tab_dram = dram("tab", (NP, C))
    k.tab_a_dram = dram("tab_a", (NP, H1))
    k.tab_h_dram = dram("tab_h", (NP, A1))
    k.tab_kv_dram = dram("tab_kv", (NP, 2 * C))
    k.value_rows_dram = dram("value_rows", (P, T * C))
    k.ramp_i = sb("ramp_i", [P, P], I32)
    k.row_i = sb("row_i", [P, 1], I32)
    k.ramp = sb("ramp", [P, P])
    k.row = sb("row", [P, 1])
    k.ident = sb("ident", [P, P])
    k.below = sb("below", [P, P])
    k.upto = sb("upto", [P, P])
    k.ones = sb("ones", [P, P])
    k.x = sb("x", [P, NB, C])
    k.h = sb("h", [P, NB, C])
    k.acc = sb("acc", [P, NB * A2])
    k.deg = sb("deg", [P, NB])
    k.dinv = sb("dinv", [P, NB])
    k.nodev = sb("nodev", [P, NB, 2 * H1])
    k.asrc = sb("asrc", [P, NB, H1])
    k.wide = k.acc[:, 0:BODY * 2 * C].rearrange("p (m c) -> p m c", c=2 * C)
    k.maxa = sb("maxa", [P, NB * H1])
    k.idx = sb("idx", [P, T + BODY], I32)
    k.loc = sb("loc", [P, T + G])
    k.cut = sb("cut", [P, T])
    k.block_of = {"dst": sb("block_dst", [1, NG + 1], I32), "src": sb("block_src", [1, NG + 1], I32)}
    k.big = sb("big", [P, T * H2])
    sizes = (BODY * A2, BODY * P, 2 * G * P, 4 * G * C)
    room = sb("room", [P, sum(sizes)])
    ends = [sum(sizes[:m + 1]) for m in range(4)]
    k.gat = room[:, 0:ends[0]].rearrange("p (m c) -> p m c", c=A2)
    k.oneh = room[:, ends[0]:ends[1]].rearrange("p (m c) -> p m c", c=P)
    k.hot_t = room[:, ends[1]:ends[2]].rearrange("p (m c) -> p m c", c=G * P)
    k.wk = room[:, ends[2]:ends[3]]
    k.chunk_room = room
    k.stage = sb("stage", [P, BODY], I32)
    k.tmp = sb("tmp", [P, 256])
    k.offs = sb("offs", [P, NB])
    k.st = sb("st", [P, BC, 16])
    k.psum_pair = [ctx.enter_context(nc.psum_tensor(f"banks{i}", [P, 1024], F32))[:, :] for i in range(4)]
    k.psum = [k.psum_pair[i // 2][:, i % 2 * 512:(i % 2 + 1) * 512] for i in range(8)]
    k.w = {n: sb("m_" + n, [P, C]) for n in MATS}
    k.top = {n: sb("t_" + n, [P, C]) for n in HALVES}
    k.bot = {n: sb("b_" + n, [P, C]) for n in HALVES}
    k.v = {n: sb("v_" + n, [P, C]) for n in VECS + ATTS}
    k.be2 = sb("be2", [P, H2])
    k.temb = sb("temb", [P, 1])
    k.be1 = sb("be1", [P, 1])
    k.we1 = sb("we1", [1, P])
    k.we2 = sb("we2", [H2, P])
    k.we2t = sb("we2t", [P, H2])
    f = [k.big[0:EP, i * EC:(i + 1) * EC] for i in range(6)]
    k.dst_f, k.w_f, k.sloc, k.shi, k.dhi, k.mask = f
    xx = k.x[:, :, :].rearrange("p b c -> p (b c)")
    k.src_f, k.dloc = xx[0:EP, 0:EC], xx[0:EP, EC:2 * EC]
    hh = k.h[:, :, :].rearrange("p b c -> p (b c)")
    k.zeros = hh[0:EP, 0:EC]
    k.pos = {"src": hh[0:EP, EC:2 * EC].bitcast(I32), "dst": hh[0:EP, 2 * EC:3 * EC].bitcast(I32)}
    k.raw_s, k.raw_d = k.acc[0:EP, 0:EC].bitcast(I32), k.acc[0:EP, EC:2 * EC].bitcast(I32)
    k.shifted = k.acc[0:EP, 2 * EC:3 * EC].bitcast(I32)
    k.scan, k.posf = k.acc[0:EP, 3 * EC:4 * EC], k.acc[0:EP, 0:EC]
    lasting = lambda name: ctx.enter_context(nc.semaphore(name))
    k.gathered = [lasting(f"gathered{i}") for i in range(BODY)]
    k.gathered_base = 0
    k.const = lasting("const")
    k.passed = lasting("passed")
    return k


def load_phase(nc, k):
    a = k.a
    loaded, iotas, filled, zero_done = (k.sem(n) for n in ("loaded", "iotas", "filled", "zero_done"))
    link = Link(k.sem("const_step"))
    pattern = k.h[:, :, :].rearrange("p b c -> p (b c)")
    with nc.Block() as block:
        @block.sync
        def _(sp):
            count = [0]

            def load(dst, src):
                sp.dma_start(dst, src).then_inc(loaded, 16)
                count[0] += 16
            load(k.raw_s, a["src"].rearrange("(p c) -> p c", p=EP))
            load(k.raw_d, a["dst"].rearrange("(p c) -> p c", p=EP))
            load(k.w_f, a["edge_weight1"].rearrange("(p c) o -> p (c o)", p=EP))
            for n in MATS:
                load(k.w[n][:, :], a[n])
            for n in HALVES:
                load(k.top[n][:, :], a[n][0:C, :])
                load(k.bot[n][:, :], a[n][C:2 * C, :])
            for n in VECS:
                load(k.v[n][:, :], a[n].partition_broadcast(P))
            for n in ATTS:
                load(k.v[n][:, :], a[n].rearrange("h c -> (h c)").partition_broadcast(P))
            load(k.be2[:, :], a["L2_gnn_be2"].partition_broadcast(P))
            load(k.temb[:, :], a["L0_gnn_t_emb"].rearrange("(c o) -> c o", o=1))
            load(k.be1[:, :], a["L2_gnn_be1"].rearrange("(c o) -> c o", o=1))
            load(k.we1[:, :], a["L2_gnn_We1"].rearrange("c o -> o c"))
            load(k.we2[:, :], a["L2_gnn_We2"])
            sp.wait_ge(loaded, count[0])

        @block.scalar
        def _(act):
            act.wait_ge(filled, 2)
            half = P * T // 2 // P
            rows = k.by_src_dram.rearrange("(p s r) f -> p s (r f)", p=P, s=2)
            for s in range(2):
                act.dma_start(rows[:, s, :], pattern[:, 0:half * 4]).then_inc(zero_done, 16)
            rows = k.by_dst_dram.rearrange("(p s r) f -> p s (r f)", p=P, s=2)
            for s in range(2):
                act.dma_start(rows[:, s, :], pattern[:, half * 4:half * 6]).then_inc(zero_done, 16)
            act.wait_ge(zero_done, 64)

        @block.gpsimd
        def _(pool):
            pool.iota(k.ramp_i[:, :], pattern=[[1, P]], base=0, channel_multiplier=0).then_inc(iotas, 1)
            pool.iota(k.idx[:, 0:NG], pattern=[[1, NG]], base=0, channel_multiplier=0).then_inc(iotas, 1)
            pool.iota(k.row_i[:, :], pattern=[[1, 1]], base=0, channel_multiplier=1).then_inc(iotas, 1)

        @block.vector
        def _(dve):
            half = P * T // 2 // P
            link(dve, dve.memset(pattern[:, 0:half * 6], 0.0))
            p4 = pattern[:, 0:half * 4].rearrange("p (r f) -> p r f", f=4)
            p2 = pattern[:, half * 4:half * 6].rearrange("p (r f) -> p r f", f=2)
            dve.memset(p4[:, :, 1:2], PAD).then_inc(filled, 1)
            dve.memset(p2[:, :, 1:2], PAD).then_inc(filled, 1)
            dve.memset(k.ones[:, :], 1.0)
            dve.wait_ge(iotas, 3)
            dve.tensor_copy(k.loc[:, 0:NG], k.idx[:, 0:NG])
            link(dve, dve.tensor_copy(k.ramp[:, :], k.ramp_i[:, :]))
            link(dve, dve.tensor_copy(k.row[:, :], k.row_i[:, :]))
            dve.tensor_scalar(k.ident[:, :], k.ramp[:, :], k.row[:, 0:1], None, ALU.is_equal)
            dve.tensor_scalar(k.below[:, :], k.ramp[:, :], k.row[:, 0:1], None, ALU.is_gt)
            dve.tensor_scalar(k.upto[:, :], k.ramp[:, :], k.row[:, 0:1], None, ALU.is_ge).then_inc(k.const, 1)


def fields_phase(nc, k):
    link = Link(k.sem("field_step"))
    with nc.Block() as block:
        @block.vector
        def _(dve):
            for raw, full, loc, hi in ((k.raw_s, k.src_f, k.sloc, k.shi), (k.raw_d, k.dst_f, k.dloc, k.dhi)):
                dve.tensor_copy(full, raw)
                link(dve, dve.tensor_scalar(k.shifted, raw, 7, None, ALU.arith_shift_right))
                link(dve, dve.tensor_copy(hi, k.shifted))
                link(dve, dve.tensor_scalar(k.shifted, raw, P - 1, None, ALU.bitwise_and))
                link(dve, dve.tensor_copy(loc, k.shifted))


class Rank:

    def __init__(self, k, key):
        self.k, self.key = k, key
        self.counted, self.summed, self.rounded, self.ended, self.compared, self.tabled, self.tabled_read, \
            self.picked, self.merged = (k.sem(f"{key}_{s}") for s in (
                "counted", "summed", "rounded", "ended", "compared", "tabled", "tabled_read", "picked", "merged"))
        self.link = Link(k.sem(key + "_step"))
        self.spans = [(lo, min(lo + 512, EC)) for lo in range(0, EC, 512)]
        self.cnt = k.tmp[:, 0:NB]
        self.col_i, self.col = k.st[0:NB, 0, 0:1].bitcast(I32), k.st[0:NB, 0, 1:2]
        self.group = k.loc[0:NB, 0:NG]
        self.past = k.cut[0:NB, 0:NG]

    def tensor(self, pe):
        k, ps, cnt = self.k, self.k.psum, self.cnt
        pe.wait_ge(self.counted, 1)
        pe.matmul(ps[0][:, 0:NB], k.ones[0:EP, :], cnt[0:EP, :], start=True, stop=True)
        pe.matmul(ps[1][0:EP, 0:NB], k.below[0:EP, 0:EP], cnt[0:EP, :], start=True, stop=True)
        pe.matmul(ps[2][0:NB, 0:1], cnt[0:EP, :], k.ones[0:EP, 0:1], start=True, stop=True)\
            .then_inc(self.summed, 1)
        pe.wait_ge(self.rounded, 1)
        pe.matmul(ps[3][0:NB, 0:1], k.upto[0:NB, 0:NB], self.col, start=True, stop=True).then_inc(self.ended, 1)
        pe.wait_ge(self.compared, 1)
        pe.matmul(ps[4][0:1, 0:512], k.ones[0:NB, 0:1], self.past[:, 0:512], start=True, stop=True)
        pe.matmul(ps[5][0:1, 0:NG - 512], k.ones[0:NB, 0:1], self.past[:, 512:NG], start=True, stop=True)\
            .then_inc(self.tabled, 1)
        pe.wait_ge(self.tabled_read, 1)

        def add(rows, start, stop):
            for m, (lo, up) in enumerate(self.spans):
                last = pe.matmul(ps[m][0:EP, 0:up - lo], k.ident[0:EP, 0:EP], rows[:, lo:up], start=start,
                                 stop=stop, skip_group_check=True)
            last.then_inc(self.merged, 1)
        add(k.zeros, True, False)
        with pe.Fori(0, NB) as b:
            pe.wait_ge(self.picked, b + 1)
            add(k.posf, False, False)
        add(k.zeros, False, True)

    def vector(self, dve):
        k, ps, link, cnt = self.k, self.k.psum, self.link, self.cnt
        hi = {"src": k.shi, "dst": k.dhi}[self.key]
        tot_i, tot = k.tmp[:, 64:64 + NB].bitcast(I32), k.tmp[:, 128:128 + NB]
        pre = k.tmp[:, 192:192 + NB]
        end = k.st[0:NB, 0, 2:3]
        link(dve, dve.memset(k.zeros, 0.0))
        with dve.Fori(0, NB) as b:
            link.loop(b, 1)
            link(dve, dve.tensor_scalar(k.mask, hi, k.ramp[0:EP, bass.ds(b, 1)], 0.0, ALU.is_equal,
                                        ALU.add, accum_out=cnt[0:EP, bass.ds(b, 1)]))
        link.end(NB)
        dve.sem_inc(self.counted, 1)
        dve.wait_ge(self.summed, 1)
        link(dve, dve.tensor_scalar(tot_i, ps[0][:, 0:NB], float(GE - 1), None, ALU.add))
        link(dve, dve.tensor_scalar(tot_i, tot_i, GSH, None, ALU.arith_shift_right))
        link(dve, dve.tensor_copy(tot, tot_i))
        link(dve, dve.tensor_tensor_scan(pre[0:EP, :], tot[0:EP, :], k.zeros[:, 0:NB], 0.0, ALU.add, ALU.add))
        link(dve, dve.tensor_tensor(pre[0:EP, :], pre[0:EP, :], tot[0:EP, :], ALU.subtract))
        link(dve, dve.scalar_tensor_tensor(k.offs[0:EP, :], pre[0:EP, :], float(GE), ps[1][0:EP, 0:NB],
                                           ALU.mult, ALU.add))
        link(dve, dve.tensor_scalar(self.col_i, ps[2][0:NB, 0:1], float(GE - 1), None, ALU.add))
        link(dve, dve.tensor_scalar(self.col_i, self.col_i, GSH, None, ALU.arith_shift_right))
        dve.tensor_copy(self.col, self.col_i).then_inc(self.rounded, 1)
        dve.wait_ge(self.ended, 1)
        link(dve, dve.tensor_copy(end, ps[3][0:NB, 0:1]))
        dve.tensor_scalar(self.past, self.group, end, None, ALU.is_ge).then_inc(self.compared, 1)
        dve.wait_ge(self.tabled, 1)
        table = k.block_of[self.key]
        dve.memset(table[0:1, NG:NG + 1], 0)
        dve.tensor_scalar(table[0:1, 0:512], ps[4][0:1, 0:512], float(NB - 1), None, ALU.min)
        dve.tensor_scalar(table[0:1, 512:NG], ps[5][0:1, 0:NG - 512], float(NB - 1), None, ALU.min)\
            .then_inc(self.tabled_read, 1)
        with dve.Fori(0, NB) as b:
            link.loop(b, 2)
            link(dve, dve.tensor_scalar(k.mask, hi, k.ramp[0:EP, bass.ds(b, 1)], None, ALU.is_equal))
            link(dve, dve.tensor_tensor_scan(k.scan, k.mask, k.zeros, k.offs[0:EP, bass.ds(b, 1)],
                                             ALU.add, ALU.add))
            dve.wait_ge(self.merged, b + 1)
            dve.tensor_tensor(k.posf, k.scan, k.mask, ALU.mult).then_inc(self.picked, 1)
            dve.wait_ge(self.picked, b + 1)
        link.end(NB)
        dve.wait_ge(self.merged, NB + 2)
        for m, (lo, up) in enumerate(self.spans):
            link(dve, dve.tensor_copy(k.posf[:, lo:up], ps[m][0:EP, 0:up - lo]))
        slot = k.pos[self.key]
        link(dve, dve.tensor_scalar(slot, k.posf, -1.0, None, ALU.add))
        link(dve, dve.tensor_scalar(k.shifted, slot, 7, None, ALU.arith_shift_right))
        link(dve, dve.tensor_copy(k.scan, k.shifted))
        link(dve, dve.tensor_scalar(k.shifted, slot, P - 1, None, ALU.bitwise_and))
        link(dve, dve.tensor_copy(k.posf, k.shifted))
        link(dve, dve.scalar_tensor_tensor(slot, k.posf, float(T), k.scan, ALU.mult, ALU.add))


class Scatter:

    def __init__(self, k, key):
        self.k = k
        self.staged, self.scattered = k.sem("staged"), [k.sem(f"scattered{h}") for h in range(2)]
        self.fields = {"src": (k.dst_f, k.sloc, k.w_f), "dst": (k.src_f, k.dloc)}[key]
        self.target = {"src": k.by_src_dram, "dst": k.by_dst_dram}[key]
        self.rec = k.gat[:, :, 0:len(self.fields) + len(self.fields) % 2]
        self.slots = k.pos[key]
        self.per = len(self.fields) + 1

    def clear(self, act):
        if len(self.fields) % 2:
            act.activation(self.rec[0:EP, :, len(self.fields)], self.fields[0][:, 0:BODY], ACT.Copy)

    def stage(self, act, i, h, first=False):
        if not first:
            act.wait_ge(self.scattered[h], i * (16 * HALF))
        at, to = bass.ds(i * BODY + h * HALF, HALF), slice(h * HALF, (h + 1) * HALF)
        act.activation(self.k.stage[0:EP, to], self.slots[:, at], ACT.Copy).then_inc(self.staged, 1)
        for m, field in enumerate(self.fields):
            act.activation(self.rec[0:EP, to, m], field[:, at], ACT.Copy).then_inc(self.staged, 1)

    def gpsimd(self, pool):
        k, turns = self.k, EC // BODY
        with pool.Fori(0, turns) as i:
            for h in range(2):
                pool.wait_ge(self.staged, i * (2 * self.per) + self.per * (h + 1))
                pool.sem_inc(k.passed, 1)
                for m in range(h * HALF, (h + 1) * HALF):
                    pool.indirect_dma_start(
                        self.target, bass.IndirectOffsetOnAxis(k.stage[0:EP, m:m + 1], axis=0),
                        self.rec[0:EP, m, :], None).then_inc(self.scattered[h], 16)
        for h in range(2):
            pool.wait_ge(self.scattered[h], turns * 16 * HALF)


class Degree:

    def __init__(self, k):
        self.k = k
        self.hot, self.taken, self.zeroed, self.summed = (k.sem("deg_" + n) for n in (
            "hot", "taken", "zeroed", "summed"))
        self.link = Link(k.sem("deg_step"))
        self.lo = k.wk[:, 0:G * C].bitcast(BF16).rearrange("p (r c) -> p r c", r=4)
        self.hi = k.wk[:, G * C:2 * G * C].bitcast(BF16).rearrange("p (r c) -> p r c", r=4)
        self.none = k.wk[:, 2 * G * C:3 * G * C].bitcast(BF16)[0:EP, 0:P]
        self.dest = k.psum[7][:, 0:NB]

    def vector(self, dve):
        k = self.k
        dve.memset(self.none, 0.0).then_inc(self.zeroed, 1)
        with dve.Fori(0, EC // 4) as i:
            for r in range(4):
                dve.wait_ge(self.taken, i * 4 + r + 1)
                dve.tensor_scalar(self.lo[0:EP, r, :], k.ramp[0:EP, :], k.dloc[:, bass.ds(i * 4 + r, 1)], None,
                                  ALU.is_equal).then_inc(self.hot, 1)
                dve.tensor_scalar(self.hi[0:EP, r, 0:NB], k.ramp[0:EP, 0:NB], k.dhi[:, bass.ds(i * 4 + r, 1)],
                                  None, ALU.is_equal).then_inc(self.hot, 1)
        dve.wait_ge(self.summed, 1)
        self.link(dve, dve.tensor_copy(k.deg[:, :], self.dest))

    def tensor(self, pe):
        pe.wait_ge(self.zeroed, 1)
        pe.matmul(self.dest, self.none, self.none[:, 0:NB], start=True, stop=False, skip_group_check=True)\
            .then_inc(self.taken, 4)
        with pe.Fori(0, EC // 4) as i:
            for r in range(4):
                pe.wait_ge(self.hot, i * 8 + 2 * (r + 1))
                pe.matmul(self.dest, self.lo[0:EP, r, :], self.hi[0:EP, r, 0:NB], start=False, stop=False,
                          skip_group_check=True).then_inc(self.taken, 1)
        pe.matmul(self.dest, self.none, self.none[:, 0:NB], start=False, stop=True, skip_group_check=True)\
            .then_inc(self.summed, 1)


def rank_phase(nc, k):
    rank = Rank(k, "src")
    turned = k.sem("we2_turned")
    with nc.Block() as block:
        @block.tensor
        def _(pe):
            pe.transpose(k.psum[7][:, 0:H2], k.we2[:, :], k.ident[0:H2, 0:H2]).then_inc(turned, 1)
            rank.tensor(pe)

        @block.vector
        def _(dve):
            dve.wait_ge(turned, 1)
            dve.tensor_copy(k.we2t[:, :], k.psum[7][:, 0:H2])
            rank.vector(dve)


def first_scatter_phase(nc, k):
    scatter, rank, degree = Scatter(k, "src"), Rank(k, "dst"), Degree(k)
    with nc.Block() as block:
        @block.gpsimd
        def _(pool):
            scatter.gpsimd(pool)

        @block.scalar
        def _(act):
            scatter.clear(act)
            for h in range(2):
                scatter.stage(act, 0, h, first=True)
            with act.Fori(1, EC // BODY) as i:
                for h in range(2):
                    scatter.stage(act, i, h)

        @block.tensor
        def _(pe):
            rank.tensor(pe)
            degree.tensor(pe)

        @block.vector
        def _(dve):
            rank.vector(dve)
            degree.vector(dve)


def second_scatter_phase(nc, k):
    scatter = Scatter(k, "dst")
    loaded, turned, copied, rowed, halved, sined = (k.sem("cut_" + s) for s in (
        "loaded", "turned", "copied", "rowed", "halved", "sined"))
    fetched = [k.sem("bias_fetched0"), k.sem("bias_fetched1")]
    outer, hidden, mixed, added = (k.sem("bias_" + n) for n in ("outer", "hidden", "mixed", "added"))
    link = Link(k.sem("cut_step"))
    rec = k.acc[:, 0:T * 4].rearrange("p (t f) -> p t f", f=4)
    w, hh = k.big[:, 0:T], k.big[:, T:2 * T]
    W = 4
    S = BODY // W
    wrow = k.acc[0:1, 0:2 * BODY * P].rearrange("o (r c) -> o r c", r=2)
    hid = k.acc[:, 2 * BODY * P:2 * BODY * P + 2 * W * P].rearrange("p (r c) -> p r c", r=2)
    bank, mix = (k.psum[2], k.psum[3]), (k.psum[4], k.psum[5])
    with nc.Block() as block:
        @block.gpsimd
        def _(pool):
            scatter.gpsimd(pool)

        @block.sync
        def _(sp):
            sp.dma_start(rec, k.by_src_dram.rearrange("(p t) f -> p t f", p=P)).then_inc(loaded, 16)
            for m in range(T // P):
                sp.wait_ge(copied, m + 1)
                sp.dma_start(k.w_rows_dram[m * P:(m + 1) * P, :], k.wk[:, m % 4 * P:(m % 4 + 1) * P])\
                    .then_inc(rowed, 16)
                sp.wait_ge(rowed, 16 * (m + 1))
            link_done = 10
            sp.wait_ge(link.sem, link_done)

            def fetch(i, r):
                sp.dma_start(wrow[:, r, :], k.w_rows_dram[bass.ds(i * BODY, BODY), :]
                             .rearrange("(o t) q -> o (t q)", o=1)).then_inc(fetched[r], 16)
            fetch(0, 0)
            fetch(1, 1)
            with sp.Fori(1, IT // 2) as i:
                for r in range(2):
                    sp.wait_ge(outer, i * (2 * S) + (r - 1) * S)
                    fetch(i * 2 + r, r)

        @block.tensor
        def _(pe):
            pe.wait_ge(loaded, 16)
            for m in range(T // P):
                if m >= 2:
                    pe.wait_ge(copied, m - 1)
                pe.transpose(k.psum[m % 2][:, 0:P], rec[:, m * P:(m + 1) * P, 2], k.ident[:, :])\
                    .then_inc(turned, 1)

            def body(i, first):
                for n in range(2 * S):
                    r, q = n // S, n % 2
                    if n % S == 0:
                        pe.wait_ge(fetched[r], i * 16 + 16)
                    if not first or n >= 2:
                        pe.wait_ge(hidden, i * (2 * S) + n - 1)
                    pe.matmul(bank[q][:, :], k.we1[:, :], wrow[:, r, n % S * W * P:(n % S + 1) * W * P],
                              start=True, stop=True).then_inc(outer, 1)
                    if not first or n >= 1:
                        mix_step(i, n - 1, first)

            def mix_step(i, n, first):
                pe.wait_ge(hidden, i * (2 * S) + n + 1)
                if not first or n >= 2:
                    pe.wait_ge(added, i * (2 * S) + n - 1)
                for t in range(W):
                    last = pe.matmul(mix[n % 2][:, t * H2:(t + 1) * H2], hid[:, n % 2, t * P:(t + 1) * P],
                                     k.we2t[:, :], start=True, stop=True)
                last.then_inc(mixed, 1)
            body(0, True)
            with pe.Fori(1, IT // 2) as i:
                body(i, False)
            mix_step(IT // 2 - 1, 2 * S - 1, False)

        @block.scalar
        def _(act):
            for h in range(2):
                scatter.stage(act, 0, h, first=True)
            act.wait_ge(halved, 1)
            act.activation(w, w, ACT.Sin).then_inc(sined, 1)

            def silu(i, n, first):
                act.wait_ge(outer, i * (2 * S) + n + 1)
                if not first or n >= 2:
                    act.wait_ge(mixed, i * (2 * S) + n - 1)
                act.activation(hid[:, n % 2, :], bank[n % 2][:, :], ACT.Silu, bias=k.be1[:, 0:1])\
                    .then_inc(hidden, 1)

            def body(i, first, stage=True):
                for n in range(2 * S):
                    silu(i, n, first)
                    if n % 2 and stage and not (first and n < 4):
                        scatter.stage(act, i * 2 + n // 4, n // 2 % 2)
            body(0, True)
            turns = EC // BODY // 2
            with act.Fori(1, turns) as i:
                body(i, False)
            with act.Fori(turns, IT // 2) as i:
                body(i, False, stage=False)

        @block.vector
        def _(dve):
            dve.wait_ge(loaded, 16)
            link(dve, dve.tensor_scalar(w, rec[:, :, 2], 0.5 / CUTOFF, None, ALU.mult))
            link(dve, dve.tensor_scalar(hh, w, ROUND, -ROUND, ALU.add, ALU.add))
            link(dve, dve.tensor_tensor(w, w, hh, ALU.subtract))
            link(dve, dve.tensor_scalar(hh, w, -1.0, None, ALU.mult))
            link(dve, dve.tensor_tensor(w, w, hh, ALU.max))
            link(dve, dve.tensor_scalar(w, w, -2.0 * math.pi, 0.5 * math.pi, ALU.mult, ALU.add))
            dve.tensor_scalar(w, w, 1.5707963, -1.5707963, ALU.min, ALU.max).then_inc(halved, 1)
            neg = k.loc[:, 0:T]
            link(dve, dve.tensor_scalar(neg, rec[:, :, 1], float(P), NEG, ALU.is_ge, ALU.mult))
            dve.wait_ge(sined, 1)
            link(dve, dve.tensor_scalar(w, w, 0.5, 0.5, ALU.mult, ALU.add))
            link(dve, dve.scalar_tensor_tensor(k.cut[:, :], rec[:, :, 2], CUTOFF, w, ALU.is_lt, ALU.mult))
            for m in range(T // P):
                dve.wait_ge(turned, m + 1)
                if m >= 4:
                    dve.wait_ge(rowed, 16 * (m - 3))
                dve.tensor_copy(k.wk[:, m % 4 * P:(m % 4 + 1) * P], k.psum[m % 2][:, 0:P])\
                    .then_inc(copied, 1)
            dve.wait_ge(copied, T // P)
            dve.sem_inc(link.sem, 1)
            b2 = k.be2[:, :].unsqueeze(1).to_broadcast([P, W, H2])
            with dve.Fori(0, IT // 2) as i:
                for n in range(2 * S):
                    dve.wait_ge(mixed, i * (2 * S) + n + 1)
                    dve.tensor_tensor(
                        k.big[:, bass.ds((i * (2 * S) + n) * (W * H2), W * H2)]
                        .rearrange("p (t h) -> p t h", h=H2),
                        mix[n % 2][:, 0:W * H2].rearrange("p (t h) -> p t h", h=H2), b2, ALU.add)\
                        .then_inc(added, 1)
            dve.wait_ge(added, T // W)
            lg = k.big[:, :].rearrange("p (t h) -> p t h", h=H2)
            dve.tensor_tensor(lg, lg, neg.unsqueeze(2).to_broadcast([P, T, H2]), ALU.add)


def prepare_phase(nc, k):
    turned, copied, summed, spread, plus_one, rooted = (k.sem("prep_" + n) for n in (
        "turned", "copied", "summed", "spread", "plus_one", "rooted"))
    link = Link(k.sem("prep_step"))
    turn = ("L2_gnn_Wq", "L2_gnn_Wk", "L2_gnn_Wv", "L2_gnn_Wo")
    temb_rep = k.wk[:, 0:C]
    x_clear, x_loaded = k.sem("x_clear"), k.sem("x_loaded")
    with nc.Block() as block:
        @block.sync
        def _(sp):
            sp.dma_start(k.x[:, 0:NB - 1, :], k.a["x"][0:(NB - 1) * P, :].rearrange("(b p) c -> p b c", p=P))\
                .then_inc(x_loaded, 16)
            sp.wait_ge(x_clear, 1)
            sp.dma_start(k.x[0:REM, NB - 1, :], k.a["x"][(NB - 1) * P:N, :]).then_inc(x_loaded, 16)
            sp.wait_ge(x_loaded, 32)

        @block.tensor
        def _(pe):
            for m, n in enumerate(turn):
                last = pe.transpose(k.psum[0][:, m * C:(m + 1) * C], k.w[n][:, :], k.ident[:, :])
            last.then_inc(turned, 1)
            pe.wait_ge(spread, 1)
            pe.matmul(k.psum[2][:, 0:C], temb_rep, k.w["L0_gnn_Wt1"][:, :], start=True, stop=True)
            pe.matmul(k.psum[2][:, C:2 * C], temb_rep, k.w["L0_gnn_Wt2"][:, :], start=True, stop=True)\
                .then_inc(summed, 1)

        @block.scalar
        def _(act):
            act.wait_ge(plus_one, 1)
            act.activation(k.dinv[:, :], k.dinv[:, :], ACT.Sqrt).then_inc(rooted, 1)

        @block.vector
        def _(dve):
            dve.memset(k.x[:, NB - 1, :], 0.0).then_inc(x_clear, 1)
            dve.tensor_scalar(k.dinv[:, :], k.deg[:, :], 1.0, None, ALU.add).then_inc(plus_one, 1)
            dve.tensor_scalar(temb_rep, k.ones[:, :], k.temb[:, 0:1], None, ALU.mult).then_inc(spread, 1)
            dve.wait_ge(turned, 1)
            for m, n in enumerate(turn):
                dve.tensor_copy(k.w[n][:, :], k.psum[0][:, m * C:(m + 1) * C])
            dve.wait_ge(rooted, 1)
            link(dve, dve.reciprocal(k.dinv[:, :], k.dinv[:, :]))
            dve.wait_ge(summed, 1)
            for m, (b, bt) in enumerate((("L0_gnn_b1", "L0_gnn_bt1"), ("L0_gnn_b2", "L0_gnn_bt2"))):
                link(dve, dve.tensor_tensor(k.v[b][:, :], k.v[b][:, :], k.v[bt][:, :], ALU.add))
                link(dve, dve.tensor_tensor(k.v[b][:, :], k.v[b][:, :], k.psum[2][:, m * C:(m + 1) * C],
                                            ALU.add))


def lists_phase(nc, k, which):
    loaded = k.sem("lists_loaded")
    full = {"dst": 2, "src": 4}[which]
    source = {"dst": k.by_dst_dram, "src": k.by_src_dram}[which]
    rec = k.acc[:, 0:T * full].rearrange("p (t f) -> p t f", f=full)
    with nc.Block() as block:
        @block.sync
        def _(sp):
            sp.dma_start(rec, source.rearrange("(p t) f -> p t f", p=P)).then_inc(loaded, 16)

        @block.vector
        def _(dve):
            dve.wait_ge(loaded, 16)
            dve.tensor_copy(k.idx[:, 0:T], rec[:, :, 0])
            dve.memset(k.idx[:, T:T + BODY], 0)
            dve.tensor_copy(k.loc[:, 0:T], rec[:, :, 1])
            dve.memset(k.loc[:, T:T + G], PAD)


def pass_phase(nc, k, name, which, table, row, kind):
    n = name + "_"
    staged, hot, turned, copied, looked, scored, weighed, ready, ready_too, matched, reduced, added = (
        k.sem(n + s) for s in ("staged", "hot", "turned", "copied", "looked", "scored", "weighed", "ready",
                               "ready_too", "matched", "reduced", "added"))
    summed, leaned, lowered, multiplied, scaled, finished = (
        k.sem(n + s) for s in ("summed", "leaned", "lowered", "multiplied", "scaled", "finished"))
    link = Link(k.sem(n + "step"))
    base = k.gathered_base
    if kind != "value":
        k.gathered_base += 16 * IT
    kept = [k.sem(f"{n}kept{q}") for q in range(QUARTERS)]
    loaded = [k.sem(f"{n}loaded{q}") for q in range(QUARTERS)]
    far = k.wide if kind == "logit" else k.gat
    width = {"sum": C, "gat": A1, "value": A2, "max": 0, "logit": 0}[kind]
    looks = {"gat": 2 * H1, "logit": C}.get(kind, 0)
    near = {"gat": k.nodev[:, :, :].rearrange("p b c -> p (b c)"),
            "logit": k.h[:, :, :].rearrange("p b c -> p (b c)")}.get(kind)
    blocks = k.block_of[which]
    agg, tb, vb = k.psum[0:SUM_RING], k.psum[4:6], k.psum[6:8]
    diag = k.acc[:, 0:MAX_RING * G * H1 * P].rearrange("p (s t h c) -> p s t h c", s=MAX_RING, t=G, h=H1)
    peaks = k.wk[:, 0:2 * H1].rearrange("p (s h) -> p s h", s=2)
    sums = k.wk[:, 0:G * H1].rearrange("p (t h) -> p t h", h=H1)
    z = k.wk[:, G * H1:3 * G * H1].rearrange("p (s t h) -> p s t h", s=2, h=H1)
    prod = k.wk[:, 0:2 * G * C].rearrange("p (s t c) -> p s t c", s=2, t=G)
    qk = k.wk[:, 2 * G * C:2 * G * C + 2 * G * H2].rearrange("p (s c) -> p s c", s=2)

    def turns(eng, stages):
        for j in range(GB):
            for lag, stage in stages:
                if j >= lag:
                    stage(j - lag, 0, j - lag)
        with eng.Fori(1, IT) as i:
            for j in range(GB):
                for lag, stage in stages:
                    stage(i * GB + j - lag, i, j - lag)
        for j in range(max(lag for lag, _ in stages)):
            for lag, stage in stages:
                if j < lag:
                    stage(NG + j - lag, IT, j - lag)

    def wait(eng, sem, count):
        if not (isinstance(count, int) and count <= 0):
            eng.wait_ge(sem, count)

    def arrived(eng, i, j):
        if kind == "value":
            eng.wait_ge(loaded[ring(j) // QUARTER], i * 16 + (16 if j >= 0 else 0))
            return
        for t in range(G):
            eng.wait_ge(k.gathered[(G * j + t) % BODY], i * 16 + base + (16 if j >= 0 else 0))

    def ring(j):
        return G * (j % GB)

    used = {"logit": scored}.get(kind, matched)

    with nc.Block() as block:
        def load_quarter(sp, i, q):
            columns = bass.ds((i * BODY + q * QUARTER) * C, QUARTER * C)
            sp.dma_start(k.gat[:, q * QUARTER:(q + 1) * QUARTER, 0:C],
                         k.value_rows_dram[:, columns].rearrange("p (m c) -> p m c", c=C))\
                .then_inc(loaded[q], 16)

        if kind == "value":
            @block.sync
            def _(sp):
                for q in range(QUARTERS):
                    load_quarter(sp, 0, q)
                with sp.Fori(1, IT) as i:
                    for q in range(QUARTERS):
                        sp.wait_ge(matched, i * GB + (q + 1) * (QUARTER // G) - GB)
                        load_quarter(sp, i, q)

        if kind == "logit":
            @block.sync
            def _(sp):
                with sp.Fori(0, IT) as i:
                    for q in range(QUARTERS):
                        for m in range(q * QUARTER, (q + 1) * QUARTER):
                            sp.wait_ge(k.gathered[m], i * 16 + base + 16)
                        columns = bass.ds((i * BODY + q * QUARTER) * C, QUARTER * C)
                        sp.dma_start(k.value_rows_dram[:, columns].rearrange("p (m c) -> p m c", c=C),
                                     k.wide[:, q * QUARTER:(q + 1) * QUARTER, C:2 * C]).then_inc(kept[q], 16)
                for q in range(QUARTERS):
                    sp.wait_ge(kept[q], IT * 16)

        @block.gpsimd
        def _(pool):
            def message(g, i, j):
                arrived(pool, i, j)
                pool.wait_ge(weighed, g + 1)
                rows = k.gat[:, ring(j):ring(j) + G, 0:C].rearrange("p t (h c) -> p t h c", h=H2)
                wts = k.gat[:, ring(j):ring(j) + G, C:C + H2].unsqueeze(3).to_broadcast([P, G, H2, D2])
                pool.tensor_tensor(rows, rows, wts, ALU.mult).then_inc(ready, 1)

            if kind == "value":
                turns(pool, [(0, message)])
                return
            with pool.Fori(0, IT) as i:
                for q in range(QUARTERS):
                    pool.wait_ge(staged, i * QUARTERS + q + 1)
                    pool.sem_inc(k.passed, 1)
                    for m in range(q * QUARTER, (q + 1) * QUARTER):
                        pool.indirect_dma_start(
                            far[:, m, 0:row], None, table,
                            bass.IndirectOffsetOnAxis(k.stage[:, m:m + 1], axis=0)).then_inc(k.gathered[m], 16)

        @block.scalar
        def _(act):
            def stage_indices(g, i, j):
                if j % 2 == 0 or (isinstance(i, int) and i == IT):
                    return
                act.wait_ge(used, g + 1)
                if kind == "logit":
                    act.wait_ge(kept[ring(j - 1) // QUARTER], i * 16 + (16 if j >= 1 else 0))
                act.activation(k.stage[:, ring(j - 1):ring(j - 1) + QUARTER],
                               k.idx[:, bass.ds(i * BODY + G * (j - 1 + GB), QUARTER)],
                               ACT.Copy).then_inc(staged, 1)

            def turn_hot(g, i, j):
                act.wait_ge(turned, g + 1)
                act.activation(k.hot_t[:, j % 2, :], tb[j % 2][:, 0:G * P], ACT.Copy).then_inc(copied, 1)

            def exp_scores(g, i, j):
                act.wait_ge(scored, g + 1)
                act.activation(k.gat[:, ring(j):ring(j) + G, C:A1], z[:, j % 2, :, :], ACT.Exp).then_inc(weighed, 1)

            def weights(g, i, j):
                wait(act, matched, g + 1 - GB)
                act.activation(k.gat[:, ring(j):ring(j) + G, C:A2],
                               k.big[:, bass.ds((i * BODY + G * j) * H2, G * H2)]
                               .rearrange("p (t h) -> p t h", h=H2), ACT.Copy).then_inc(weighed, 1)

            def diagonals(g, i, j):
                arrived(act, i, j)
                wait(act, matched, g + 1 - MAX_RING)
                for t in range(G):
                    for hd in range(H1):
                        if (t, hd) != (G - 1, H1 - 1):
                            last = act.activation(diag[:, j % MAX_RING, t, hd, :], k.ident[:, :], ACT.Copy,
                                                  scale=k.gat[:, ring(j) + t, hd:hd + 1])
                last.then_inc(ready, 1)

            for q in range(QUARTERS if kind != "value" else 0):
                act.activation(k.stage[:, q * QUARTER:(q + 1) * QUARTER],
                               k.idx[:, q * QUARTER:(q + 1) * QUARTER], ACT.Copy).then_inc(staged, 1)
            turns(act, {"sum": [(2, stage_indices)],
                        "max": [(0, diagonals), (3, stage_indices)],
                        "gat": [(3, exp_scores), (0, turn_hot), (6, stage_indices)],
                        "logit": [(0, turn_hot), (5, stage_indices)],
                        "value": [(0, weights)]}[kind])

        @block.tensor
        def _(pe):
            def turn(g, i, j):
                pe.wait_ge(hot, g + 1)
                wait(pe, copied, g - 1)
                for t in range(G):
                    last = pe.transpose(tb[j % 2][:, t * P:(t + 1) * P], k.oneh[:, ring(j) + t, :],
                                        k.ident[:, :])
                last.then_inc(turned, 1)

            def look(g, i, j):
                b = pe.value_load(blocks[0:1, bass.ds(g, 1)], min_val=0, max_val=NB - 1)
                pe.wait_ge(copied, g + 1)
                wait(pe, scored, g - 1)
                for t in range(G):
                    last = pe.matmul(vb[j % 2][:, t * looks:(t + 1) * looks],
                                     k.hot_t[:, j % 2, t * P:(t + 1) * P], near[:, bass.ds(b * looks, looks)],
                                     start=True, stop=True)
                last.then_inc(looked, 1)

            def multiply(g, i, j):
                pe.wait_ge(hot, g + 1)
                if kind == "max":
                    wait(pe, reduced, g + 1 - MAX_RING)
                else:
                    wait(pe, added, g + 1 - SUM_RING)
                if kind == "sum":
                    arrived(pe, i, j)
                else:
                    pe.wait_ge(ready, g + 1)
                if kind == "max":
                    pe.wait_ge(ready_too, g + 1)
                for t in range(G):
                    oh = k.oneh[:, ring(j) + t, :]
                    if kind == "max":
                        rhs = diag[:, j % MAX_RING, t, :, :].rearrange("p h c -> p (h c)")
                        last = pe.matmul(k.psum[G * (j % MAX_RING) + t][:, :], oh, rhs, start=True, stop=True)
                    else:
                        last = pe.matmul(agg[j % SUM_RING][:, 0:width], oh, k.gat[:, ring(j) + t, 0:width],
                                         start=(t == 0), stop=(t == G - 1))
                last.then_inc(matched, 1)

            turns(pe, {"gat": [(5, multiply), (2, look), (0, turn)],
                       "logit": [(2, look), (0, turn)],
                       "value": [(1, multiply)]}.get(kind, [(0, multiply)]))

        @block.vector
        def _(dve):
            def make_hot(g, i, j):
                for t in range(G):
                    last = dve.tensor_scalar(k.oneh[:, ring(j) + t, :], k.ramp[:, :],
                                             k.loc[:, bass.ds(i * BODY + G * j + t, 1)], None, ALU.is_equal)
                last.then_inc(hot, 1)

            def add(g, i, j):
                b = dve.value_load(blocks[0:1, bass.ds(g, 1)], min_val=0, max_val=NB - 1)
                dve.wait_ge(matched, g + 1)
                wait(dve, added, g)
                mine = k.acc[:, bass.ds(b * width, width)]
                dve.tensor_tensor(mine, mine, agg[j % SUM_RING][:, 0:width], ALU.add).then_inc(added, 1)

            def diagonal(g, i, j):
                arrived(dve, i, j)
                wait(dve, matched, g + 1 - MAX_RING)
                dve.tensor_scalar(diag[:, j % MAX_RING, G - 1, H1 - 1, :], k.ident[:, :],
                                  k.gat[:, ring(j) + G - 1, H1 - 1:H1], None, ALU.mult).then_inc(ready_too, 1)

            def reduce_peaks(g, i, j):
                dve.wait_ge(matched, g + 1)
                wait(dve, added, g - 1)
                view = k.psum_pair[j % MAX_RING].rearrange("p (t h c) -> p h t c", t=G, h=H1)
                dve.tensor_reduce(peaks[:, j % 2, :], view, AX.XY, ALU.max).then_inc(reduced, 1)

            def take_peaks(g, i, j):
                b = dve.value_load(blocks[0:1, bass.ds(g, 1)], min_val=0, max_val=NB - 1)
                dve.wait_ge(reduced, g + 1)
                wait(dve, added, g)
                mine = k.maxa[:, bass.ds(b * H1, H1)]
                dve.tensor_tensor(mine, mine, peaks[:, j % 2, :], ALU.max).then_inc(added, 1)

            def endpoint_values(j):
                return vb[j % 2][:, 0:G * looks].rearrange("p (t c) -> p t c", t=G)

            def sum_scores(g, i, j):
                arrived(dve, i, j)
                dve.wait_ge(looked, g + 1)
                wait(dve, scored, g)
                dve.tensor_tensor(sums, k.gat[:, ring(j):ring(j) + G, C:A1], endpoint_values(j)[:, :, 0:H1],
                                  ALU.add).then_inc(summed, 1)

            def lean_scores(g, i, j):
                dve.wait_ge(summed, g + 1)
                dve.scalar_tensor_tensor(sums, sums, 0.2, sums, ALU.mult, ALU.max).then_inc(leaned, 1)

            def lower_scores(g, i, j):
                dve.wait_ge(leaned, g + 1)
                dve.tensor_tensor(sums, sums, endpoint_values(j)[:, :, H1:2 * H1], ALU.subtract)\
                    .then_inc(lowered, 1)

            def bound_scores(g, i, j):
                dve.wait_ge(lowered, g + 1)
                wait(dve, weighed, g - 1)
                dve.tensor_scalar(z[:, j % 2, :, :], sums, 0.0, None, ALU.min).then_inc(scored, 1)

            def message(g, i, j):
                dve.wait_ge(weighed, g + 1)
                rows = k.gat[:, ring(j):ring(j) + G, 0:C].rearrange("p t (h c) -> p t h c", h=H1)
                wts = k.gat[:, ring(j):ring(j) + G, C:C + H1].unsqueeze(3).to_broadcast([P, G, H1, D1])
                dve.tensor_tensor(rows, rows, wts, ALU.mult).then_inc(ready, 1)

            def multiply_endpoints(g, i, j):
                arrived(dve, i, j)
                dve.wait_ge(looked, g + 1)
                wait(dve, scored, g - 1)
                dve.tensor_tensor(prod[:, j % 2, :, :], far[:, ring(j):ring(j) + G, 0:C], endpoint_values(j),
                                  ALU.mult).then_inc(multiplied, 1)

            def sum_heads(g, i, j):
                dve.wait_ge(multiplied, g + 1)
                wait(dve, finished, g - 1)
                dve.tensor_reduce(qk[:, j % 2, :], prod[:, j % 2, :, :].rearrange("p t (h d) -> p (t h) d", d=D2),
                                  AX.X, ALU.add).then_inc(scored, 1)

            def scale_logits(g, i, j):
                mine = qk[:, j % 2, :]
                dve.wait_ge(scored, g + 1)
                dve.scalar_tensor_tensor(mine, mine, 1.0 / math.sqrt(D2),
                                         k.big[:, bass.ds((i * BODY + G * j) * H2, G * H2)],
                                         ALU.mult, ALU.add).then_inc(scaled, 1)

            def cut_logits(g, i, j):
                dve.wait_ge(scaled, g + 1)
                for t in range(G):
                    at = i * BODY + G * j + t
                    last = dve.tensor_scalar(k.big[:, bass.ds(at * H2, H2)], qk[:, j % 2, t * H2:(t + 1) * H2],
                                             k.cut[:, bass.ds(at, 1)], None, ALU.mult)
                last.then_inc(finished, 1)

            if kind == "max":
                link(dve, dve.tensor_copy(k.maxa[:, :], k.asrc[:, :, :].rearrange("p b h -> p (b h)")))
            elif width:
                link(dve, dve.memset(k.acc[:, 0:NB * width], 0.0))
            turns(dve, {
                "sum": [(0, make_hot), (2, add)],
                "max": [(2, reduce_peaks), (0, make_hot), (0, diagonal), (2, take_peaks)],
                "gat": [(3, sum_scores), (4, message), (3, lean_scores), (0, make_hot), (3, lower_scores), (6, add),
                        (3, bound_scores)],
                "logit": [(3, multiply_endpoints), (4, scale_logits), (0, make_hot), (4, cut_logits),
                          (3, sum_heads)],
                "value": [(0, make_hot), (3, add)]}[kind])


class Chunk:

    def __init__(self, nc, k, name):
        self.nc, self.k, self.name = nc, k, name
        self.link = Link(k.sem(name + "_step"))
        self.rows_ready, self.turned, self.copied, self.product, self.asked, self.given, self.to_store, \
            self.stored = (k.sem(f"{name}_{s}") for s in (
                "rows_ready", "turned", "copied", "product", "asked", "given", "to_store", "stored"))
        self.room = k.sem(name + "_room")
        f = k.chunk_room
        w = BC * C
        self.y, self.yt, self.s, self.o = (f[:, m * w:(m + 1) * w].rearrange("p (b c) -> p b c", c=C)
                                           for m in range(4))

    def ask(self, dve, i, n, per):
        dve.wait_ge(self.given, i * per + n)

    def norm(self, dve, i, n, per, src, dst):
        k, link, st = self.k, self.link, self.k.st
        for b in range(BC):
            last = dve.bn_stats(st[:, b, 0:6], src[:, b, :])
        link(dve, last)
        dve.sem_inc(k.passed, 1)
        for b in range(BC):
            last = dve.bn_aggr(st[:, b, 6:8], st[:, b, 0:6])
        link(dve, last)
        dve.tensor_scalar(st[:, :, 8], st[:, :, 7], EPS, None, ALU.add).then_inc(self.asked, 1)
        self.ask(dve, i, n, per)
        link(dve, dve.reciprocal(st[:, :, 10], st[:, :, 9]))
        for b in range(BC):
            last = dve.tensor_scalar(dst[:, b, :], src[:, b, :], st[:, b, 6:7], st[:, b, 10:11],
                                     ALU.subtract, ALU.mult)
        link(dve, last)

    def bc(self, vector):
        return vector.unsqueeze(1).to_broadcast([P, BC, C])


def by_blocks(tensor, i):
    return tensor[:, bass.ds(i * BC, BC), :]


def by_heads(rows, heads):
    return rows.rearrange("p b (h d) -> p b h d", h=heads)


def halves():
    return ((0, 0, 4), (1, 4, BC))


def dense_phase(nc, k, name, before, after, mats, jobs, stores=()):
    c = Chunk(nc, k, name)
    link = c.link
    with nc.Block() as block:
        @block.vector
        def _(dve):
            with dve.Fori(0, NCH) as i:
                link.loop(i, before.links + after.links)
                before(c, dve, i)
                if mats:
                    dve.wait_ge(c.product, i + 1)
                after(c, dve, i)
            link.end(NCH)

        @block.scalar
        def _(act):
            with act.Fori(0, NCH) as i:
                for n, job in enumerate(jobs):
                    if job == "turn":
                        act.wait_ge(c.turned, i + 1)
                        for bank, lo, up in halves():
                            last = act.activation(c.yt[:, lo:up, :], k.psum[bank][:, 0:(up - lo) * C]
                                                  .rearrange("p (b c) -> p b c", c=C), ACT.Copy)
                        last.then_inc(c.copied, 1)
                    else:
                        m = len([q for q in jobs[:n + 1] if q != "turn"])
                        act.wait_ge(c.asked, i * len([q for q in jobs if q != "turn"]) + m)
                        job(c, act).then_inc(c.given, 1)

        if mats:
            @block.tensor
            def _(pe):
                with pe.Fori(0, NCH) as i:
                    pe.wait_ge(c.rows_ready, i + 1)
                    for bank, lo, up in halves():
                        for b in range(lo, up):
                            last = pe.transpose(k.psum[bank][:, (b - lo) * C:(b - lo + 1) * C], c.y[:, b, :],
                                                k.ident[:, :])
                    last.then_inc(c.turned, 1)
                    pe.wait_ge(c.copied, i + 1)
                    for m, mat in enumerate(mats):
                        for bank, lo, up in halves():
                            for b in range(lo, up):
                                last = pe.matmul(k.psum[2 + 2 * m + bank][:, (b - lo) * C:(b - lo + 1) * C],
                                                 c.yt[:, b, :], mat[:, :], start=True, stop=True)
                    last.then_inc(c.product, 1)

        if stores:
            @block.sync
            def _(sp):
                sp.sem_inc(c.room, 1)
                with sp.Fori(0, NCH) as i:
                    sp.wait_ge(c.to_store, i + 1)
                    for table, rows in stores:
                        sp.dma_start(table.rearrange("(b p) c -> p b c", p=P)[:, bass.ds(i * BC, BC), :], rows(c))\
                            .then_inc(c.stored, 16)
                    sp.wait_ge(c.stored, i * (16 * len(stores)) + 16 * len(stores))
                    sp.sem_inc(c.room, 1)


def product(k, m):
    return k.psum_pair[1 + m][:, 0:BC * C].rearrange("p (b c) -> p b c", c=C)


def sqrt_job(c, act):
    return act.activation(c.k.st[:, :, 9], c.k.st[:, :, 8], ACT.Sqrt)


def silu_job(c, act):
    return act.activation(c.s, c.s, ACT.Silu)


def stage_gcn_in(k):
    def before(c, dve, i):
        link = c.link
        c.norm(dve, i, 1, 1, by_blocks(k.x, i), c.y)
        link(dve, dve.tensor_tensor(c.y, c.y, c.bc(k.v["L0_gnn_g1"][:, :]), ALU.mult))
        dve.tensor_tensor(c.y, c.y, c.bc(k.v["L0_gnn_bn1"][:, :]), ALU.add).then_inc(c.rows_ready, 1)
    before.links = 5
    return before, gcn_out(k)


def gcn_out(k):
    def after(c, dve, i):
        link = c.link
        h = by_blocks(k.h, i)
        link(dve, copy(dve, h, product(k, 0)))
        dve.wait_ge(c.room, i + 1)
        inv = k.dinv[:, bass.ds(i * BC, BC)].unsqueeze(2).to_broadcast([P, BC, C])
        dve.tensor_tensor(c.o, h, inv, ALU.mult).then_inc(c.to_store, 1)
    after.links = 1
    return after


def gcn_sum(k, c, dve, i, bias):
    link = c.link
    inv = k.dinv[:, bass.ds(i * BC, BC)].unsqueeze(2).to_broadcast([P, BC, C])
    link(dve, dve.tensor_tensor(c.s, by_blocks(k.h, i), inv, ALU.mult))
    acc = k.acc[:, bass.ds(i * (BC * C), BC * C)].rearrange("p (b c) -> p b c", c=C)
    link(dve, dve.tensor_tensor(c.s, c.s, acc, ALU.add))
    link(dve, dve.tensor_tensor(c.s, c.s, inv, ALU.mult))
    dve.tensor_tensor(c.s, c.s, c.bc(bias[:, :]), ALU.add).then_inc(c.asked, 1)
    c.ask(dve, i, 1, 2)


def stage_gcn_mid(k):
    def before(c, dve, i):
        link = c.link
        gcn_sum(k, c, dve, i, k.v["L0_gnn_b1"])
        c.norm(dve, i, 2, 2, c.s, c.y)
        link(dve, dve.tensor_tensor(c.y, c.y, c.bc(k.v["L0_gnn_g2"][:, :]), ALU.mult))
        dve.tensor_tensor(c.y, c.y, c.bc(k.v["L0_gnn_bn2"][:, :]), ALU.add).then_inc(c.rows_ready, 1)
    before.links = 8
    return before, gcn_out(k)


def stage_gcn_out(k):
    def before(c, dve, i):
        link = c.link
        gcn_sum(k, c, dve, i, k.v["L0_gnn_b2"])
        x = by_blocks(k.x, i)
        link(dve, dve.tensor_tensor(c.s, c.s, x, ALU.add))
        link(dve, dve.tensor_tensor(c.s, c.s, x, ALU.add))
        c.norm(dve, i, 2, 2, c.s, x)
        copy(dve, c.y, x).then_inc(c.rows_ready, 1)
    before.links = 9

    def after(c, dve, i):
        link = c.link
        h = by_blocks(k.h, i)
        link(dve, copy(dve, h, product(k, 0)))
        link(dve, dve.tensor_tensor(c.s, h, c.bc(k.v["L1_gnn_att_src"][:, :]), ALU.mult))
        link(dve, dve.tensor_reduce(by_blocks(k.asrc, i), by_heads(c.s, H1), AX.X, ALU.add))
        link(dve, dve.tensor_tensor(c.s, h, c.bc(k.v["L1_gnn_att_dst"][:, :]), ALU.mult))
        link(dve, dve.tensor_reduce(by_blocks(k.nodev, i)[:, :, 0:H1], by_heads(c.s, H1), AX.X, ALU.add))
    after.links = 5
    return before, after


def extreme_phase(nc, k, name, src, width, use):
    turned, diagonal, spread, ready = (k.sem(f"{name}_{s}") for s in ("turned", "diagonal", "spread", "ready"))
    link = Link(k.sem(name + "_step"))
    part = k.tmp[:, 32:32 + width]
    top = k.tmp[0:width, 64:65]
    diag = k.tmp[0:width, 96:96 + width]
    with nc.Block() as block:
        @block.vector
        def _(dve):
            src(dve, link, part)
            dve.sem_inc(ready, 1)
            dve.wait_ge(turned, 1)
            link(dve, dve.tensor_reduce(top, k.psum[0][0:width, 0:P], AX.X, ALU.max))
            dve.tensor_scalar(diag, k.ident[0:width, 0:width], top, None, ALU.mult).then_inc(diagonal, 1)
            dve.wait_ge(spread, 1)
            link(dve, dve.tensor_copy(k.tmp[:, 0:width], k.psum[1][:, 0:width]))
            use(dve, link)

        @block.tensor
        def _(pe):
            pe.wait_ge(ready, 1)
            pe.transpose(k.psum[0][0:width, 0:P], part, k.ident[:, :]).then_inc(turned, 1)
            pe.wait_ge(diagonal, 1)
            pe.matmul(k.psum[1][:, 0:width], k.ones[0:width, :], diag, start=True, stop=True)\
                .then_inc(spread, 1)


def shift_phase(nc, k):
    stored, to_store, room = k.sem("shift_stored"), k.sem("shift_to_store"), k.sem("shift_room")

    def src(dve, link, part):
        link(dve, dve.tensor_reduce(part, k.asrc[:, :, :].rearrange("p b h -> p h b"), AX.X, ALU.min))
        link(dve, dve.tensor_scalar(part, part, -1.0, None, ALU.mult))

    def use(dve, link):
        low = k.tmp[:, 0:H1].unsqueeze(1).to_broadcast([P, NB, H1])
        link(dve, dve.tensor_tensor(k.asrc[:, :, :], k.asrc[:, :, :], low, ALU.add))
        link(dve, dve.tensor_tensor(k.nodev[:, :, 0:H1], k.nodev[:, :, 0:H1], low, ALU.subtract))
        link(dve, dve.tensor_scalar(k.asrc[:, :, :], k.asrc[:, :, :], 0.0, None, ALU.max))
    extreme_phase(nc, k, "low", src, H1, use)
    with nc.Block() as block:
        @block.sync
        def _(sp):
            rows = k.tab_h_dram.rearrange("(b p) c -> p b c", p=P)
            with nc.allow_non_contiguous_dma(reason="four floats beside each row"):
                sp.dma_start(k.tab_a_dram.rearrange("(b p) c -> p b c", p=P), k.asrc[:, :, :])\
                    .then_inc(stored, 16)
                sp.dma_start(rows[:, :, 0:C], k.h[:, :, :]).then_inc(stored, 16)
                sp.dma_start(rows[:, :, C:A1], k.asrc[:, :, :]).then_inc(stored, 16)
            sp.wait_ge(stored, 48)


def leaky(dve, link, out, rows, tmp):
    link(dve, dve.tensor_scalar(tmp, rows, 0.2, None, ALU.mult))
    link(dve, dve.tensor_tensor(out, rows, tmp, ALU.max))


def gat_maximum_phase(nc, k):
    asked, given = k.sem("self_asked"), k.sem("self_given")
    link = Link(k.sem("self_step"))
    with nc.Block() as block:
        d = k.nodev[:, :, 0:H1]
        m = k.nodev[:, :, H1:2 * H1]
        maxa = k.maxa[:, :].rearrange("p (b h) -> p b h", h=H1)
        tmp = k.wk[:, 0:NB * H1].rearrange("p (b h) -> p b h", h=H1)
        tmp2 = k.wk[:, NB * H1:2 * NB * H1].rearrange("p (b h) -> p b h", h=H1)

        @block.vector
        def _(dve):
            link(dve, dve.tensor_tensor(maxa, maxa, d, ALU.add))
            leaky(dve, link, m, maxa, tmp)
            link(dve, dve.tensor_tensor(tmp2, k.asrc[:, :, :], d, ALU.add))
            leaky(dve, link, maxa, tmp2, tmp)
            dve.tensor_tensor(maxa, maxa, m, ALU.subtract).then_inc(asked, 1)

        @block.scalar
        def _(act):
            act.wait_ge(asked, 1)
            act.activation(maxa, maxa, ACT.Exp).then_inc(given, 1)
            act.wait_ge(given, 1)


def stage_gat_out(k):
    def tanh_job(c, act):
        return act.activation(c.s, c.s, ACT.Tanh)

    def before(c, dve, i):
        link = c.link
        acc = k.acc[:, bass.ds(i * (BC * A1), BC * A1)].rearrange("p (b c) -> p b c", c=A1)
        own = k.maxa[:, bass.ds(i * (BC * H1), BC * H1)].rearrange("p (b h) -> p b h", h=H1)
        rep = own.unsqueeze(3).to_broadcast([P, BC, H1, D1])
        link(dve, dve.tensor_tensor(by_heads(c.s, H1), by_heads(by_blocks(k.h, i), H1), rep, ALU.mult))
        link(dve, dve.tensor_tensor(c.s, c.s, acc[:, :, 0:C], ALU.add))
        den = c.o[:, 0, 0:BC * H1].rearrange("p (b h) -> p b h", h=H1)
        link(dve, dve.tensor_tensor(den, own, acc[:, :, C:A1], ALU.add))
        link(dve, dve.tensor_scalar(den, den, 1e-16, None, ALU.add))
        link(dve, dve.reciprocal(den, den))
        link(dve, dve.tensor_tensor(by_heads(c.s, H1), by_heads(c.s, H1),
                                    den.unsqueeze(3).to_broadcast([P, BC, H1, D1]), ALU.mult))
        dve.tensor_tensor(c.s, c.s, c.bc(k.v["L1_gnn_bias"][:, :]), ALU.add).then_inc(c.asked, 1)
        c.ask(dve, i, 1, 2)
        x = by_blocks(k.x, i)
        link(dve, dve.tensor_tensor(c.s, c.s, x, ALU.add))
        c.norm(dve, i, 2, 2, c.s, x)
        copy(dve, c.y, x).then_inc(c.rows_ready, 1)
    before.links = 11

    def after(c, dve, i):
        link = c.link
        link(dve, dve.tensor_tensor(by_blocks(k.h, i), product(k, 0), c.bc(k.v["L2_gnn_bq"][:, :]), ALU.add))
        dve.wait_ge(c.room, i + 1)
        link(dve, dve.tensor_tensor(c.o, product(k, 1), c.bc(k.v["L2_gnn_bk"][:, :]), ALU.add))
        dve.tensor_tensor(c.s, product(k, 2), c.bc(k.v["L2_gnn_bv"][:, :]), ALU.add).then_inc(c.to_store, 1)
        dve.wait_ge(c.room, i + 2)
    after.links = 2
    return before, after, tanh_job


def softmax_phase(nc, k):
    lg = k.big[:, :].rearrange("p (t h) -> p t h", h=H2)

    def src(dve, link, part):
        link(dve, dve.tensor_reduce(part, k.big[:, :].rearrange("p (t h) -> p h t", h=H2), AX.X, ALU.max))

    def use(dve, link):
        top = k.tmp[:, 0:H2].unsqueeze(1).to_broadcast([P, T, H2])
        link(dve, dve.tensor_tensor(lg, lg, top, ALU.subtract))
    extreme_phase(nc, k, "top", src, H2, use)
    done = k.sem("exp_done")
    with nc.Block() as block:
        @block.scalar
        def _(act):
            act.activation(k.big[:, :], k.big[:, :], ACT.Exp).then_inc(done, 1)
            act.wait_ge(done, 1)


def stage_attention_out(k):
    def before(c, dve, i):
        link = c.link
        acc = k.acc[:, bass.ds(i * (BC * A2), BC * A2)].rearrange("p (b c) -> p b c", c=A2)
        den = c.s[:, 0, 0:BC * H2].rearrange("p (b h) -> p b h", h=H2)
        link(dve, dve.tensor_scalar(den, acc[:, :, C:A2], 1e-8, None, ALU.add))
        link(dve, dve.reciprocal(den, den))
        dve.tensor_tensor(by_heads(c.y, H2), by_heads(acc[:, :, 0:C], H2),
                          den.unsqueeze(3).to_broadcast([P, BC, H2, D2]), ALU.mult).then_inc(c.rows_ready, 1)
    before.links = 2

    def after(c, dve, i):
        link = c.link
        x = by_blocks(k.x, i)
        link(dve, dve.tensor_tensor(c.s, product(k, 0), c.bc(k.v["L2_gnn_bo"][:, :]), ALU.add))
        link(dve, dve.tensor_tensor(c.s, c.s, x, ALU.add))
        c.norm(dve, i, 1, 2, c.s, c.s)
        link(dve, dve.tensor_tensor(c.s, c.s, c.bc(k.v["L2_gnn_ln_g"][:, :]), ALU.mult))
        link(dve, dve.tensor_tensor(c.s, c.s, c.bc(k.v["L2_gnn_ln_b"][:, :]), ALU.add))
        link(dve, dve.tensor_tensor(c.s, c.s, x, ALU.add))
        c.norm(dve, i, 2, 2, c.s, x)
        dve.wait_ge(c.room, i + 1)
        copy(dve, c.o, x).then_inc(c.to_store, 1)
    after.links = 13
    return before, after


def stage_message_mid(k):
    def before(c, dve, i):
        copy(dve, c.y, by_blocks(k.x, i)).then_inc(c.rows_ready, 1)
    before.links = 0

    def after(c, dve, i):
        link = c.link
        link(dve, dve.tensor_tensor(c.s, product(k, 0), c.bc(k.v["L3_gnn_b_msg"][:, :]), ALU.add))
        times = k.deg[:, bass.ds(i * BC, BC)].unsqueeze(2).to_broadcast([P, BC, C])
        link(dve, dve.tensor_tensor(by_blocks(k.h, i), c.s, times, ALU.mult))
        part = k.big[:, bass.ds(i * (BC * C), BC * C)].rearrange("p (b c) -> p b c", c=C)
        link(dve, dve.tensor_tensor(part, product(k, 1), c.bc(k.v["L3_gnn_b_upd"][:, :]), ALU.add))
        link(dve, dve.tensor_tensor(part, part, by_blocks(k.x, i), ALU.add))
    after.links = 4
    return before, after


def stage_message_sum(k):
    def before(c, dve, i):
        acc = k.acc[:, bass.ds(i * (BC * C), BC * C)].rearrange("p (b c) -> p b c", c=C)
        copy(dve, c.y, acc).then_inc(c.rows_ready, 1)
    before.links = 0

    def after(c, dve, i):
        c.link(dve, dve.tensor_tensor(by_blocks(k.h, i), by_blocks(k.h, i), product(k, 0), ALU.add))
    after.links = 1
    return before, after


def stage_message_out(k):
    def before(c, dve, i):
        copy(dve, c.y, by_blocks(k.h, i)).then_inc(c.rows_ready, 1)
    before.links = 0

    def after(c, dve, i):
        link = c.link
        part = k.big[:, bass.ds(i * (BC * C), BC * C)].rearrange("p (b c) -> p b c", c=C)
        link(dve, dve.tensor_tensor(c.s, part, product(k, 0), ALU.add))
        c.norm(dve, i, 1, 1, c.s, by_blocks(k.x, i))
    after.links = 5
    return before, after


def store_phase(nc, k):
    stored = k.sem("out_stored")
    with nc.Block() as block:
        @block.sync
        def _(sp):
            sp.dma_start(k.out[0:(NB - 1) * P, :].rearrange("(b p) c -> p b c", p=P), k.x[:, 0:NB - 1, :])\
                .then_inc(stored, 16)
            sp.dma_start(k.out[(NB - 1) * P:N, :], k.x[0:REM, NB - 1, :]).then_inc(stored, 16)
            sp.wait_ge(stored, 32)


def build(nc, a, out):
    with ExitStack() as ctx:
        k = allocate(nc, ctx, a, out)

        def run(phase, *args):
            phase(nc, k, *args)
            nc.clear_and_free_semaphores(k.phase_sems)
            k.phase_sems = []
            nc.all_engine_barrier()

        run(load_phase)
        run(fields_phase)
        run(rank_phase)
        run(first_scatter_phase)
        run(second_scatter_phase)
        run(prepare_phase)
        run(lists_phase, "dst")
        run(dense_phase, "gcn_in", *stage_gcn_in(k), [k.w["L0_gnn_W1"]], [sqrt_job, "turn"],
            [(k.tab_dram, lambda c: c.o)])
        run(pass_phase, "gcn1", "dst", k.tab_dram, C, "sum")
        run(dense_phase, "gcn_mid", *stage_gcn_mid(k), [k.w["L0_gnn_W2"]], [silu_job, sqrt_job, "turn"],
            [(k.tab_dram, lambda c: c.o)])
        run(pass_phase, "gcn2", "dst", k.tab_dram, C, "sum")
        run(dense_phase, "gcn_out", *stage_gcn_out(k), [k.w["L1_gnn_W"]], [silu_job, sqrt_job, "turn"])
        run(shift_phase)
        run(pass_phase, "gat_max", "dst", k.tab_a_dram, H1, "max")
        run(gat_maximum_phase)
        run(pass_phase, "gat", "dst", k.tab_h_dram, A1, "gat")
        before, after, tanh_job = stage_gat_out(k)
        run(dense_phase, "gat_out", before, after, [k.w[n] for n in ("L2_gnn_Wq", "L2_gnn_Wk", "L2_gnn_Wv")],
            [tanh_job, sqrt_job, "turn"], [(k.tab_kv_dram[:, 0:C], lambda c: c.o), (k.tab_kv_dram[:, C:2 * C], lambda c: c.s)])
        run(lists_phase, "src")
        run(pass_phase, "logit", "src", k.tab_kv_dram, 2 * C, "logit")
        run(softmax_phase)
        run(pass_phase, "value", "src", None, C, "value")
        run(dense_phase, "att_out", *stage_attention_out(k), [k.w["L2_gnn_Wo"]], ["turn", sqrt_job, sqrt_job],
            [(k.tab_dram, lambda c: c.o)])
        run(lists_phase, "dst")
        run(dense_phase, "msg_mid", *stage_message_mid(k), [k.bot["L3_gnn_W_msg"], k.top["L3_gnn_W_upd"]],
            ["turn"])
        run(pass_phase, "msg", "dst", k.tab_dram, C, "sum")
        run(dense_phase, "msg_sum", *stage_message_sum(k), [k.top["L3_gnn_W_msg"]], ["turn"])
        run(dense_phase, "msg_out", *stage_message_out(k), [k.bot["L3_gnn_W_upd"]], ["turn", sqrt_job])
        run(store_phase)


INPUTS = ("x", "src", "dst", "edge_weight1") + MATS + HALVES + VECS + ATTS + (
    "L0_gnn_t_emb", "L2_gnn_We1", "L2_gnn_be1", "L2_gnn_We2", "L2_gnn_be2")


def kernel(**inputs):
    import numpy as _np
    import concourse.bacc as _bacc
    from concourse.bass_utils import run_bass_kernel_spmd as _run

    nc = _bacc.Bacc("TRN2", target_bir_lowering=False, num_devices=1)
    arrays, args = {}, {}
    for name in INPUTS:
        arr = _np.ascontiguousarray(inputs[name])
        arrays[f"in_{name}"] = arr
        args[name] = nc.dram_tensor(f"in_{name}", arr.shape, mybir.dt.from_np(arr.dtype), kind="ExternalInput").ap()
    out = nc.dram_tensor("out", (N, C), F32, kind="ExternalOutput").ap()
    build(nc, args, out)
    return _run(nc, [arrays], core_ids=[0]).results[0]["out"]
```
